# Optimizing a Trainium2 kernel written in Bass

```python
import numpy as np
import jax
import jax.numpy as jnp

def _softmax(x, axis=-1):
    return jax.nn.softmax(x, axis=axis)

def _gelu(x):
    return jax.nn.gelu(x, approximate=True)

def _silu(x):
    return jax.nn.silu(x)

def _sigmoid(x):
    return jax.nn.sigmoid(x)

def _layernorm(x, axis=-1, eps=1e-05):
    m = jnp.mean(x, axis=axis, keepdims=True)
    v = jnp.var(x, axis=axis, keepdims=True)
    return (x - m) / jnp.sqrt(v + eps)

def _scatter_add(tgt, idx, src, axis=0):
    return tgt.at[idx].add(src)

def _segment_sum(src, seg, n):
    return jax.ops.segment_sum(src, seg, n)
kernel_name = 'mk_gnn_preln_d4_gnn_r16_80e69e'

def setup_inputs(seed: int=0):
    np.random.seed(seed)
    _w = jnp.asarray

    def _rec_inputs():
        import jax
        import jax.numpy as jnp
        _gk = jax.random.key(seed)
        x = -0.000202 + 1 * jax.random.normal(jax.random.fold_in(_gk, 1), (6250, 64), jnp.float32)
        src = jax.random.randint(jax.random.fold_in(_gk, 2), (100000,), 0, 6250, jnp.int32)
        dst = jnp.minimum((6250 * jax.random.uniform(jax.random.fold_in(_gk, 3), (100000,)) ** 2.0).astype(jnp.int32), 99999)
        _o = jnp.argsort(dst, stable=True)
        src = src[_o]
        dst = dst[_o]
        edge_attr_18 = 0.000175535 + 1.00015 * jax.random.normal(jax.random.fold_in(_gk, 11), (100000, 18), jnp.float32)
        return (x, src, dst, edge_attr_18)
    x, src, dst, edge_attr_18 = _rec_inputs()

    def _L0_gnn_setup():
        import jax, jax.numpy as jnp
        import numpy as np
        N_NODES = 6250
        N_EDGES = 100000
        D = 64
        N_LAYERS = 3
        BN_EPS = 1e-05
        key = jax.random.key(seed)
        ks = jax.random.split(key, 8)
        x = jax.random.normal(ks[0], (N_NODES, D), dtype=jnp.float32)
        edge_index = jax.random.randint(ks[1], (2, N_EDGES), 0, N_NODES, dtype=jnp.int64)
        scale = 1.0 / np.sqrt(D)
        W_l = jax.random.normal(ks[2], (N_LAYERS, D, D), dtype=jnp.float32) * scale
        W_r = jax.random.normal(ks[3], (N_LAYERS, D, D), dtype=jnp.float32) * scale
        b = jax.random.normal(ks[4], (N_LAYERS, D), dtype=jnp.float32) * scale
        gamma = jnp.ones((N_LAYERS, D), dtype=jnp.float32)
        beta = jnp.zeros((N_LAYERS, D), dtype=jnp.float32)
        run_mean = jnp.zeros((N_LAYERS, D), dtype=jnp.float32)
        run_var = jnp.ones((N_LAYERS, D), dtype=jnp.float32)
        return {'x': x, 'edge_index': edge_index, 'W_l': W_l, 'W_r': W_r, 'b': b, 'gamma': gamma, 'beta': beta, 'run_mean': run_mean, 'run_var': run_var}
    _L0_gnn_all = _L0_gnn_setup()
    _L0_gnn_in = {k: v for k, v in _L0_gnn_all.items() if k in ('W_l', 'W_r', 'b', 'gamma', 'beta', 'run_mean', 'run_var')}
    del _L0_gnn_all

    def _L1_gnn_setup():
        import jax, jax.numpy as jnp
        import numpy as np
        N = 6250
        D = 64
        DEG = 16
        H = 2
        ALPHA = 0.2
        key = jax.random.key(seed)
        k1, k2, k3 = jax.random.split(key, 3)
        inputs = jax.random.normal(k1, (N, D), dtype=jnp.float32)
        rnd = jax.random.randint(k2, (2, N * DEG), 0, N)
        self_loops = jnp.tile(jnp.arange(N)[None, :], (2, 1))
        edge_index = jnp.concatenate([self_loops, rnd], axis=1)
        W = jnp.ones((H, D), dtype=jnp.float32)
        stdv = 1.0 / np.sqrt(D * 2)
        a = jax.random.uniform(k3, (H, 2 * D), dtype=jnp.float32, minval=-stdv, maxval=stdv)
        return {'inputs': inputs, 'edge_index': edge_index, 'W': W, 'a': a}
    _L1_gnn_all = _L1_gnn_setup()
    _L1_gnn_in = {k: v for k, v in _L1_gnn_all.items() if k in ('W', 'a')}
    del _L1_gnn_all

    def _L2_gnn_setup():
        import jax, jax.numpy as jnp
        import numpy as np
        N, E, L, HEADS, HID = (3125, 37500, 4, 8, 128)
        IN_C, OUT_C = (64, 64)
        D_HEAD = HID // HEADS

        def _layer_norm(x, g, b, eps=1e-05):
            m = jnp.mean(x, axis=-1, keepdims=True)
            v = jnp.mean((x - m) ** 2, axis=-1, keepdims=True)
            return (x - m) * jax.lax.rsqrt(v + eps) * g + b

        def _transformer_conv(h, src, dst, Wq, bq, Wk, bk, Wv, bv, Ws, bs, Wbeta):
            n, f = h.shape
            q = (h @ Wq.T + bq)[dst].reshape(-1, HEADS, D_HEAD)
            k = (h @ Wk.T + bk)[src].reshape(-1, HEADS, D_HEAD)
            v = (h @ Wv.T + bv)[src].reshape(-1, HEADS, D_HEAD)
            alpha = jnp.sum(q * k, axis=-1) / float(np.sqrt(D_HEAD))
            amax = jax.ops.segment_max(alpha, dst, num_segments=n)
            ex = jnp.exp(alpha - amax[dst])
            denom = jax.ops.segment_sum(ex, dst, num_segments=n)
            a = ex / (denom[dst] + 1e-16)
            out = jax.ops.segment_sum((a[:, :, None] * v).reshape(-1, f), dst, num_segments=n)
            x_r = h @ Ws.T + bs
            beta = jax.nn.sigmoid(jnp.concatenate([out, x_r, out - x_r], axis=-1) @ Wbeta.T)
            return beta * x_r + (1.0 - beta) * out

        def _forward(x, src, dst, Wi, bi, Wq, bq, Wk, bk, Wv, bv, Ws, bs, Wbeta, ln_g, ln_b, W1, b1, W2, b2, Wo, bo):
            h = jax.nn.gelu(x @ Wi.T + bi, approximate=False)
            for i in range(L):
                res = h
                h = _transformer_conv(h, src, dst, Wq[i], bq[i], Wk[i], bk[i], Wv[i], bv[i], Ws[i], bs[i], Wbeta[i])
                h = _layer_norm(h + res, ln_g[i], ln_b[i])
                res = h
                f = jax.nn.gelu(h @ W1[i].T + b1[i], approximate=False) @ W2[i].T + b2[i]
                h = f + res
            return h @ Wo.T + bo
        key = jax.random.key(seed)
        ks = jax.random.split(key, 24)
        rn = lambda k, shp, s=0.05: jax.random.normal(k, shp, jnp.float32) * s
        x = jax.random.normal(ks[0], (N, IN_C), jnp.float32)
        edge_index = jax.random.randint(ks[1], (2, E), 0, N, dtype=jnp.int64)
        return {'x': x, 'edge_index': edge_index, 'Wi': rn(ks[2], (HID, IN_C)), 'bi': jnp.zeros((HID,), jnp.float32), 'Wq': rn(ks[3], (L, HID, HID)), 'bq': jnp.zeros((L, HID), jnp.float32), 'Wk': rn(ks[4], (L, HID, HID)), 'bk': jnp.zeros((L, HID), jnp.float32), 'Wv': rn(ks[5], (L, HID, HID)), 'bv': jnp.zeros((L, HID), jnp.float32), 'Ws': rn(ks[6], (L, HID, HID)), 'bs': jnp.zeros((L, HID), jnp.float32), 'Wbeta': rn(ks[7], (L, 1, 3 * HID)), 'ln_g': jnp.ones((L, HID), jnp.float32), 'ln_b': jnp.zeros((L, HID), jnp.float32), 'W1': rn(ks[8], (L, 4 * HID, HID)), 'b1': jnp.zeros((L, 4 * HID), jnp.float32), 'W2': rn(ks[9], (L, HID, 4 * HID)), 'b2': jnp.zeros((L, HID), jnp.float32), 'Wo': rn(ks[10], (OUT_C, HID)), 'bo': jnp.zeros((OUT_C,), jnp.float32)}
    _L2_gnn_all = _L2_gnn_setup()
    _L2_gnn_in = {k: v for k, v in _L2_gnn_all.items() if k in ('Wi', 'bi', 'Wq', 'bq', 'Wk', 'bk', 'Wv', 'bv', 'Ws', 'bs', 'Wbeta', 'ln_g', 'ln_b', 'W1', 'b1', 'W2', 'b2', 'Wo', 'bo')}
    del _L2_gnn_all

    def _L3_gnn_setup():
        import jax, jax.numpy as jnp
        import numpy as np
        N = 6250
        E = 100000
        DIM = 64
        H = 4
        D = 8
        DH = D * H
        VD = DIM // H
        RPE_IN = 18
        key = jax.random.key(seed)
        ks = jax.random.split(key, 12)
        x = jax.random.normal(ks[0], (N, DIM), dtype=jnp.float32)
        edge_index = jax.random.randint(ks[1], (2, E), 0, N, dtype=jnp.int64)
        edge_attr = jax.random.normal(ks[2], (E, RPE_IN), dtype=jnp.float32)
        sc = lambda fan_in: 1.0 / np.sqrt(fan_in)
        qkv_w = jax.random.uniform(ks[3], (DIM, 2 * DH + DIM), jnp.float32, -sc(DIM), sc(DIM))
        qkv_b = jax.random.uniform(ks[4], (2 * DH + DIM,), jnp.float32, -sc(DIM), sc(DIM))
        k_rpe_w = jax.random.uniform(ks[5], (RPE_IN, DH), jnp.float32, -sc(RPE_IN), sc(RPE_IN))
        k_rpe_b = jax.random.uniform(ks[6], (DH,), jnp.float32, -sc(RPE_IN), sc(RPE_IN))
        q_rpe_w = jax.random.uniform(ks[7], (RPE_IN, DH), jnp.float32, -sc(RPE_IN), sc(RPE_IN))
        q_rpe_b = jax.random.uniform(ks[8], (DH,), jnp.float32, -sc(RPE_IN), sc(RPE_IN))
        v_rpe_w = jax.random.uniform(ks[9], (RPE_IN, DIM), jnp.float32, -sc(RPE_IN), sc(RPE_IN))
        v_rpe_b = jax.random.uniform(ks[10], (DIM,), jnp.float32, -sc(RPE_IN), sc(RPE_IN))
        return {'x': x, 'edge_index': edge_index, 'edge_attr': edge_attr, 'qkv_w': qkv_w, 'qkv_b': qkv_b, 'k_rpe_w': k_rpe_w, 'k_rpe_b': k_rpe_b, 'q_rpe_w': q_rpe_w, 'q_rpe_b': q_rpe_b, 'v_rpe_w': v_rpe_w, 'v_rpe_b': v_rpe_b}
    _L3_gnn_all = _L3_gnn_setup()
    _L3_gnn_in = {k: v for k, v in _L3_gnn_all.items() if k in ('qkv_w', 'qkv_b', 'k_rpe_w', 'k_rpe_b', 'q_rpe_w', 'q_rpe_b', 'v_rpe_w', 'v_rpe_b')}
    del _L3_gnn_all
    return {'x': x, 'src': src, 'dst': dst, 'edge_attr_18': edge_attr_18, 'L0_gnn_W_l': _L0_gnn_in['W_l'], 'L0_gnn_W_r': _L0_gnn_in['W_r'], 'L0_gnn_b': _L0_gnn_in['b'], 'L0_gnn_gamma': _L0_gnn_in['gamma'], 'L0_gnn_beta': _L0_gnn_in['beta'], 'L0_gnn_run_mean': _L0_gnn_in['run_mean'], 'L0_gnn_run_var': _L0_gnn_in['run_var'], 'L1_gnn_W': _L1_gnn_in['W'], 'L1_gnn_a': _L1_gnn_in['a'], 'L2_gnn_Wi': _L2_gnn_in['Wi'], 'L2_gnn_bi': _L2_gnn_in['bi'], 'L2_gnn_Wq': _L2_gnn_in['Wq'], 'L2_gnn_bq': _L2_gnn_in['bq'], 'L2_gnn_Wk': _L2_gnn_in['Wk'], 'L2_gnn_bk': _L2_gnn_in['bk'], 'L2_gnn_Wv': _L2_gnn_in['Wv'], 'L2_gnn_bv': _L2_gnn_in['bv'], 'L2_gnn_Ws': _L2_gnn_in['Ws'], 'L2_gnn_bs': _L2_gnn_in['bs'], 'L2_gnn_Wbeta': _L2_gnn_in['Wbeta'], 'L2_gnn_ln_g': _L2_gnn_in['ln_g'], 'L2_gnn_ln_b': _L2_gnn_in['ln_b'], 'L2_gnn_W1': _L2_gnn_in['W1'], 'L2_gnn_b1': _L2_gnn_in['b1'], 'L2_gnn_W2': _L2_gnn_in['W2'], 'L2_gnn_b2': _L2_gnn_in['b2'], 'L2_gnn_Wo': _L2_gnn_in['Wo'], 'L2_gnn_bo': _L2_gnn_in['bo'], 'L3_gnn_qkv_w': _L3_gnn_in['qkv_w'], 'L3_gnn_qkv_b': _L3_gnn_in['qkv_b'], 'L3_gnn_k_rpe_w': _L3_gnn_in['k_rpe_w'], 'L3_gnn_k_rpe_b': _L3_gnn_in['k_rpe_b'], 'L3_gnn_q_rpe_w': _L3_gnn_in['q_rpe_w'], 'L3_gnn_q_rpe_b': _L3_gnn_in['q_rpe_b'], 'L3_gnn_v_rpe_w': _L3_gnn_in['v_rpe_w'], 'L3_gnn_v_rpe_b': _L3_gnn_in['v_rpe_b']}

def reference(x, src, dst, edge_attr_18, L0_gnn_W_l, L0_gnn_W_r, L0_gnn_b, L0_gnn_gamma, L0_gnn_beta, L0_gnn_run_mean, L0_gnn_run_var, L1_gnn_W, L1_gnn_a, L2_gnn_Wi, L2_gnn_bi, L2_gnn_Wq, L2_gnn_bq, L2_gnn_Wk, L2_gnn_bk, L2_gnn_Wv, L2_gnn_bv, L2_gnn_Ws, L2_gnn_bs, L2_gnn_Wbeta, L2_gnn_ln_g, L2_gnn_ln_b, L2_gnn_W1, L2_gnn_b1, L2_gnn_W2, L2_gnn_b2, L2_gnn_Wo, L2_gnn_bo, L3_gnn_qkv_w, L3_gnn_qkv_b, L3_gnn_k_rpe_w, L3_gnn_k_rpe_b, L3_gnn_q_rpe_w, L3_gnn_q_rpe_b, L3_gnn_v_rpe_w, L3_gnn_v_rpe_b):
    import jax
    import jax.numpy as jnp

    def _L0_gnn_ref(x, edge_index, W_l, W_r, b, gamma, beta, run_mean, run_var):
        import jax, jax.numpy as jnp
        import numpy as np
        N_NODES = 6250
        N_EDGES = 100000
        D = 64
        N_LAYERS = 3
        BN_EPS = 1e-05
        n = x.shape[0]
        src, dst = (edge_index[0], edge_index[1])
        cnt = jax.ops.segment_sum(jnp.ones((src.shape[0],), x.dtype), dst, num_segments=n)
        denom = jnp.maximum(cnt, 1.0)[:, None]
        for i in range(N_LAYERS):
            agg = jax.ops.segment_sum(x[src], dst, num_segments=n) / denom
            h = agg @ W_l[i] + x @ W_r[i] + b[i]
            h = (h - run_mean[i]) * jax.lax.rsqrt(run_var[i] + BN_EPS) * gamma[i] + beta[i]
            x = jax.nn.elu(h)
        return x

    def _L1_gnn_ref(inputs, edge_index, W, a):
        import jax, jax.numpy as jnp
        import numpy as np
        N = 6250
        D = 64
        DEG = 16
        H = 2
        ALPHA = 0.2
        n = inputs.shape[0]
        row, col = (edge_index[0], edge_index[1])

        def head(Wh, ah):
            h = inputs * Wh
            score = (h @ ah[:D])[row] + (h @ ah[D:])[col]
            e = jnp.exp(jnp.where(score > 0, score, ALPHA * score))
            rowsum = jax.ops.segment_sum(e, row, num_segments=n)
            h_prime = jax.ops.segment_sum(e[:, None] * inputs[col], row, num_segments=n)
            return h_prime / rowsum[:, None]
        outs = jax.vmap(head)(W, a)
        return outs.mean(axis=0)

    def _L2_gnn_ref(x, edge_index, Wi, bi, Wq, bq, Wk, bk, Wv, bv, Ws, bs, Wbeta, ln_g, ln_b, W1, b1, W2, b2, Wo, bo):
        import jax, jax.numpy as jnp
        import numpy as np
        N, E, L, HEADS, HID = (3125, 37500, 4, 8, 128)
        IN_C, OUT_C = (64, 64)
        D_HEAD = HID // HEADS

        def _layer_norm(x, g, b, eps=1e-05):
            m = jnp.mean(x, axis=-1, keepdims=True)
            v = jnp.mean((x - m) ** 2, axis=-1, keepdims=True)
            return (x - m) * jax.lax.rsqrt(v + eps) * g + b

        def _transformer_conv(h, src, dst, Wq, bq, Wk, bk, Wv, bv, Ws, bs, Wbeta):
            n, f = h.shape
            q = (h @ Wq.T + bq)[dst].reshape(-1, HEADS, D_HEAD)
            k = (h @ Wk.T + bk)[src].reshape(-1, HEADS, D_HEAD)
            v = (h @ Wv.T + bv)[src].reshape(-1, HEADS, D_HEAD)
            alpha = jnp.sum(q * k, axis=-1) / float(np.sqrt(D_HEAD))
            amax = jax.ops.segment_max(alpha, dst, num_segments=n)
            ex = jnp.exp(alpha - amax[dst])
            denom = jax.ops.segment_sum(ex, dst, num_segments=n)
            a = ex / (denom[dst] + 1e-16)
            out = jax.ops.segment_sum((a[:, :, None] * v).reshape(-1, f), dst, num_segments=n)
            x_r = h @ Ws.T + bs
            beta = jax.nn.sigmoid(jnp.concatenate([out, x_r, out - x_r], axis=-1) @ Wbeta.T)
            return beta * x_r + (1.0 - beta) * out

        def _forward(x, src, dst, Wi, bi, Wq, bq, Wk, bk, Wv, bv, Ws, bs, Wbeta, ln_g, ln_b, W1, b1, W2, b2, Wo, bo):
            h = jax.nn.gelu(x @ Wi.T + bi, approximate=False)
            for i in range(L):
                res = h
                h = _transformer_conv(h, src, dst, Wq[i], bq[i], Wk[i], bk[i], Wv[i], bv[i], Ws[i], bs[i], Wbeta[i])
                h = _layer_norm(h + res, ln_g[i], ln_b[i])
                res = h
                f = jax.nn.gelu(h @ W1[i].T + b1[i], approximate=False) @ W2[i].T + b2[i]
                h = f + res
            return h @ Wo.T + bo
        src, dst = (edge_index[0], edge_index[1])
        return _forward(x, src, dst, Wi, bi, Wq, bq, Wk, bk, Wv, bv, Ws, bs, Wbeta, ln_g, ln_b, W1, b1, W2, b2, Wo, bo)

    def _L3_gnn_ref(x, edge_index, edge_attr, qkv_w, qkv_b, k_rpe_w, k_rpe_b, q_rpe_w, q_rpe_b, v_rpe_w, v_rpe_b):
        import jax, jax.numpy as jnp
        import numpy as np
        N = 6250
        E = 100000
        DIM = 64
        H = 4
        D = 8
        DH = D * H
        VD = DIM // H
        RPE_IN = 18
        n = x.shape[0]
        e = edge_index.shape[1]
        qkv = x @ qkv_w + qkv_b
        q = qkv[:, :DH].reshape(n, H, D)
        k = qkv[:, DH:2 * DH].reshape(n, H, D)
        v = qkv[:, 2 * DH:].reshape(n, H, VD)
        s = edge_index[0]
        t = edge_index[1]
        scale = jnp.float32(D) ** (-0.5)
        qe = q[s] * scale
        qe = qe + (edge_attr @ q_rpe_w + q_rpe_b).reshape(e, H, D)
        ke = k[t] + (edge_attr @ k_rpe_w + k_rpe_b).reshape(e, H, D)
        ve = v[t] + (edge_attr @ v_rpe_w + v_rpe_b).reshape(e, H, VD)
        compat = jnp.einsum('ehd,ehd->eh', qe, ke)
        m = jax.ops.segment_max(compat, s, num_segments=n)
        ex = jnp.exp(compat - m[s])
        den = jax.ops.segment_sum(ex, s, num_segments=n)
        attn = ex / (den[s] + 1e-16)
        msg = (ve * attn[..., None]).reshape(e, DIM)
        out = jax.ops.segment_sum(msg, s, num_segments=n)
        return out
    edge_index = jnp.stack([src, dst])
    h = jnp.maximum(_layernorm(x, axis=-1), 0.0)
    x = x + _L0_gnn_ref(h, edge_index, L0_gnn_W_l, L0_gnn_W_r, L0_gnn_b, L0_gnn_gamma, L0_gnn_beta, L0_gnn_run_mean, L0_gnn_run_var)
    h = jnp.maximum(_layernorm(x, axis=-1), 0.0)
    x = x + _L1_gnn_ref(h, edge_index, L1_gnn_W, L1_gnn_a)
    h = jnp.maximum(_layernorm(x, axis=-1), 0.0)
    x = x + _L2_gnn_ref(h, edge_index, L2_gnn_Wi, L2_gnn_bi, L2_gnn_Wq, L2_gnn_bq, L2_gnn_Wk, L2_gnn_bk, L2_gnn_Wv, L2_gnn_bv, L2_gnn_Ws, L2_gnn_bs, L2_gnn_Wbeta, L2_gnn_ln_g, L2_gnn_ln_b, L2_gnn_W1, L2_gnn_b1, L2_gnn_W2, L2_gnn_b2, L2_gnn_Wo, L2_gnn_bo)
    h = jnp.maximum(_layernorm(x, axis=-1), 0.0)
    x = x + _L3_gnn_ref(h, edge_index, edge_attr_18, L3_gnn_qkv_w, L3_gnn_qkv_b, L3_gnn_k_rpe_w, L3_gnn_k_rpe_b, L3_gnn_q_rpe_w, L3_gnn_q_rpe_b, L3_gnn_v_rpe_w, L3_gnn_v_rpe_b)
    return x

_drawn_inputs = setup_inputs


def setup_inputs(seed=0):
    import zlib

    import numpy as np

    out = dict(_drawn_inputs(seed))
    spreads = {'L0_gnn_gamma': (1.0, 0.2),
     'L0_gnn_beta': (0.0, 0.1),
     'L0_gnn_run_mean': (0.0, 0.1),
     'L0_gnn_run_var': (1.0, 0.2),
     'L1_gnn_W': (1.0, 0.6),
     'L2_gnn_bi': (0.0, 0.1),
     'L2_gnn_bq': (0.0, 0.8),
     'L2_gnn_bk': (0.0, 0.8),
     'L2_gnn_bv': (0.0, 0.1),
     'L2_gnn_bs': (0.0, 0.1),
     'L2_gnn_ln_g': (1.0, 0.2),
     'L2_gnn_ln_b': (0.0, 0.1),
     'L2_gnn_b1': (0.0, 0.1),
     'L2_gnn_b2': (0.0, 0.1),
     'L2_gnn_bo': (0.0, 0.1)}
    factors = {'L1_gnn_a': 4.931, 'L2_gnn_Wq': 8.0, 'L2_gnn_Wk': 8.0}
    for name, (base, spread) in spreads.items():
        noise = np.random.default_rng([zlib.crc32(name.encode()), seed]).standard_normal(out[name].shape)
        drawn = base * np.exp(spread * noise) if base else spread * noise
        out[name] = jnp.asarray(drawn.astype(out[name].dtype))
    for name, factor in factors.items():
        out[name] = (out[name] * factor).astype(out[name].dtype)
    return out
```

```python
from contextlib import ExitStack

import numpy as np
import concourse.bass as bass
from concourse import mybir

F32 = mybir.dt.float32
I32 = mybir.dt.int32
BF = mybir.dt.bfloat16
ALU = mybir.AluOpType
ACT = mybir.ActivationFunctionType
AX = mybir.AxisListType

N, E, B = 6250, 100000, 49
NP = B * 128
EP, ET = 125, 800
T = 832
NG = T // 16
SLOTS = T * 128
BIG = 1.0e30
LEAD = 512


class Count:

    def __init__(self, g, sem, step=1, eng=None):
        self.g, self.sem, self.step, self.at = g, sem, step, 0
        self.enter, self.eng = 0, eng
        g.counts.append(self)

    def inc(self, ins, label=None):
        ins.then_inc(self.sem, self.step)
        if self.eng is not None:
            self.g.waited = {w for w in self.g.waited if w[0] != self.eng.engine}
        self.at += self.step
        return self.now(label)

    def now(self, label=None):
        t = (self, self.at)
        if label is not None:
            self.g.plan[(self.g.loop_no, label)] = self.at - self.enter
        return t


class Gen:

    def __init__(self, nc, plan, dry):
        self.nc, self.plan, self.dry = nc, plan, dry
        self.counts, self.i, self.loop_no, self.n_loops = [], None, None, 0
        self.waited = set()

    def loop(self, n):
        return Loop(self, n)

    def wait(self, eng, *toks):
        for tok in toks:
            if tok is None:
                continue
            c, v = tok
            if self.i is not None and v > c.enter:
                per = self.plan.get((self.loop_no, id_of(self, c)), 1)
                self.wait_reg(eng, c, self.i * per + v)
            elif v > 0:
                eng.wait_ge(c.sem, v)

    def wait_reg(self, eng, c, v):
        if (eng.engine, c.sem) in self.waited:
            eng.sem_inc(self.misc, 1)
            self.waited = {w for w in self.waited if w[0] != eng.engine}
        eng.wait_ge(c.sem, v)
        if eng is self.nc.sync:
            eng.sem_inc(self.misc, 1)
        else:
            self.waited.add((eng.engine, c.sem))

    def before(self, eng, c, label):
        per = self.plan.get((self.loop_no, id_of(self, c)), 1)
        at = self.plan.get((self.loop_no, label), 1)
        v = c.enter + at - per
        assert self.dry or v > 0
        self.wait_reg(eng, c, self.i * per + max(v, 1))


def id_of(g, c):
    return ("per", g.counts.index(c))


class Loop:
    def __init__(self, g, n):
        self.g, self.n = g, n

    def __enter__(self):
        g = self.g
        g.loop_no = g.n_loops
        g.n_loops += 1
        for c in g.counts:
            c.enter = c.at
        self.f = g.nc.Fori(0, self.n)
        g.i = self.f.__enter__()
        return g.i

    def __exit__(self, *a):
        g = self.g
        for c in g.counts:
            per = c.at - c.enter
            key = (g.loop_no, id_of(g, c))
            assert g.dry or g.plan.get(key) == per
            g.plan[key] = per
            c.at = c.enter + per * self.n
            c.enter = 0
        g.i = g.loop_no = None
        self.f.__exit__(*a)


def build(nc, d, plan, dry, stop=None, dbg=None):
    with ExitStack() as ctx:
        g = Gen(nc, plan, dry)
        sp, act, dve, pe, pool = nc.sync, nc.scalar, nc.vector, nc.tensor, nc.gpsimd

        def sb(name, shape, dt=F32):
            return ctx.enter_context(nc.sbuf_tensor(name, shape, dt))

        def dram(name, shape, dt=F32):
            return nc.dram_tensor(name, shape, dt, kind="Internal").ap()

        def count(name, step=1, eng=None):
            return Count(g, ctx.enter_context(nc.semaphore(name)), step, eng)

        PS = [ctx.enter_context(nc.psum_tensor(f"ps{i}", [128, 512], F32)) for i in range(8)]

        cv, cs = count("c_dve", 1, dve), count("c_act", 1, act)
        cp, cg = count("c_pe", 1, pe), count("c_pool", 1, pool)
        misc = count("c_misc")
        g.misc = misc.sem
        cx = [count(f"c_x{k}", 16) for k in range(8)]
        ca = [count(f"c_in{k}", 16) for k in range(2)]
        cb = [count(f"c_out{k}", 16) for k in range(2)]
        cl, ck = count("c_load", 16), count("c_pre", 16)
        for c in [c for c in g.counts if c not in cx]:
            sp.sem_inc(c.sem, LEAD)
            c.at = LEAD
        nc.all_engine_barrier()

        def V(ins, label=None):
            return cv.inc(ins, label)

        def A(ins, label=None):
            return cs.inc(ins, label)

        def M(ins, label=None):
            return cp.inc(ins, label)

        def G(ins, label=None):
            return cg.inc(ins, label)

        def VV(ins):
            t = cv.inc(ins)
            g.wait(dve, t)
            return t

        def AA(ins):
            t = cs.inc(ins)
            g.wait(act, t)
            return t

        def phase():
            for c in [*cx, *ca, *cb, cl, ck]:
                g.wait(sp, c.now())
            nc.all_engine_barrier()

        def regs(eng, n, name):
            return [eng.alloc_register(f"{name}{k}") for k in range(n)]

        R_dve, R_pe = regs(dve, 8, "bd"), regs(pe, 8, "bp")

        iota = sb("iota", [128, 128])
        iotab = sb("iotab", [128, 128], BF)
        ident = sb("ident", [128, 128])
        identb = sb("identb", [128, 128], BF)
        tri = sb("tri", [128, 128])
        ones = sb("ones", [128, 128])
        zer = sb("zer", [128, 128], BF)
        io = lambda out, pat, cm: pool.iota(out, pat, base=0, channel_multiplier=cm,
                                            allow_small_or_imprecise_dtypes=True)
        G(io(iota[:, :], [[1, 128]], 0))
        G(io(iotab[:, :], [[1, 128]], 0))
        G(io(tri[:, :], [[1, 128]], -1))
        V(dve.memset(ones[:, :], 1.0))
        V(dve.memset(zer[:, :], 0.0))
        g.wait(dve, cg.now())
        V(dve.tensor_scalar(ident[:, :], tri[:, :], 0.0, None, ALU.is_equal))
        VV(dve.tensor_scalar(identb[:, :], tri[:, :], 0.0, None, ALU.is_equal))
        VV(dve.tensor_scalar(tri[:, :], tri[:, :], 0.0, None, ALU.is_lt))

        phase()

        def hold(eng):
            eng.sem_inc(misc.sem, 1)

        idx = [sb(f"idx{k}", [128, T], I32) for k in range(2)]
        node = [sb(f"node{k}", [128, T]) for k in range(2)]
        loc = [sb(f"loc{k}", [128, T]) for k in range(2)]
        bI = [sb(f"bI{k}", [1, T], I32) for k in range(2)]
        cnt = sb("cnt", [B, 128])

        WORK = sb("work", [128, 38400])

        def area(off, shape, dt=F32):
            n = int(np.prod(shape[1:]))
            w = n if dt != BF else n // 2
            v = WORK[0:shape[0], off:off + w]
            if dt != F32:
                v = v.bitcast(dt)
            if len(shape) == 3:
                v = v.rearrange("p (a b) -> p a b", a=shape[1])
            elif len(shape) == 4:
                v = v.rearrange("p (a b c) -> p a b c", a=shape[1], b=shape[2])
            return v, off + w

        first, _ = area(0, [128, 8, 2], I32)
        zi, _ = area(16, [128, 1], I32)
        g.wait(pool, V(dve.memset(zi, 0)))
        for k in range(8):
            cx[k].inc(pool.indirect_dma_start(first[:, k, :], None, d["pair"].rearrange("p t w -> (p t) w"),
                                              bass.IndirectOffsetOnAxis(ap=zi, axis=0)))
        phase()

        WT = [2, 20]
        tab = [dram("tab0", [SLOTS, 2], I32), dram("tab1", [SLOTS, 20], I32)]

        def group_edges(k):
            W = WT[k]
            key_d, keyT_d = (d["dst"], d["dstT"]) if k == 0 else (d["src"], d["srcT"])
            o = 0
            ki, o = area(o, [EP, ET], I32)
            kf, o = area(o, [EP, ET])
            hi, o = area(o, [EP, ET])
            lo, o = area(o, [EP, ET])
            t1, o = area(o, [EP, ET], I32)
            fill, o = area(o, [128, 52, W], I32)
            OHh, o = area(o, [EP, 2, 16, 64], BF)
            OHl, o = area(o, [EP, 2, 16, 128], BF)
            OHhT, o = area(o, [50, 2, 16, 128])
            KT, o = area(o, [EP, 2, 16, EP], I32)
            junk, o = area(o, [EP, 16, 128])
            Rs, o = area(o, [B, 2, 128])
            PAY, o = area(o, [EP, 2, 16, W], I32)
            POS, o = area(o, [EP, 2, 16])
            RNK, o = area(o, [EP, 2, 16])
            kg, o = area(o, [EP, 2, 16])
            hg, o = area(o, [EP, 2, 16, 2])
            ti, o = area(o, [EP, 2, 16], I32)
            tf, o = area(o, [EP, 2, 16])
            rowI, o = area(o, [EP, 2, 16], I32)
            s1, o = area(o, [B, 128])
            s2, o = area(o, [B, 128])
            c1, o = area(o, [B, 8])
            c1i, o = area(o, [B, 8], I32)
            cmp, o = area(o, [B, T])
            tio, o = area(o, [B, T])
            assert o <= 38400, o
            cl.inc(sp.dma_start(ki, key_d))
            V(dve.memset(fill, 0))
            g.wait(dve, cv.now())
            V(dve.memset(fill[:, :, 0 if k else 1], -1))
            g.wait(act, cv.now())
            for q in range(16):
                ck.inc(act.dma_start(tab[k].rearrange("(p q a) w -> p q (a w)", p=128, q=16)[:, q, :],
                                     fill.rearrange("p a w -> p (a w)")))
            G(io(tio, [[1, T]], 0))
            g.wait(dve, cl.now(), cg.now())
            V(dve.tensor_scalar(t1, ki, 7, None, ALU.arith_shift_right))
            V(dve.tensor_copy(kf, ki))
            g.wait(dve, cv.now())
            VV(dve.tensor_copy(hi, t1))
            VV(dve.tensor_scalar(t1, ki, 127, None, ALU.bitwise_and))
            VV(dve.tensor_copy(lo, t1))
            H = PS[0][0:B, 0:128]
            M(pe.matmul(H, zer[:, 0:B], zer[:, :], start=True, stop=False, skip_group_check=True))
            phase()

            def onehots(i, u):
                a = i * 32 + 16 * u
                V(dve.tensor_tensor(OHh[:, u, :, 0:50],
                                    iota[0:EP, None, 0:50].to_broadcast([EP, 16, 50]),
                                    hi[:, bass.ds(a, 16)][:, :, None].to_broadcast([EP, 16, 50]),
                                    ALU.is_equal))
                return V(dve.tensor_tensor(OHl[:, u, :, :],
                                           iota[0:EP, None, :].to_broadcast([EP, 16, 128]),
                                           lo[:, bass.ds(a, 16)][:, :, None].to_broadcast([EP, 16, 128]),
                                           ALU.is_equal))

            with g.loop(ET // 32) as i:
                for u in range(2):
                    g.before(dve, cp, f"h{u}")
                    t = onehots(i, u)
                    g.wait(pe, t)
                    for n in range(16):
                        mm = pe.matmul(H, OHh[:, u, n, 0:B], OHl[:, u, n, :], start=False, stop=False,
                                       skip_group_check=True)
                    M(mm, f"h{u}")
            phase()
            VV(dve.tensor_copy(s1, H))
            if k == 0:
                V(dve.tensor_copy(cnt[:, :], s1))
            VV(dve.tensor_tensor_scan(s2, ones[0:B, :], s1, 0.0, ALU.mult, ALU.add))
            VV(dve.tensor_scalar(c1[:, 0:1], s2[:, 127:128], 127.0, None, ALU.add))
            VV(dve.tensor_copy(c1i[:, 0:1], c1[:, 0:1]))
            VV(dve.tensor_scalar(c1i[:, 1:2], c1i[:, 0:1], 7, None, ALU.arith_shift_right))
            VV(dve.tensor_copy(c1[:, 1:2], c1i[:, 1:2]))
            VV(dve.tensor_tensor(s1, s2, s1, ALU.subtract))
            g.wait(pe, cv.now())
            g.wait(dve, M(pe.transpose(PS[1][0:B, 0:B], tri[0:B, 0:B], ident[0:B, 0:B])))
            g.wait(pe, VV(dve.tensor_copy(cmp[:, 0:B], PS[1][0:B, 0:B])))
            g.wait(dve, M(pe.matmul(PS[1][0:B, 64:65], cmp[:, 0:B], c1[:, 1:2], start=True, stop=True)))
            VV(dve.tensor_copy(c1[:, 2:3], PS[1][0:B, 64:65]))
            VV(dve.tensor_scalar(c1[:, 3:4], c1[:, 2:3], 128.0, None, ALU.mult))
            VV(dve.tensor_scalar(s1, s1, c1[:, 3:4], None, ALU.add))
            VV(dve.tensor_scalar(cmp, tio, c1[:, 2:3], None, ALU.is_ge))
            g.wait(pe, cv.now())
            R = PS[0][0:B, 0:128]
            pe.matmul(PS[2][:, 0:416], ones[0:B, :], cmp[:, 0:416], start=True, stop=True)
            pe.matmul(PS[3][:, 0:416], ones[0:B, :], cmp[:, 416:832], start=True, stop=True)
            M(pe.matmul(R, ident[0:B, 0:B], s1, start=True, stop=False, skip_group_check=True))
            g.wait(dve, cp.now())
            for q in range(2):
                V(dve.tensor_scalar(loc[k][:, 416 * q:416 * q + 416], PS[2 + q][:, 0:416], -1.0, None, ALU.add))
                V(dve.tensor_scalar(bI[k][0:1, 416 * q:416 * q + 416], PS[2 + q][0:1, 0:416], -1.0, None, ALU.add))
            g.wait(act, cp.now())
            A(act.copy(Rs[:, 0, :], R))
            phase()

            BT = [PS[2][0:50, :].bitcast(BF), PS[3][0:50, :].bitcast(BF), PS[4][0:50, :].bitcast(BF), PS[5][0:50, :].bitcast(BF)]
            with g.loop(ET // 32) as i:
                for u in range(2):
                    a = i * 32 + 16 * u
                    g.before(sp, cv, f"rank{u}")
                    for n in range(4):
                        g.before(sp, cx[4 * u + n], f"sc{n}.{u}")
                    kt = ca[u].inc(sp.dma_start(KT[:, u, :, :], keyT_d[bass.ds(a, 16), :][None, :, :].to_broadcast([EP, 16, EP])))
                    pt = cb[u].inc(sp.dma_start(PAY[:, u, :, 0:2], d["pair"][:, bass.ds(a, 16), :]))
                    if k:
                        pt = cb[u].inc(sp.dma_start(PAY[:, u, :, 2:20], d["attr"][:, bass.ds(a, 16), :].bitcast(I32)))
                    g.before(dve, cp, f"acc15.{u}")
                    g.before(dve, cp, f"tr{u}")
                    oh = onehots(i, u)
                    V(dve.tensor_copy(kg[:, u, :], kf[:, bass.ds(a, 16)]))
                    g.wait(pe, oh)
                    g.before(pe, cs, f"ohT{u}")
                    hold(pe)
                    for n in range(16):
                        mm = pe.transpose(BT[2 * u + n // 8][:, 128 * (n % 8):128 * (n % 8) + EP], OHh[:, u, n, 0:50],
                                          identb[0:EP, 0:EP])
                    tr = M(mm, f"tr{u}")
                    g.wait(act, tr)
                    g.before(act, cp, f"acc15.{u}")
                    for q in range(2):
                        oht = A(act.copy(OHhT[:, u, 8 * q:8 * q + 8, 0:EP],
                                         BT[2 * u + q].rearrange("p (n e) -> p n e", n=8)[:, :, 0:EP]), f"ohT{u}")
                    g.wait(dve, kt, cv.now())
                    for n in range(16):
                        jw = V(dve.scalar_tensor_tensor(junk[:, n, 0:EP], KT[:, u, n, :], kg[:, u, n:n + 1],
                                                   tri[0:EP, 0:EP], ALU.is_equal, ALU.mult,
                                                   accum_out=RNK[:, u, n:n + 1]), f"rank{u}")
                    g.wait(dve, jw)
                    for n in range(16):
                        SEL = PS[6 + n % 2][0:EP, 0:128]
                        if n == 0:
                            g.wait(pe, oht)
                        if u == 0 and n < 1:
                            g.before(pe, cs, "snap15.1")
                            g.before(pe, cv, "pos14.1")
                        else:
                            g.wait(pe, snap)
                        if not (u == 0 and n < 2):
                            g.wait(pe, pos[n % 2])
                        elif n == 1:
                            g.before(pe, cv, "pos15.1")
                        m1 = M(pe.matmul(SEL, OHhT[:, u, n, 0:EP][0:B, :], Rs[:, n % 2, :], start=True, stop=True))
                        m2 = M(pe.matmul(R, OHh[:, u, n, 0:B], OHl[:, u, n, :], start=False, stop=False,
                                         skip_group_check=True), f"acc{n}.{u}")
                        g.wait(act, m2)
                        snap = A(act.copy(Rs[:, (n + 1) % 2, :], R), f"snap{n}.{u}")
                        g.wait(dve, m1)
                        p_ = V(dve.scalar_tensor_tensor(junk[:, n, :], SEL, 1.0, OHl[:, u, n, :],
                                                        ALU.mult, ALU.mult, accum_out=POS[:, u, n:n + 1]), f"pos{n}.{u}")
                        pos = (p_, pos[1]) if n % 2 == 0 and (u or n) else ((p_, None) if n == 0 else (pos[0], p_))
                    g.wait(dve, p_)
                    VV(dve.tensor_tensor(POS[:, u, :], POS[:, u, :], RNK[:, u, :], ALU.add))
                    VV(dve.tensor_copy(ti[:, u, :], POS[:, u, :]))
                    VV(dve.tensor_scalar(rowI[:, u, :], ti[:, u, :], 7, None, ALU.arith_shift_right))
                    VV(dve.tensor_copy(tf[:, u, :], rowI[:, u, :]))
                    VV(dve.scalar_tensor_tensor(POS[:, u, :], tf[:, u, :], -128.0, POS[:, u, :], ALU.mult, ALU.add))
                    VV(dve.scalar_tensor_tensor(tf[:, u, :], POS[:, u, :], float(T), tf[:, u, :], ALU.mult, ALU.add))
                    for n in range(4):
                        g.before(dve, cx[4 * u + n], f"sc{n}.{u}")
                    ro = V(dve.tensor_copy(rowI[:, u, :], tf[:, u, :]))
                    g.wait(pool, ro, pt)
                    hold(pool)
                    for n in range(16):
                        cx[4 * u + n // 4].inc(pool.indirect_dma_start(
                            tab[k], bass.IndirectOffsetOnAxis(ap=rowI[:, u, n:n + 1], axis=0),
                            PAY[:, u, n, :], None), f"sc{n // 4}.{u}")
            phase()
            S4 = T // 4
            stage, _ = area(0, [128, S4, W], I32)
            bF, _ = area(S4 * W, [128, T])
            V(dve.tensor_copy(bF, loc[k][:, :]))
            for q in range(4):
                g.wait(sp, cv.now())
                ld = cl.inc(sp.dma_start(stage, tab[k].rearrange("(p t) w -> p t w", p=128)[:, S4 * q:S4 * q + S4, :]))
                g.wait(dve, ld)
                V(dve.tensor_copy(idx[k][:, S4 * q:S4 * q + S4], stage[:, :, 1 if k else 0]))
                VV(dve.tensor_copy(node[k][:, S4 * q:S4 * q + S4], stage[:, :, 0 if k else 1]))
            VV(dve.scalar_tensor_tensor(loc[k][:, :], bF, -128.0, node[k][:, :], ALU.mult, ALU.add))
            phase()

        def out_dbg(name, ap, dtype=F32):
            o = nc.dram_tensor(name, list(ap.shape), dtype, kind="ExternalOutput").ap()
            cl.inc(sp.dma_start(o, ap))
            phase()

        group_edges(0)
        x = sb("x", [128, B, 64])
        padm = sb("padm", [128, B])

        def bc(v, shape):
            return v.to_broadcast(shape)

        def load(dst, name, src=None):
            return cl.inc(sp.dma_start(dst, d[name] if src is None else src))

        def loadb(dst, ap1):
            return cl.inc(sp.dma_start(dst, ap1[None, :].to_broadcast([128, ap1.shape[0]])))

        def norm(out, src, F, st, relu, gam=None, bet=None, sq=None):
            m, v = st[:, 0, :], st[:, 1, :]
            VV(dve.tensor_reduce(m, src, AX.X, ALU.add))
            VV(dve.tensor_scalar(m, m, 1.0 / F, None, ALU.mult))
            VV(dve.tensor_tensor(out, src, bc(m[:, :, None], [128, B, F]), ALU.subtract))
            VV(dve.tensor_tensor(sq, out, out, ALU.mult))
            VV(dve.tensor_reduce(v, sq, AX.X, ALU.add))
            g.wait(act, VV(dve.tensor_scalar(v, v, 1.0 / F, 1e-5, ALU.mult, ALU.add)))
            g.wait(dve, A(act.sqrt(m, v)))
            VV(dve.reciprocal(v, m))
            VV(dve.tensor_tensor(out, out, bc(v[:, :, None], [128, B, F]), ALU.mult))
            if relu:
                VV(dve.tensor_scalar(out, out, 0.0, None, ALU.max))
            if gam is not None:
                VV(dve.tensor_tensor(out, out, bc(gam[:, None, :], [128, B, F]), ALU.mult))
                VV(dve.tensor_tensor(out, out, bc(bet[:, None, :], [128, B, F]), ALU.add))

        def dense(src, K, rhs, F, bias, CT, evac):
            done, copied = {}, {}
            n_out = 1 if F <= 128 else 4
            for c in range((B + 3) // 4):
                b0, nb = 4 * c, min(4, B - 4 * c)
                g.wait(pe, copied.get(c - 2))
                for j in range(nb):
                    mm = pe.transpose(PS[c % 2][0:K, 128 * j:128 * j + 128], src(b0 + j), ident[:, :])
                g.wait(act, M(mm))
                t = A(act.copy(CT[0:K, c % 2, 0:128 * nb], PS[c % 2][0:K, 0:128 * nb]))
                copied[c] = t
                g.wait(pe, t)
                if n_out == 1:
                    bank = [PS[2 + c % 2]]
                    g.wait(pe, *done.get(c - 2, []))
                    at = lambda j: bank[0][:, F * j:F * j + F]
                else:
                    bank = PS[2:2 + n_out]
                    g.wait(pe, *done.get(c - 1, []))
                    at = lambda j: bank[j][:, 0:F]
                for j in range(nb):
                    mm = pe.matmul(at(j), CT[0:K, c % 2, 128 * j:128 * j + 128], rhs, start=True, stop=bias is None)
                    if bias is not None:
                        mm = pe.matmul(at(j), ones[0:1, :], bias, start=False, stop=True)
                t = M(mm)
                if n_out == 1:
                    views = bank[0][:, 0:F * nb].rearrange("p (a f) -> p a f", a=nb)
                else:
                    views = [at(j) for j in range(nb)]
                done[c] = evac(c, b0, nb, views, t)

        def onehot_nodes(P, k, i, u):
            a = i * 16 + 8 * u
            return V(dve.tensor_tensor(P[:, u, :, :], bc(iota[:, None, :], [128, 8, 128]),
                                       bc(loc[k][:, bass.ds(a, 8)][:, :, None], [128, 8, 128]), ALU.is_equal),
                     f"P{u}")

        def blocks(eng, R, k, i, u):
            eng.load(R, bI[k][0:1, bass.ds(i * 16 + 8 * u, 8)])
            return [eng.snap(r, min_val=0, max_val=B - 1) for r in R]

        def gathers(table, X, RI, k, i, u, free):
            for c, label in free:
                g.before(pool, c, label)
            t = G(pool.tensor_copy(RI[:, u, :], idx[k][:, bass.ds(i * 16 + 8 * u, 8)]))
            g.wait(pool, t)
            hold(pool)
            return [cx[2 * u + n // 4].inc(pool.indirect_dma_start(
                X[:, u, n, :], None, table, bass.IndirectOffsetOnAxis(ap=RI[:, u, n:n + 1], axis=0)))
                for n in range(8)][3::4]

        def add_blocks(acc, bs, view, F, u, i):
            for n in range(8):
                t = V(dve.tensor_tensor(acc[:, bass.ds(bs[n], 1), :].rearrange("p a f -> p (a f)"),
                                        acc[:, bass.ds(bs[n], 1), :].rearrange("p a f -> p (a f)"),
                                        view(n), ALU.add), f"add{u}" if n == 7 else None)
                g.wait(dve, t)

        def transposed(P, PT, u, bank):
            g.before(pe, cs, f"PT{u}")
            if u:
                g.wait(pe, g.ptc)
            else:
                g.before(pe, cs, "PT1")
            hold(pe)
            for n in range(8):
                mm = pe.transpose(PS[bank + n // 4][:, 128 * (n % 4):128 * (n % 4) + 128], P[:, u, n, :], ident[:, :])
                if n % 4 == 3:
                    g.wait(act, M(mm))
                    t = A(act.copy(PT[:, u, n - 3:n + 1, :].rearrange("p a e -> p (a e)"), PS[bank + n // 4][:, :]), f"PT{u}")
            g.ptc = t
            return t

        V(dve.memset(x[:, :, :], 0.0))
        VV(dve.memset(padm[:, :], 0.0))
        pcol, _ = area(0, [128, 1])
        g.wait(dve, G(io(pcol, [[0, 1]], 1)))
        VV(dve.tensor_scalar(padm[:, B - 1:B], pcol, float(N - 128 * (B - 1)), None, ALU.is_ge))
        g.wait(sp, cv.now())
        load(x[:, 0:B - 1, :], None, d["x"][0:128 * (B - 1), :].rearrange("(b p) f -> p b f", p=128))
        load(x[0:N - 128 * (B - 1), B - 1, :], None, d["x"][128 * (B - 1):N, :])
        phase()

        def network0():
            o = 0
            CAT, o = area(o, [128, B, 128])
            X, o = area(o, [128, 2, 8, 64])
            P, o = area(o, [128, 2, 8, 128])
            RI, o = area(o, [128, 2, 8], I32)
            tmp, o = area(o, [128, B, 64])
            st, o = area(o, [128, 4, B])
            rdeg, o = area(o, [128, B])
            CT, o = area(o, [128, 2, 512])
            Wc, o = area(o, [128, 3, 64])
            prm, o = area(o, [128, 5, 64])
            sc, o = area(o, [128, 3, 64])
            bi, o = area(o, [128, 3, 64])
            ta, o = area(o, [128, 2, 4, 64])
            te, o = area(o, [128, 2, 4, 64])
            assert o <= 38400
            table = dram("t0", [NP, 64])
            h = CAT[:, :, 64:128]
            norm(h, x[:, :, :], 64, st, True, sq=tmp)
            g.wait(dve, M(pe.transpose(PS[7][:, 0:B], cnt[:, :], ident[0:B, 0:B])))
            VV(dve.tensor_scalar(rdeg, PS[7][:, 0:B], 1.0, None, ALU.max))
            VV(dve.reciprocal(rdeg, rdeg))
            for l in range(3):
                load(Wc[0:64, l, :], None, d["L0_gnn_W_l"][l])
                load(Wc[64:128, l, :], None, d["L0_gnn_W_r"][l])
                for j, n in enumerate(["b", "gamma", "beta", "run_mean", "run_var"]):
                    t = loadb(prm[:, j, :], d["L0_gnn_" + n][l])
                g.wait(dve, t, cl.now())
                g.wait(act, VV(dve.tensor_scalar(prm[:, 4, :], prm[:, 4, :], 1e-5, None, ALU.add)))
                g.wait(dve, A(act.sqrt(sc[:, l, :], prm[:, 4, :])))
                VV(dve.reciprocal(sc[:, l, :], sc[:, l, :]))
                VV(dve.tensor_tensor(sc[:, l, :], sc[:, l, :], prm[:, 1, :], ALU.mult))
                VV(dve.tensor_tensor(bi[:, l, :], prm[:, 0, :], prm[:, 3, :], ALU.subtract))
                VV(dve.tensor_tensor(bi[:, l, :], bi[:, l, :], sc[:, l, :], ALU.mult))
                VV(dve.tensor_tensor(bi[:, l, :], bi[:, l, :], prm[:, 2, :], ALU.add))
                g.wait(sp, VV(dve.tensor_tensor(Wc[:, l, :], Wc[:, l, :], sc[:, l, :], ALU.mult)))
            for l in range(3):
                g.wait(sp, cv.now())
                cl.inc(sp.dma_start(table.rearrange("(b p) f -> p b f", p=128), h))
                V(dve.memset(CAT[:, :, 0:64], 0.0))
                phase()
                with g.loop(NG) as i:
                    for u in range(2):
                        gt = gathers(table, X, RI, 0, i, u, [(cp, f"mm{u}")])
                        g.before(dve, cp, f"mm{u}")
                        g.wait(pe, onehot_nodes(P, 0, i, u))
                        bs = blocks(dve, R_dve, 0, i, u)
                        for n in range(8):
                            if n % 4 == 0:
                                g.wait(pe, gt[n // 4])
                            mm = pe.matmul(PS[u][:, 64 * n:64 * n + 64], P[:, u, n, :], X[:, u, n, :], start=True, stop=True)
                        g.wait(dve, M(mm, f"mm{u}"))
                        add_blocks(CAT[:, :, 0:64], bs, lambda n: PS[u][:, 64 * n:64 * n + 64], 64, u, i)
                phase()
                VV(dve.tensor_tensor(CAT[:, :, 0:64], CAT[:, :, 0:64], bc(rdeg[:, :, None], [128, B, 64]), ALU.mult))
                g.wait(pe, cv.now())

                def evac(c, b0, nb, ps, t):
                    a, e = ta[:, c % 2, 0:nb, :], te[:, c % 2, 0:nb, :]
                    g.wait(dve, t)
                    r = VV(dve.tensor_tensor(a, ps, bc(bi[:, l, :][:, None, :], [128, nb, 64]), ALU.add))
                    VV(dve.tensor_scalar(e, a, 0.0, None, ALU.min))
                    g.wait(act, cv.now())
                    g.wait(dve, A(act.activation(e, e, ACT.Exp)))
                    VV(dve.tensor_scalar(a, a, 0.0, -1.0, ALU.max, ALU.add))
                    VV(dve.tensor_tensor(h[:, b0:b0 + nb, :], a, e, ALU.add))
                    return [r]

                dense(lambda b: CAT[:, b, :], 128, Wc[:, l, :], 64, None, CT, evac)
            VV(dve.tensor_tensor(x[:, :, :], x[:, :, :], h, ALU.add))
            phase()

        network0()

        def network1():
            o = 0
            TB, o = area(o, [128, B, 66])
            X, o = area(o, [128, 2, 8, 66])
            P, o = area(o, [128, 2, 8, 128])
            PT, o = area(o, [128, 2, 8, 128])
            RI, o = area(o, [128, 2, 8], I32)
            tmp, o = area(o, [128, B, 64])
            st, o = area(o, [128, 4, B])
            S1, o = area(o, [128, B, 2])
            acc, o = area(o, [128, B, 130])
            wa, o = area(o, [128, 2, 2, 64])
            wv, o = area(o, [128, 2, 64])
            eg, o = area(o, [128, 2, 8, 2])
            el, o = area(o, [128, 2, 8, 2])
            ms, o = area(o, [128, 2, 8, 130])
            assert o <= 38400, o
            table = dram("t1", [NP, 66])
            h = TB[:, :, 0:64]
            norm(h, x[:, :, :], 64, st, True, sq=tmp)
            for q in range(2):
                loadb(wv[:, q, :], d["L1_gnn_W"][q])
                loadb(wa[:, q, :, :].rearrange("p a f -> p (a f)"), d["L1_gnn_a"][q])
            g.wait(dve, cl.now())
            for q in range(2):
                for s_ in range(2):
                    VV(dve.tensor_tensor(wa[:, q, s_, :], wa[:, q, s_, :], wv[:, q, :], ALU.mult))
                    VV(dve.tensor_tensor(tmp, h, bc(wa[:, q, s_, :][:, None, :], [128, B, 64]), ALU.mult))
                    VV(dve.tensor_reduce(S1[:, :, q] if s_ == 0 else TB[:, :, 64 + q], tmp, AX.X, ALU.add))
            g.wait(sp, cv.now())
            cl.inc(sp.dma_start(table.rearrange("(b p) f -> p b f", p=128), TB))
            V(dve.memset(acc, 0.0))
            phase()
            with g.loop(NG) as i:
                for u in range(2):
                    gt = gathers(table, X, RI, 1, i, u, [(cv, f"msg{u}")])
                    g.before(dve, cp, f"mm{u}")
                    g.wait(pe, onehot_nodes(P, 1, i, u))
                    bp = blocks(pe, R_pe, 1, i, u)
                    bs = blocks(dve, R_dve, 1, i, u)
                    pt = transposed(P, PT, u, 0)
                    g.wait(pe, pt)
                    for n in range(8):
                        mm = pe.matmul(PS[2 + u][:, 2 * n:2 * n + 2], PT[:, u, n, :],
                                       S1[:, bass.ds(bp[n], 1), :].rearrange("p a f -> p (a f)"), start=True, stop=True)
                    g.wait(dve, M(mm, f"s{u}"), *gt)
                    V(dve.tensor_tensor(eg[:, u], PS[2 + u][:, 0:16].rearrange("p (n f) -> p n f", f=2),
                                        X[:, u, :, 64:66], ALU.add), f"sc{u}")
                    g.wait(dve, cv.now())
                    t = V(dve.scalar_tensor_tensor(eg[:, u], eg[:, u], 0.2, eg[:, u], ALU.mult, ALU.max))
                    g.wait(act, t)
                    t = A(act.activation(el[:, u], eg[:, u], ACT.Exp))
                    g.wait(dve, t)
                    for q in range(2):
                        V(dve.tensor_tensor(ms[:, u, :, 64 * q:64 * q + 64], X[:, u, :, 0:64],
                                            bc(el[:, u, :, q:q + 1], [128, 8, 64]), ALU.mult))
                    t = V(dve.tensor_copy(ms[:, u, :, 128:130], el[:, u]), f"msg{u}")
                    g.wait(pe, t)
                    view = lambda n: PS[4 + n // 3][:, 130 * (n % 3):130 * (n % 3) + 130]
                    for n in range(8):
                        mm = pe.matmul(view(n), P[:, u, n, :], ms[:, u, n, :], start=True, stop=True)
                    g.wait(dve, M(mm, f"mm{u}"))
                    add_blocks(acc, bs, view, 130, u, i)
            phase()
            r = st
            for q in range(2):
                VV(dve.tensor_tensor(r[:, q, :], acc[:, :, 128 + q], padm[:, :], ALU.add))
                VV(dve.reciprocal(r[:, q, :], r[:, q, :]))
                VV(dve.scalar_tensor_tensor(tmp, acc[:, :, 64 * q:64 * q + 64], 0.5,
                                            bc(r[:, q, :][:, :, None], [128, B, 64]), ALU.mult, ALU.mult))
                VV(dve.tensor_tensor(x[:, :, :], x[:, :, :], tmp, ALU.add))
            phase()

        group_edges(1)
        network1()

        def id_flags(k, H, FL, IDT, stage, SF, CC, row):
            P_ = 16 * H
            nv = node[k][:, :].rearrange("p (c j) -> p c j", c=16)
            cop = {}
            sv = stage[:, 0:52 * P_].rearrange("p (j c h) -> p j c h", j=52, c=16)
            for j in range(52):
                V(dve.tensor_copy(sv[:, j], bc(nv[:, :, j:j + 1], [128, 16, H])))
            g.wait(pe, cv.now())
            for q in range(13):
                g.wait(pe, cop.get(q - 2))
                for j in range(4):
                    mm = pe.transpose(PS[q % 2][0:P_, 128 * j:128 * j + 128],
                                      stage[:, P_ * (4 * q + j):P_ * (4 * q + j) + P_], ident[:, :])
                g.wait(act, M(mm))
                cop[q] = A(act.copy(IDT[0:P_, 512 * q:512 * q + 512], PS[q % 2][0:P_, :]))
            g.wait(dve, cs.now())
            V(dve.memset(FL[:, :], 0.0))
            g.wait(dve, cv.now())
            VV(dve.tensor_tensor(FL[0:P_, 1:6656], IDT[0:P_, 1:6656], IDT[0:P_, 0:6655], ALU.is_equal))
            VV(dve.tensor_scalar(FL[0:P_, 1:6656], FL[0:P_, 1:6656], -1.0, BIG, ALU.add, ALU.mult))
            V(dve.tensor_copy(CC[0:P_, 0:1], IDT[0:P_, 0:1]))
            VV(dve.tensor_copy(CC[0:P_, 1:2], IDT[0:P_, 6655:6656]))
            to_row(CC, H, row)
            VV(dve.memset(SF[0:1, :], 0.0))
            n = H * 32
            VV(dve.tensor_tensor(SF[0:1, 1:n], row[0:1, 2:n + 1], row[0:1, 1:n], ALU.is_equal))
            for h_ in range(H):
                VV(dve.memset(SF[0:1, 32 * h_:32 * h_ + 1], 0.0))
            VV(dve.tensor_scalar(SF[0:1, 0:n + 1], SF[0:1, 0:n + 1], -1.0, BIG, ALU.add, ALU.mult))

        def to_row(CC, H, row):
            P_ = 16 * H
            g.wait(pe, cv.now(), cs.now())
            for w in range(2):
                mm = pe.transpose(PS[7][0:1, 128 * w:128 * w + P_], CC[0:P_, w:w + 1], ident[0:P_, 0:P_])
            g.wait(dve, M(mm))
            rv = row[0:1, 1:1 + 32 * H].rearrange("p (h c w) -> p h c w", h=H, c=16)
            for w in range(2):
                VV(dve.tensor_copy(rv[:, :, :, w], PS[7][0:1, 128 * w:128 * w + P_].rearrange("p (c h) -> p h c", h=H)))

        def softmax_weights(H, Ev, AT, Fm, FL, SF, CC, row, rowf, rowb, cr):
            P_, n = 16 * H, 32 * H
            ev = Ev.rearrange("p (c j) h -> p c j h", c=16)
            cop = {}
            sv = Fm[:, 0:52 * P_].rearrange("p (j c h) -> p j c h", j=52, c=16)
            for q in range(13):
                t = V(dve.tensor_copy(sv[:, 4 * q:4 * q + 4], ev[:, :, 4 * q:4 * q + 4, :].rearrange("p c j h -> p j c h")))
                g.wait(pe, t, cop.get(q - 2))
                for j in range(4):
                    mm = pe.transpose(PS[q % 2][0:P_, 128 * j:128 * j + 128],
                                      Fm[:, P_ * (4 * q + j):P_ * (4 * q + j) + P_], ident[:, :])
                g.wait(act, M(mm))
                cop[q] = A(act.copy(AT[0:P_, 512 * q:512 * q + 512], PS[q % 2][0:P_, :]))
            g.wait(dve, cs.now())
            fwd = lambda ini: VV(dve.tensor_tensor_scan(Fm[0:P_, 0:6656], FL[0:P_, 0:6656], AT[0:P_, 0:6656], ini, ALU.add, ALU.max))
            back = lambda ini: VV(dve.tensor_tensor_scan(Fm[0:P_, 6655::-1] if False else Fm[0:P_, 0:6656][:, ::-1],
                                                         FL[0:P_, 1:6657][:, ::-1],
                                                         Fm[0:P_, 0:6656][:, ::-1], ini, ALU.add, ALU.max))
            fwd(-BIG)
            VV(dve.tensor_copy(CC[0:P_, 1:2], Fm[0:P_, 6655:6656]))
            back(-BIG)
            VV(dve.tensor_copy(CC[0:P_, 0:1], Fm[0:P_, 0:1]))
            for r in (row, rowf, rowb):
                VV(dve.memset(r[0:1, :], -BIG))
            to_row(CC, H, row)
            VV(dve.tensor_tensor_scan(rowf[0:1, 1:n + 1], SF[0:1, 0:n], row[0:1, 1:n + 1], -BIG, ALU.add, ALU.max))
            VV(dve.tensor_tensor_scan(rowb[0:1, 1:n + 1][:, ::-1], SF[0:1, 1:n + 1][:, ::-1],
                                      row[0:1, 1:n + 1][:, ::-1], -BIG, ALU.add, ALU.max))
            sf0 = SF[0:1, 0:n].rearrange("p (h c w) -> p h c w", h=H, c=16)[:, :, :, 0]
            sf2 = SF[0:1, 1:n + 1].rearrange("p (h c w) -> p h c w", h=H, c=16)[:, :, :, 1]
            lf = rowf[0:1, 0:n].rearrange("p (h c w) -> p h c w", h=H, c=16)[:, :, :, 0]
            rb = rowb[0:1, 2:n + 2].rearrange("p (h c w) -> p h c w", h=H, c=16)[:, :, :, 1]
            cv_ = lambda w: cr[0:1, w, 0:P_].rearrange("p (c h) -> p h c", h=H)
            VV(dve.tensor_tensor(cv_(0), lf, sf0, ALU.add))
            g.wait(pe, VV(dve.tensor_tensor(cv_(1), rb, sf2, ALU.add)))
            for w in range(2):
                mm = pe.matmul(PS[7][0:P_, 256 + w:257 + w], cr[0:1, w, 0:P_], ones[0:1, 0:1], start=True, stop=True)
            g.wait(dve, M(mm))
            VV(dve.tensor_copy(CC[0:P_, 0:2], PS[7][0:P_, 256:258]))
            fwd(CC[0:P_, 0:1])
            back(CC[0:P_, 1:2])
            for q in range(13):
                s = slice(512 * q, 512 * q + 512)
                g.wait(act, V(dve.tensor_tensor(AT[0:P_, s], AT[0:P_, s], Fm[0:P_, s], ALU.subtract)))
                g.wait(pe, A(act.activation(AT[0:P_, s], AT[0:P_, s], ACT.Exp)), cop.get(("b", q - 2)))
                w = 4 * P_
                for j in range(4):
                    mm = pe.transpose(PS[2 + q % 2][:, P_ * j:P_ * j + P_], AT[0:P_, 512 * q + 128 * j:512 * q + 128 * j + 128],
                                      ident[0:P_, 0:P_])
                g.wait(act, M(mm))
                for j in range(4):
                    cop["b", q] = A(act.copy(ev[:, :, 4 * q + j, :], PS[2 + q % 2][:, P_ * j:P_ * j + P_].rearrange("p (c h) -> p c h", h=H)))
            phase()

        def weigh(k, H, Ev, vsp, acc, Vr, P, ms):
            F = 16 * H
            W = F + H
            per = 512 // W
            VV(dve.memset(acc, 0.0))
            phase()
            with g.loop(NG) as i:
                for u in range(2):
                    g.before(sp, cv, f"msg{u}")
                    ld = ca[u].inc(sp.dma_start(Vr[:, u], vsp[:, bass.ds(i * 2 + u, 1), :]))
                    g.before(dve, cp, f"mm{u}")
                    onehot_nodes(P, k, i, u)
                    bs = blocks(dve, R_dve, k, i, u)
                    a = i * 16 + 8 * u
                    ex = Ev[:, bass.ds(a, 8), :]
                    g.wait(dve, ld)
                    V(dve.tensor_tensor(ms[:, u, :, 0:F].rearrange("p n (h e) -> p n h e", h=H) if False else
                                        ms[:, u, :, 0:F].rearrange("p n (h e) -> p n h e", h=H),
                                        Vr[:, u].rearrange("p (n h e) -> p n h e", n=8, h=H),
                                        bc(ex[:, :, :, None], [128, 8, H, 16]), ALU.mult))
                    t = V(dve.tensor_copy(ms[:, u, :, F:W], ex), f"msg{u}")
                    g.wait(pe, t)
                    view = lambda n: PS[4 * u + n // per][:, W * (n % per):W * (n % per) + W]
                    for n in range(8):
                        mm = pe.matmul(view(n), P[:, u, n, :], ms[:, u, n, :], start=True, stop=True)
                    g.wait(dve, M(mm, f"mm{u}"))
                    add_blocks(acc, bs, view, W, u, i)
            phase()

        def network2():
            h, o = area(0, [128, B, 128])
            Ev, o = area(o, [128, T, 8])
            FL, o = area(o, [128, 6658], BF)
            SM, o = area(o, [128, 2048])
            Wp, o = area(o, [128, 3 * 512])
            vec, o = area(o, [128, 6, 128])
            brow, o = area(o, [1, 512 + 512 + 128])
            SF, o = area(o, [1, 258])
            CC, o = area(o, [128, 2])
            row, o = area(o, [1, 260])
            rowf, o = area(o, [1, 260])
            rowb, o = area(o, [1, 260])
            cr, o = area(o, [1, 2, 128])
            st, o = area(o, [128, 4, B])
            RI, o = area(o, [128, 2, 8], I32)
            U = o
            assert U + 13312 <= 38400, U
            q_, o = area(U, [128, B, 128])
            X, o = area(o, [128, 2, 8, 256])
            P, o = area(o, [128, 2, 8, 128])
            PT = SM.rearrange("p (u n e) -> p u n e", u=2, n=8)
            AT, o = area(U, [128, 6656])
            Fm, o = area(o, [128, 6656])
            acc, o = area(U, [128, B, 136])
            Vr, o = area(o, [128, 2, 1024])
            P2, o = area(o, [128, 2, 8, 128])
            ms, o = area(o, [128, 2, 8, 136])
            assert o <= U + 13312
            xr = Ev.rearrange("p t h -> p (t h)")[:, 0:B * 128].rearrange("p (b f) -> p b f", b=B)
            tmp, _ = area(U + B * 136, [128, B, 128])
            CT, _ = area(U + B * 128, [128, 2, 512])
            KV, _ = area(U + B * 128 + 1024, [128, 2, 4, 256])
            table = dram("t2", [NP, 256])
            vsp = dram("v2", [128, 2 * NG, 1024])
            Wq = Wp[:, 0:512]
            W1 = Wp[:, 512:1024]
            W2 = Wp[:, 1024:1536].rearrange("p (a f) -> p a f", a=4)

            x0 = tmp[:, :, 0:64]
            norm(x0, x[:, :, :], 64, st, True, sq=tmp[:, :, 64:128])
            load(Wp[0:64, 0:128], "WiT")
            t = load(brow[:, 0:128], None, d["L2_gnn_bi"][None, :])
            g.wait(pe, cv.now(), t, cl.now())
            CT0 = SM[:, 0:1024].rearrange("p (a f) -> p a f", a=2)

            def ev0(c, b0, nb, ps, t):
                g.wait(act, t)
                return [A(act.activation(h[:, b0:b0 + nb, :], ps, ACT.Gelu))]

            dense(lambda b: x0[:, b, :], 64, Wp[0:64, 0:128], 128, brow[:, 0:128], CT0, ev0)
            phase()
            id_flags(0, 8, FL, AT, Fm, SF, CC, row)
            phase()
            for l in range(4):
                load(Wp, None, d["W2all"][l])
                load(brow, None, d["b2all"][l][None, :])
                for j, n in enumerate(["ln_g", "ln_b", "b2"]):
                    loadb(vec[:, j, :], d["L2_gnn_" + n][l])
                t = cl.inc(sp.dma_start(vec[:, 3:6, :].rearrange("p a f -> p (a f)"),
                                        d["L2_gnn_Wbeta"][l].to_broadcast([128, 384])))
                phase()
                prev = {}

                def ev1(c, b0, nb, ps, t):
                    g.wait(act, t, prev.get(c - 2))
                    for j in range(nb):
                        A(act.activation(q_[:, b0 + j, :], ps[j][:, 0:128], ACT.Copy, scale=0.25))
                        a_ = A(act.copy(KV[:, c % 2, j, :], ps[j][:, 128:384]))
                    g.wait(sp, a_)
                    prev[c] = cb[c % 2].inc(sp.dma_start(
                        table[128 * b0:128 * (b0 + nb), :].rearrange("(b p) f -> p b f", p=128), KV[:, c % 2, 0:nb, :]))
                    return [a_]

                dense(lambda b: h[:, b, :], 128, Wq[:, 0:384], 384, brow[:, 0:384], CT, ev1)
                phase()
                with g.loop(NG) as i:
                    for u in range(2):
                        gt = gathers(table, X, RI, 0, i, u, [(cv, f"prod{u}"), (cb[u], f"sp{u}")])
                        g.before(dve, cp, f"tr{u}")
                        g.wait(pe, onehot_nodes(P, 0, i, u))
                        bp = blocks(pe, R_pe, 0, i, u)
                        pt = transposed(P, PT, u, 0)
                        M_ = M(pe.nop(), f"tr{u}") if False else None
                        g.wait(pe, pt)
                        for n in range(8):
                            mm = pe.matmul(PS[2 + 2 * u + n // 4][:, 128 * (n % 4):128 * (n % 4) + 128], PT[:, u, n, :],
                                           q_[:, bass.ds(bp[n], 1), :].rearrange("p a f -> p (a f)"), start=True, stop=True)
                        g.wait(dve, M(mm, f"tr{u}"), *gt)
                        g.wait(sp, *gt)
                        if True:
                            hold(sp)
                        cb[u].inc(sp.dma_start(vsp[:, bass.ds(i * 2 + u, 1), :].rearrange("p a (n f) -> p (a n) f", n=8),
                                               X[:, u, :, 128:256]), f"sp{u}")
                        for z in range(2):
                            kx = X[:, u, 4 * z:4 * z + 4, 0:128]
                            VV(dve.tensor_tensor(kx, kx, PS[2 + 2 * u + z][:, :].rearrange("p (n f) -> p n f", n=4), ALU.mult))
                            t = V(dve.tensor_reduce(Ev[:, bass.ds(i * 16 + 8 * u + 4 * z, 4), :],
                                                    kx.rearrange("p n (h e) -> p n h e", h=8), AX.X, ALU.add), f"prod{u}")
                phase()
                softmax_weights(8, Ev, AT, Fm, FL, SF, CC, row, rowf, rowb, cr)
                weigh(0, 8, Ev, vsp, acc, Vr, P2, ms)

                rd = SM[:, 0:B * 8].rearrange("p (b h) -> p b h", b=B)
                VV(dve.tensor_scalar(rd, acc[:, :, 128:136], 1e-16, None, ALU.add))
                VV(dve.reciprocal(rd, rd))
                out = acc[:, :, 0:128]
                for h_ in range(8):
                    oh = acc[:, :, 16 * h_:16 * h_ + 16]
                    V(dve.tensor_tensor(oh, oh, bc(rd[:, :, h_:h_ + 1], [128, B, 16]), ALU.mult))
                g.wait(dve, cv.now())
                g.wait(pe, cv.now())

                def ev2(c, b0, nb, ps, t):
                    g.wait(act, t)
                    return [A(act.copy(xr[:, b0:b0 + nb, :], ps))]

                CT2 = SM[:, 512:1536].rearrange("p (a f) -> p a f", a=2)
                dense(lambda b: h[:, b, :], 128, Wq[:, 384:512], 128, brow[:, 384:512], CT2, ev2)
                g.wait(dve, cs.now())
                VV(dve.tensor_tensor(vec[:, 3, :], vec[:, 3, :], vec[:, 5, :], ALU.add))
                VV(dve.tensor_tensor(vec[:, 4, :], vec[:, 4, :], vec[:, 5, :], ALU.subtract))
                S = [128, B, 128]
                z0, z1 = st[:, 0, :], st[:, 1, :]
                VV(dve.tensor_tensor(tmp, out, bc(vec[:, 3, :][:, None, :], S), ALU.mult))
                VV(dve.tensor_reduce(z0, tmp, AX.X, ALU.add))
                VV(dve.tensor_tensor(tmp, xr, bc(vec[:, 4, :][:, None, :], S), ALU.mult))
                VV(dve.tensor_reduce(z1, tmp, AX.X, ALU.add))
                g.wait(act, VV(dve.tensor_tensor(z0, z0, z1, ALU.add)))
                g.wait(dve, A(act.activation(z0, z0, ACT.Exp, scale=-1.0)))
                VV(dve.tensor_scalar(z0, z0, 1.0, None, ALU.add))
                VV(dve.reciprocal(z0, z0))
                VV(dve.tensor_tensor(xr, xr, out, ALU.subtract))
                VV(dve.tensor_tensor(xr, xr, bc(z0[:, :, None], S), ALU.mult))
                VV(dve.tensor_tensor(xr, xr, out, ALU.add))
                VV(dve.tensor_tensor(xr, xr, h, ALU.add))
                norm(h, xr, 128, st, False, vec[:, 0, :], vec[:, 1, :], sq=tmp)
                hT = SM[:, 0:256].rearrange("p (a f) -> p a f", a=2)
                ge = SM[:, 512:1536].rearrange("p (a q f) -> p a q f", a=2, q=4)
                V(dve.tensor_tensor(xr, h, bc(vec[:, 2, :][:, None, :], S), ALU.add))
                g.wait(pe, cv.now())
                tA, tB, tC, tD = {}, {}, {}, {}

                def first_half(b):
                    g.wait(pe, tA.get(b - 2))
                    t = M(pe.transpose(PS[b % 2][:, 0:128], h[:, b, :], ident[:, :]))
                    g.wait(act, t)
                    tA[b] = A(act.copy(hT[:, b % 2, :], PS[b % 2][:, 0:128]))
                    g.wait(pe, tA[b], tB.get(b - 2))
                    for q in range(4):
                        v = PS[2 + b % 2][:, 128 * q:128 * q + 128]
                        pe.matmul(v, W1[:, 128 * q:128 * q + 128], hT[:, b % 2, :], start=True, stop=False)
                        mm = pe.matmul(v, brow[:, 512 + 128 * q:640 + 128 * q], ones[0:1, :], start=False, stop=True)
                    g.wait(act, M(mm), tC.get(b - 2))
                    tB[b] = A(act.activation(ge[:, b % 2].rearrange("p q f -> p (q f)"), PS[2 + b % 2][:, :], ACT.Gelu))

                def second_half(b):
                    g.wait(pe, tB[b], tD.get(b - 2))
                    for q in range(4):
                        mm = pe.matmul(PS[4 + b % 2][:, 0:128], ge[:, b % 2, q, :], W2[:, q, :], start=q == 0, stop=q == 3)
                    tC[b] = M(mm)
                    g.wait(dve, tC[b])
                    tD[b] = V(dve.tensor_tensor(h[:, b, :], xr[:, b, :], PS[4 + b % 2][:, 0:128], ALU.add))

                for b in range(B + 1):
                    if b < B:
                        first_half(b)
                    if b:
                        second_half(b - 1)
                phase()
            load(Wp[:, 0:64], "WoT")
            t = load(brow[:, 0:64], None, d["L2_gnn_bo"][None, :])
            g.wait(pe, t, cl.now())

            def ev3(c, b0, nb, ps, t):
                g.wait(dve, t)
                return [V(dve.tensor_tensor(x[:, b0:b0 + nb, :], x[:, b0:b0 + nb, :], ps, ALU.add))]

            dense(lambda b: h[:, b, :], 128, Wp[:, 0:64], 64, brow[:, 0:64], CT0, ev3)
            phase()

        network2()

        def network3():
            Ev, o = area(0, [128, T, 4])
            FL, o = area(o, [128, 6658], BF)
            PT, o = area(o, [128, 2, 8, 128])
            Wk, o = area(o, [64, 128])
            Wr, o = area(o, [18, 128])
            bq, o = area(o, [1, 128])
            br, o = area(o, [1, 128])
            SF, o = area(o, [1, 258])
            CC, o = area(o, [128, 2])
            row, o = area(o, [1, 260])
            rowf, o = area(o, [1, 260])
            rowb, o = area(o, [1, 260])
            cr, o = area(o, [1, 2, 128])
            st, o = area(o, [128, 4, B])
            RI, o = area(o, [128, 2, 8], I32)
            U = o
            q_, o = area(U, [128, B, 32])
            X, o = area(o, [128, 2, 8, 96])
            P, o = area(o, [128, 2, 8, 128])
            AB, o = area(o, [128, 2, 8, 20], I32)
            AtT, o = area(o, [18, 2, 8, 128])
            ve, o = area(o, [128, 2, 8, 64])
            kx, o = area(o, [128, 2, 8, 32])
            CT, o = area(o, [128, 2, 512])
            KV, o = area(o, [128, 2, 4, 96])
            h, o = area(o, [128, B, 64])
            tmp, o = area(o, [128, B, 64])
            assert o <= 38400
            AT, o = area(U, [128, 6656])
            Fm, o = area(o, [128, 6656])
            assert o <= 38400
            acc, o = area(U, [128, B, 68])
            Vr, o = area(o, [128, 2, 512])
            P2, o = area(o, [128, 2, 8, 128])
            ms, o = area(o, [128, 2, 8, 68])
            assert o <= 38400
            table = dram("t3", [NP, 96])
            vsp = dram("v3", [128, 2 * NG, 512])
            norm(h, x[:, :, :], 64, st, True, sq=tmp)
            load(Wk, "L3_gnn_qkv_w")
            load(bq, None, d["L3_gnn_qkv_b"][None, :])
            load(Wr, "rpe_w")
            load(br, None, d["rpe_b"][None, :])
            phase()
            prev = {}

            def ev1(c, b0, nb, ps, t):
                g.wait(act, t, prev.get(c - 2))
                A(act.activation(q_[:, b0:b0 + nb, :], ps[:, :, 0:32], ACT.Copy, scale=float(np.float32(8.0) ** np.float32(-0.5))))
                a_ = A(act.copy(KV[:, c % 2, 0:nb, :], ps[:, :, 32:128]))
                g.wait(sp, a_)
                prev[c] = cb[c % 2].inc(sp.dma_start(
                    table[128 * b0:128 * (b0 + nb), :].rearrange("(b p) f -> p b f", p=128), KV[:, c % 2, 0:nb, :]))
                return [a_]

            dense(lambda b: h[:, b, :], 64, Wk, 128, bq, CT, ev1)
            phase()
            tb = tab[1].rearrange("(p t) w -> p t w", p=128)
            with g.loop(NG) as i:
                for u in range(2):
                    a = i * 16 + 8 * u
                    gt = gathers(table, X, RI, 1, i, u, [(cv, f"ve{u}")])
                    g.before(sp, cp, f"at{u}")
                    ld = ca[u].inc(sp.dma_start(AB[:, u], tb[:, bass.ds(a, 8), :]))
                    g.before(dve, cp, f"tr{u}")
                    g.wait(pe, onehot_nodes(P, 1, i, u))
                    bp = blocks(pe, R_pe, 1, i, u)
                    pt = transposed(P, PT, u, 0)
                    g.wait(pe, ld)
                    if u:
                        g.wait(pe, att)
                    else:
                        g.before(pe, cs, "at1")
                    hold(pe)
                    for n in range(8):
                        mm = pe.transpose(PS[2 + n // 4][0:18, 128 * (n % 4):128 * (n % 4) + 128],
                                          AB[:, u, n, 2:20].bitcast(F32), ident[:, :])
                    g.wait(act, M(mm, f"at{u}"))
                    g.before(act, cp, f"tr{u}")
                    for z in range(2):
                        att = A(act.copy(AtT[:, u, 4 * z:4 * z + 4, :].rearrange("p a e -> p (a e)"), PS[2 + z][0:18, :]), f"at{u}")
                    g.wait(pe, att)
                    for n in range(8):
                        v = PS[4 + 2 * u + n // 4][:, 128 * (n % 4):128 * (n % 4) + 128]
                        pe.matmul(v, AtT[:, u, n, :], Wr, start=True, stop=False)
                        pe.matmul(v, ones[0:1, :], br, start=False, stop=False)
                        mm = pe.matmul(v[:, 0:32], PT[:, u, n, :],
                                       q_[:, bass.ds(bp[n], 1), :].rearrange("p a f -> p (a f)"), start=False, stop=True)
                    g.wait(dve, M(mm, f"tr{u}"), *gt)
                    for z in range(2):
                        ps = PS[4 + 2 * u + z][:, :].rearrange("p (n f) -> p n f", n=4)
                        r = slice(4 * z, 4 * z + 4)
                        V(dve.tensor_tensor(kx[:, u, r, :], X[:, u, r, 0:32], ps[:, :, 32:64], ALU.add))
                        if z == 0:
                            g.before(dve, cb[u], f"sp{u}")
                        V(dve.tensor_tensor(ve[:, u, r, :], X[:, u, r, 32:96], ps[:, :, 64:128], ALU.add), f"ve{u}")
                        g.wait(dve, cv.now())
                        VV(dve.tensor_tensor(kx[:, u, r, :], kx[:, u, r, :], ps[:, :, 0:32], ALU.mult))
                        t = VV(dve.tensor_reduce(Ev[:, bass.ds(a + 4 * z, 4), :],
                                                 kx[:, u, r, :].rearrange("p n (h e) -> p n h e", h=4), AX.X, ALU.add))
                    g.wait(sp, t)
                    cb[u].inc(sp.dma_start(vsp[:, bass.ds(i * 2 + u, 1), :],
                                           ve[:, u].rearrange("p n f -> p (n f)")), f"sp{u}")
            phase()
            id_flags(1, 4, FL, AT, Fm, SF, CC, row)
            phase()
            softmax_weights(4, Ev, AT, Fm, FL, SF, CC, row, rowf, rowb, cr)
            weigh(1, 4, Ev, vsp, acc, Vr, P2, ms)
            rd = PT[:, 0, 0:2, :].rearrange("p a b -> p (a b)")[:, 0:B * 4].rearrange("p (b h) -> p b h", b=B)
            VV(dve.tensor_scalar(rd, acc[:, :, 64:68], 1e-16, None, ALU.add))
            VV(dve.reciprocal(rd, rd))
            for h_ in range(4):
                s = slice(16 * h_, 16 * h_ + 16)
                VV(dve.tensor_tensor(acc[:, :, s], acc[:, :, s], bc(rd[:, :, h_:h_ + 1], [128, B, 16]), ALU.mult))
                VV(dve.tensor_tensor(x[:, :, s], x[:, :, s], acc[:, :, s], ALU.add))

        network3()
        g.wait(sp, cv.now())
        cl.inc(sp.dma_start(d["out"][0:128 * (B - 1), :].rearrange("(b p) f -> p b f", p=128), x[:, 0:B - 1, :]))
        cl.inc(sp.dma_start(d["out"][128 * (B - 1):N, :], x[0:N - 128 * (B - 1), B - 1, :]))
        phase()



def prepare(inputs):
    f = lambda name: np.ascontiguousarray(inputs[name])
    a = {}
    src, dst = f("src"), f("dst")
    a["src"], a["dst"] = src.reshape(EP, ET), dst.reshape(EP, ET)
    a["srcT"] = np.ascontiguousarray(a["src"].T)
    a["dstT"] = np.ascontiguousarray(a["dst"].T)
    a["pair"] = np.stack([a["src"], a["dst"]], axis=-1)
    a["attr"] = f("edge_attr_18").reshape(EP, ET, 18)
    a["x"] = f("x")
    for n_ in ("W_l", "W_r", "b", "gamma", "beta", "run_mean", "run_var"):
        a["L0_gnn_" + n_] = f("L0_gnn_" + n_)
    a["L1_gnn_W"], a["L1_gnn_a"] = f("L1_gnn_W"), f("L1_gnn_a")
    T_ = lambda n_: f("L2_gnn_" + n_).transpose(0, 2, 1)
    W2T = T_("W2").reshape(4, 4, 128, 128).transpose(0, 2, 1, 3).reshape(4, 128, 512)
    a["W2all"] = np.concatenate([T_("Wq"), T_("Wk"), T_("Wv"), T_("Ws"), T_("W1"), W2T], axis=2)
    a["b2all"] = np.concatenate([f("L2_gnn_" + n_) for n_ in ("bq", "bk", "bv", "bs", "b1", "b2")], axis=1)[:, 0:1152]
    a["WiT"], a["WoT"] = f("L2_gnn_Wi").T, f("L2_gnn_Wo").T
    for n_ in ("bi", "ln_g", "ln_b", "b2", "Wbeta", "bo"):
        a["L2_gnn_" + n_] = f("L2_gnn_" + n_)
    a["L3_gnn_qkv_w"], a["L3_gnn_qkv_b"] = f("L3_gnn_qkv_w"), f("L3_gnn_qkv_b")
    a["rpe_w"] = np.concatenate([f("L3_gnn_" + n_) for n_ in ("q_rpe_w", "k_rpe_w", "v_rpe_w")], axis=1)
    a["rpe_b"] = np.concatenate([f("L3_gnn_" + n_) for n_ in ("q_rpe_b", "k_rpe_b", "v_rpe_b")], axis=0)
    return {k: np.ascontiguousarray(v) for k, v in a.items()}


def program(new, arrays, outputs, stop=None):
    plan = {}
    for dry in (True, False):
        nc = new()
        d = {k: nc.dram_tensor(f"in_{k}", list(v.shape), mybir.dt.from_np(v.dtype), kind="ExternalInput").ap()
             for k, v in arrays.items()}
        for k, shape in outputs.items():
            d[k] = nc.dram_tensor(k, shape, F32, kind="ExternalOutput").ap()
        build(nc, d, plan, dry, stop)
    return nc


def kernel(**inputs):
    import concourse.bacc as bacc
    from concourse.bass_utils import run_bass_kernel_spmd

    arrays = prepare(inputs)
    nc = program(lambda: bacc.Bacc("TRN2", target_bir_lowering=False, num_devices=1), arrays, {"out": [N, 64]})
    r = run_bass_kernel_spmd(nc, [{f"in_{k}": v for k, v in arrays.items()}], core_ids=[0])
    return r.results[0]["out"]
```

```python
from contextlib import ExitStack

import numpy as np
import concourse.bass as bass
from concourse import mybir

F32 = mybir.dt.float32
I32 = mybir.dt.int32
BF = mybir.dt.bfloat16
ALU = mybir.AluOpType
ACT = mybir.ActivationFunctionType
AX = mybir.AxisListType

N, E, B = 6250, 100000, 49
NP = B * 128
EP, ET = 125, 800
T = 832
NG = T // 16
TR = T + 8
BIG = 1.0e30
LEAD = 512


class Count:

    def __init__(self, g, sem, step=1, eng=None):
        self.g, self.sem, self.step, self.at = g, sem, step, 0
        self.enter, self.eng = 0, eng
        g.counts.append(self)

    def inc(self, ins, label=None):
        ins.then_inc(self.sem, self.step)
        if self.eng is not None:
            self.g.waited = {w for w in self.g.waited if w[0] != self.eng.engine}
        self.at += self.step
        return self.now(label)

    def now(self, label=None):
        t = (self, self.at)
        if label is not None:
            self.g.plan[(self.g.loop_no, label)] = self.at - self.enter
        return t


class Gen:

    def __init__(self, nc, plan, dry):
        self.nc, self.plan, self.dry = nc, plan, dry
        self.counts, self.i, self.loop_no, self.n_loops = [], None, None, 0
        self.waited = set()

    def loop(self, n):
        return Loop(self, n)

    def wait(self, eng, *toks):
        for tok in toks:
            if tok is None:
                continue
            c, v = tok
            if self.i is not None and v > c.enter:
                per = self.plan.get((self.loop_no, id_of(self, c)), 1)
                self.wait_reg(eng, c, self.i * per + v)
            elif v > 0:
                eng.wait_ge(c.sem, v)

    def wait_reg(self, eng, c, v):
        if (eng.engine, c.sem) in self.waited:
            eng.sem_inc(self.misc, 1)
            self.waited = {w for w in self.waited if w[0] != eng.engine}
        eng.wait_ge(c.sem, v)
        if eng is self.nc.sync:
            eng.sem_inc(self.misc, 1)
        else:
            self.waited.add((eng.engine, c.sem))

    def before(self, eng, c, label):
        per = self.plan.get((self.loop_no, id_of(self, c)), 1)
        at = self.plan.get((self.loop_no, label), 1)
        v = c.enter + at - per
        assert self.dry or v > 0
        self.wait_reg(eng, c, self.i * per + max(v, 1))


def last_use(g, eng, c, label, seen):
    if label in seen:
        g.wait(eng, seen[label])
    else:
        g.before(eng, c, label)


def id_of(g, c):
    return ("per", g.counts.index(c))


class Loop:
    def __init__(self, g, n):
        self.g, self.n = g, n

    def __enter__(self):
        g = self.g
        g.loop_no = g.n_loops
        g.n_loops += 1
        for c in g.counts:
            c.enter = c.at
        self.f = g.nc.Fori(0, self.n)
        g.i = self.f.__enter__()
        return g.i

    def __exit__(self, *a):
        g = self.g
        for c in g.counts:
            per = c.at - c.enter
            key = (g.loop_no, id_of(g, c))
            assert g.dry or g.plan.get(key) == per
            g.plan[key] = per
            c.at = c.enter + per * self.n
            c.enter = 0
        g.i = g.loop_no = None
        self.f.__exit__(*a)


def build(nc, d, plan, dry):
    with ExitStack() as ctx:
        g = Gen(nc, plan, dry)
        sp, act, dve, pe, pool = nc.sync, nc.scalar, nc.vector, nc.tensor, nc.gpsimd

        def sb(name, shape, dt=F32):
            return ctx.enter_context(nc.sbuf_tensor(name, shape, dt))

        def dram(name, shape, dt=F32):
            return nc.dram_tensor(name, shape, dt, kind="Internal").ap()

        def count(name, step=1, eng=None):
            return Count(g, ctx.enter_context(nc.semaphore(name)), step, eng)

        PS = [ctx.enter_context(nc.psum_tensor(f"ps{i}", [128, 512], F32)) for i in range(8)]

        cv, cs = count("c_dve", 1, dve), count("c_act", 1, act)
        cp, cg = count("c_pe", 1, pe), count("c_pool", 1, pool)
        misc = count("c_misc")
        g.misc = misc.sem
        cx = [count(f"c_x{k}", 16) for k in range(8)]
        ca = [count(f"c_in{k}", 16) for k in range(2)]
        cb = [count(f"c_out{k}", 16) for k in range(2)]
        cl, ck = count("c_load", 16), count("c_pre", 16)
        for c in [c for c in g.counts if c not in cx]:
            sp.sem_inc(c.sem, LEAD)
            c.at = LEAD
        nc.all_engine_barrier()

        def V(ins, label=None):
            return cv.inc(ins, label)

        def A(ins, label=None):
            return cs.inc(ins, label)

        def M(ins, label=None):
            return cp.inc(ins, label)

        def G(ins, label=None):
            return cg.inc(ins, label)

        def VV(ins):
            t = cv.inc(ins)
            g.wait(dve, t)
            return t

        def AA(ins):
            t = cs.inc(ins)
            g.wait(act, t)
            return t

        def phase():
            for c in [*cx, *ca, *cb, cl, ck]:
                g.wait(sp, c.now())
            nc.all_engine_barrier()

        def regs(eng, n, name):
            return [eng.alloc_register(f"{name}{k}") for k in range(n)]

        R_dve, R_pe = regs(dve, 8, "bd"), regs(pe, 8, "bp")

        iota = sb("iota", [128, 128])
        iotab = sb("iotab", [128, 128], BF)
        ident = sb("ident", [128, 128])
        identb = sb("identb", [128, 128], BF)
        tri = sb("tri", [128, 128])
        ones = sb("ones", [128, 128])
        zer = sb("zer", [128, 128], BF)
        io = lambda out, pat, cm: pool.iota(out, pat, base=0, channel_multiplier=cm,
                                            allow_small_or_imprecise_dtypes=True)
        G(io(iota[:, :], [[1, 128]], 0))
        G(io(iotab[:, :], [[1, 128]], 0))
        G(io(tri[:, :], [[1, 128]], -1))
        V(dve.memset(ones[:, :], 1.0))
        V(dve.memset(zer[:, :], 0.0))
        g.wait(dve, cg.now())
        V(dve.tensor_scalar(ident[:, :], tri[:, :], 0.0, None, ALU.is_equal))
        VV(dve.tensor_scalar(identb[:, :], tri[:, :], 0.0, None, ALU.is_equal))
        VV(dve.tensor_scalar(tri[:, :], tri[:, :], 0.0, None, ALU.is_lt))

        phase()

        def hold(eng):
            eng.sem_inc(misc.sem, 1)

        idx = [sb(f"idx{k}", [128, T + 8], I32) for k in range(2)]
        node = [sb(f"node{k}", [128, T]) for k in range(2)]
        loc = [sb(f"loc{k}", [128, T + 8]) for k in range(2)]
        bI = [sb(f"bI{k}", [1, T + 8], I32) for k in range(2)]
        cnt = sb("cnt", [B, 128])

        WORDS = 38400
        WORK = sb("work", [128, WORDS])

        def area(off, shape, dt=F32):
            n = int(np.prod(shape[1:]))
            w = n if dt != BF else n // 2
            v = WORK[0:shape[0], off:off + w]
            if dt != F32:
                v = v.bitcast(dt)
            if len(shape) == 3:
                v = v.rearrange("p (a b) -> p a b", a=shape[1])
            elif len(shape) == 4:
                v = v.rearrange("p (a b c) -> p a b c", a=shape[1], b=shape[2])
            return v, off + w

        first, _ = area(0, [128, 8, 2], I32)
        zi, _ = area(16, [128, 1], I32)
        g.wait(pool, V(dve.memset(zi, 0)))
        for k in range(8):
            cx[k].inc(pool.indirect_dma_start(first[:, k, :], None, d["pair"].rearrange("p t w -> (p t) w"),
                                              bass.IndirectOffsetOnAxis(ap=zi, axis=0)))
        phase()

        WT = [2, 20]
        tab = [dram("tab0", [128 * TR, 2], I32), dram("tab1", [128 * TR, 20], I32)]

        def group_edges():
            keys = [(d["dst"], d["dstT"]), (d["src"], d["srcT"])]
            o = 0
            ki, o = area(o, [EP, 2, ET], I32)
            kf, o = area(o, [EP, 2, ET])
            hi, o = area(o, [EP, 2, ET])
            lo, o = area(o, [EP, 2, ET])
            fill, o = area(o, [128, 56, 20], I32)
            OHh, o = area(o, [EP, 4, 8, 64], BF)
            OHl, o = area(o, [EP, 4, 8, 128], BF)
            OHhT, o = area(o, [50, 4, 8, 128])
            KT, o = area(o, [EP, 4, 8, EP], I32)
            JO = o
            junk, o = area(o, [EP, 16, 128])
            junk2, o = area(o, [EP, 16, 128])
            Rs, o = area(o, [B, 4, 128])
            PAY0, o = area(o, [EP, 2, 8, 2], I32)
            PAY1, o = area(o, [EP, 2, 8, 20], I32)
            POS, o = area(o, [EP, 2, 16])
            RNK, o = area(o, [EP, 2, 16])
            kg, o = area(o, [EP, 2, 16])
            ti, o = area(o, [EP, 2, 16], I32)
            tf, o = area(o, [EP, 2, 16])
            rowI, o = area(o, [EP, 2, 16], I32)
            s1, o = area(o, [B, 2, 128])
            s2, o = area(o, [B, 128])
            c1, o = area(o, [B, 8])
            c1i, o = area(o, [B, 8], I32)
            cmp, o = area(o, [B, T])
            tio, o = area(o, [B, T])
            assert o <= WORDS, o
            PAY = [PAY0, PAY1]
            for k in range(2):
                cl.inc(sp.dma_start(ki[:, k, :], keys[k][0]))
            V(dve.memset(fill, 0))
            g.wait(dve, cv.now())
            g.wait(act, V(dve.memset(fill[:, :, 0], -1)))
            for q in range(15):
                ck.inc(act.dma_start(tab[1].rearrange("(p q a) w -> p q (a w)", p=128, q=15)[:, q, :],
                                     fill.rearrange("p a w -> p (a w)")))
            fill0, _ = area(JO, [128, TR, 2], I32)
            V(dve.memset(fill0, 0))
            g.wait(dve, cv.now())
            g.wait(act, V(dve.memset(fill0[:, :, 1], -1)))
            ck.inc(act.dma_start(tab[0].rearrange("(p a) w -> p a w", p=128), fill0))
            G(io(tio, [[1, T]], 0))
            g.wait(dve, cl.now(), cg.now())
            t1 = lo.bitcast(I32)
            V(dve.tensor_scalar(t1, ki, 7, None, ALU.arith_shift_right))
            V(dve.tensor_copy(kf, ki))
            g.wait(dve, cv.now())
            VV(dve.tensor_copy(hi, t1))
            VV(dve.tensor_scalar(ki, ki, 127, None, ALU.bitwise_and))
            VV(dve.tensor_copy(lo, ki))
            R = [PS[0][0:B, 0:128], PS[1][0:B, 0:128]]
            for k in range(2):
                M(pe.matmul(R[k], zer[:, 0:B], zer[:, :], start=True, stop=False, skip_group_check=True))
            phase()

            def onehots(i, k, u):
                a = i * 16 + 8 * u
                V(dve.tensor_tensor(OHh[:, 2 * k + u, :, 0:50],
                                    iota[0:EP, None, 0:50].to_broadcast([EP, 8, 50]),
                                    hi[:, k, bass.ds(a, 8)][:, :, None].to_broadcast([EP, 8, 50]),
                                    ALU.is_equal))
                return V(dve.tensor_tensor(OHl[:, 2 * k + u, :, :],
                                           iota[0:EP, None, :].to_broadcast([EP, 8, 128]),
                                           lo[:, k, bass.ds(a, 8)][:, :, None].to_broadcast([EP, 8, 128]),
                                           ALU.is_equal))

            with g.loop(ET // 16) as i:
                for u in range(2):
                    for k in range(2):
                        g.before(dve, cp, f"h{k}{u}")
                        g.wait(pe, onehots(i, k, u))
                        for n in range(8):
                            mm = pe.matmul(R[k], OHh[:, 2 * k + u, n, 0:B], OHl[:, 2 * k + u, n, :], start=False,
                                           stop=False, skip_group_check=True)
                        M(mm, f"h{k}{u}")
            phase()
            g.wait(dve, M(pe.transpose(PS[2][0:B, 0:B], tri[0:B, 0:B], ident[0:B, 0:B])))
            triT = junk[0:B, 0, 0:B]
            VV(dve.tensor_copy(triT, PS[2][0:B, 0:B]))
            for k in range(2):
                s = s1[:, k, :]
                VV(dve.tensor_copy(s, R[k]))
                if k == 0:
                    V(dve.tensor_copy(cnt[:, :], s))
                VV(dve.tensor_tensor_scan(s2, ones[0:B, :], s, 0.0, ALU.mult, ALU.add))
                VV(dve.tensor_scalar(c1[:, 0:1], s2[:, 127:128], 127.0, None, ALU.add))
                VV(dve.tensor_copy(c1i[:, 0:1], c1[:, 0:1]))
                VV(dve.tensor_scalar(c1i[:, 1:2], c1i[:, 0:1], 7, None, ALU.arith_shift_right))
                VV(dve.tensor_copy(c1[:, 1:2], c1i[:, 1:2]))
                VV(dve.tensor_tensor(s, s2, s, ALU.subtract))
                g.wait(pe, cv.now())
                g.wait(dve, M(pe.matmul(PS[3][0:B, 0:1], triT, c1[:, 1:2], start=True, stop=True)))
                VV(dve.tensor_copy(c1[:, 2:3], PS[3][0:B, 0:1]))
                VV(dve.tensor_scalar(c1[:, 3:4], c1[:, 2:3], 128.0, None, ALU.mult))
                VV(dve.tensor_scalar(s, s, c1[:, 3:4], None, ALU.add))
                VV(dve.tensor_scalar(cmp, tio, c1[:, 2:3], None, ALU.is_ge))
                g.wait(pe, cv.now())
                pe.matmul(PS[4][:, 0:416], ones[0:B, :], cmp[:, 0:416], start=True, stop=True)
                pe.matmul(PS[5][:, 0:416], ones[0:B, :], cmp[:, 416:832], start=True, stop=True)
                t = M(pe.matmul(R[k], ident[0:B, 0:B], s, start=True, stop=False, skip_group_check=True))
                g.wait(dve, t)
                V(dve.memset(bI[k][0:1, T:T + 8], 0))
                for q in range(2):
                    V(dve.tensor_scalar(loc[k][:, 416 * q:416 * q + 416], PS[4 + q][:, 0:416], -1.0, None, ALU.add))
                    V(dve.tensor_scalar(bI[k][0:1, 416 * q:416 * q + 416], PS[4 + q][0:1, 0:416], -1.0, None, ALU.add))
                g.wait(dve, cv.now())
                g.wait(pe, cv.now())
                g.wait(act, t)
                A(act.copy(Rs[:, 2 * k, :], R[k]))
            phase()

            BT = [PS[2][0:50, :].bitcast(BF), PS[3][0:50, :].bitcast(BF)]
            with g.loop(ET // 16) as i:
                snap = {}
                for u in range(2):
                    a = i * 16 + 8 * u
                    kt, pt, oh, oht = {}, {}, {}, {}
                    g.before(sp, cv, f"rank{u}")
                    for k in range(2):
                        kt[k] = ca[u].inc(sp.dma_start(
                            KT[:, 2 * k + u, :, :], keys[k][1][bass.ds(a, 8), :][None, :, :].to_broadcast([EP, 8, EP])))
                    for k in range(2):
                        g.before(sp, cx[2 * k + u], f"sc{k}.{u}")
                    for k in range(2):
                        pt = cb[u].inc(sp.dma_start(PAY[k][:, u, :, 0:2], d["pair"][:, bass.ds(a, 8), :]))
                    pt = cb[u].inc(sp.dma_start(PAY1[:, u, :, 2:20], d["attr"][:, bass.ds(a, 8), :].bitcast(I32)))
                    g.before(dve, cp, f"m7{u}")
                    for k in range(2):
                        oh[k] = onehots(i, k, u)
                    V(dve.tensor_copy(kg[:, u, :].rearrange("p (k n) -> p k n", k=2), kf[:, :, bass.ds(a, 8)]))
                    for k in range(2):
                        g.wait(pe, oh[k])
                        if u == 0:
                            g.before(pe, cs, f"ohT{k}1")
                        else:
                            g.wait(pe, snap[0])
                        hold(pe)
                        for n in range(8):
                            mm = pe.transpose(BT[k][:, 128 * n:128 * n + EP], OHh[:, 2 * k + u, n, 0:50],
                                              identb[0:EP, 0:EP])
                        g.wait(act, M(mm))
                        oht[k] = A(act.copy(OHhT[:, 2 * k + u, :, 0:EP],
                                            BT[k].rearrange("p (n e) -> p n e", n=8)[:, :, 0:EP]), f"ohT{k}{u}")
                    g.wait(dve, kt[1])
                    g.wait(dve, cv.now())
                    for k in range(2):
                        for n in range(8):
                            jw = V(dve.scalar_tensor_tensor(
                                junk[:, 8 * k + n, 0:EP], KT[:, 2 * k + u, n, :], kg[:, u, 8 * k + n:8 * k + n + 1],
                                tri[0:EP, 0:EP], ALU.is_equal, ALU.mult,
                                accum_out=RNK[:, u, 8 * k + n:8 * k + n + 1]), f"rank{u}")
                    pos = {}
                    for n in range(8):
                        m1, m2 = {}, {}
                        for k in range(2):
                            if n == 0:
                                g.wait(pe, oht[k])
                            elif (k, n) in snap:
                                g.wait(pe, snap[k, n])
                            m2[k] = M(pe.matmul(R[k], OHh[:, 2 * k + u, n, 0:B], OHl[:, 2 * k + u, n, :], start=False,
                                                stop=False, skip_group_check=True))
                        for k in range(2):
                            g.wait(pe, pos.get((k, n - 2)))
                            m1[k] = M(pe.matmul(PS[4 + 2 * k + n % 2][0:EP, 0:128], OHhT[:, 2 * k + u, n, 0:EP][0:B, :],
                                                Rs[:, 2 * k + n % 2, :], start=True, stop=True), f"m{n}{u}")
                        for k in range(2):
                            g.wait(act, m2[k])
                            snap[k, n + 1] = snap[0] = A(act.copy(Rs[:, 2 * k + (n + 1) % 2, :], R[k]))
                        for k in range(2):
                            g.wait(dve, m1[k])
                            pos[k, n] = V(dve.scalar_tensor_tensor(
                                junk2[:, 8 * k + n, :], PS[4 + 2 * k + n % 2][0:EP, 0:128], 1.0, OHl[:, 2 * k + u, n, :],
                                ALU.mult, ALU.mult, accum_out=POS[:, u, 8 * k + n:8 * k + n + 1]))
                    g.wait(dve, cv.now())
                    VV(dve.tensor_tensor(POS[:, u, :], POS[:, u, :], RNK[:, u, :], ALU.add))
                    VV(dve.tensor_copy(ti[:, u, :], POS[:, u, :]))
                    for k in range(2):
                        g.before(dve, cx[2 * k + u], f"sc{k}.{u}")
                    VV(dve.tensor_scalar(rowI[:, u, :], ti[:, u, :], 7, None, ALU.arith_shift_right))
                    VV(dve.tensor_copy(tf[:, u, :], rowI[:, u, :]))
                    VV(dve.scalar_tensor_tensor(POS[:, u, :], tf[:, u, :], -128.0, POS[:, u, :], ALU.mult, ALU.add))
                    VV(dve.scalar_tensor_tensor(tf[:, u, :], POS[:, u, :], float(TR), tf[:, u, :], ALU.mult, ALU.add))
                    ro = V(dve.tensor_copy(rowI[:, u, :], tf[:, u, :]))
                    g.wait(pool, ro, pt)
                    hold(pool)
                    for k in range(2):
                        for n in range(8):
                            cx[2 * k + u].inc(pool.indirect_dma_start(
                                tab[k], bass.IndirectOffsetOnAxis(ap=rowI[:, u, 8 * k + n:8 * k + n + 1], axis=0),
                                PAY[k][:, u, n, :], None), f"sc{k}.{u}")
            phase()
            S4 = T // 4
            for k in range(2):
                W = WT[k]
                bF, o = area(0, [128, T])
                g.wait(dve, cv.now())
                V(dve.tensor_copy(bF, loc[k][:, 0:T]))
                for q in range(4):
                    stage, _ = area(T + 20 * S4 * (q % 2), [128, S4, W], I32)
                    g.wait(sp, rd[q - 2] if q >= 2 else cv.now())
                    ld = ca[q % 2].inc(sp.dma_start(stage, tab[k].rearrange("(p t) w -> p t w", p=128)[:, S4 * q:S4 * q + S4, :]))
                    g.wait(dve, ld)
                    V(dve.tensor_copy(idx[k][:, S4 * q:S4 * q + S4], stage[:, :, 1 if k else 0]))
                    t = V(dve.tensor_copy(node[k][:, S4 * q:S4 * q + S4], stage[:, :, 0 if k else 1]))
                    rd = {q: t} if q == 0 else {**rd, q: t}
                V(dve.memset(idx[k][:, T:T + 8], 0))
                g.wait(dve, cv.now())
                VV(dve.scalar_tensor_tensor(loc[k][:, 0:T], bF, -128.0, node[k][:, :], ALU.mult, ALU.add))
                VV(dve.memset(loc[k][:, T:T + 8], -1.0))
            phase()


        group_edges()
        x = sb("x", [128, B, 64])
        padm = sb("padm", [128, B])

        def bc(v, shape):
            return v.to_broadcast(shape)

        def load(dst, name, src=None):
            return cl.inc(sp.dma_start(dst, d[name] if src is None else src))

        def loadb(dst, ap1):
            return cl.inc(sp.dma_start(dst, ap1[None, :].to_broadcast([128, ap1.shape[0]])))

        def norm(out, src, F, st, relu, gam=None, bet=None, sq=None):
            m, v = st[:, 0, :], st[:, 1, :]
            VV(dve.tensor_reduce(m, src, AX.X, ALU.add))
            VV(dve.tensor_scalar(m, m, 1.0 / F, None, ALU.mult))
            VV(dve.tensor_tensor(out, src, bc(m[:, :, None], [128, B, F]), ALU.subtract))
            VV(dve.tensor_tensor(sq, out, out, ALU.mult))
            VV(dve.tensor_reduce(v, sq, AX.X, ALU.add))
            g.wait(act, VV(dve.tensor_scalar(v, v, 1.0 / F, 1e-5, ALU.mult, ALU.add)))
            g.wait(dve, A(act.sqrt(m, v)))
            VV(dve.reciprocal(v, m))
            VV(dve.tensor_tensor(out, out, bc(v[:, :, None], [128, B, F]), ALU.mult))
            if relu:
                VV(dve.tensor_scalar(out, out, 0.0, None, ALU.max))
            if gam is not None:
                VV(dve.tensor_tensor(out, out, bc(gam[:, None, :], [128, B, F]), ALU.mult))
                VV(dve.tensor_tensor(out, out, bc(bet[:, None, :], [128, B, F]), ALU.add))

        def dense(src, K, rhs, F, bias, CT, evac):
            done, copied = {}, {}
            n_out = 1 if F <= 128 else 4
            for c in range((B + 3) // 4):
                b0, nb = 4 * c, min(4, B - 4 * c)
                g.wait(pe, copied.get(c - 2))
                for j in range(nb):
                    mm = pe.transpose(PS[c % 2][0:K, 128 * j:128 * j + 128], src(b0 + j), ident[:, :])
                g.wait(act, M(mm))
                t = A(act.copy(CT[0:K, c % 2, 0:128 * nb], PS[c % 2][0:K, 0:128 * nb]))
                copied[c] = t
                g.wait(pe, t)
                if n_out == 1:
                    bank = [PS[2 + c % 2]]
                    g.wait(pe, *done.get(c - 2, []))
                    at = lambda j: bank[0][:, F * j:F * j + F]
                else:
                    bank = PS[2:2 + n_out]
                    g.wait(pe, *done.get(c - 1, []))
                    at = lambda j: bank[j][:, 0:F]
                for j in range(nb):
                    mm = pe.matmul(at(j), CT[0:K, c % 2, 128 * j:128 * j + 128], rhs, start=True, stop=bias is None)
                    if bias is not None:
                        mm = pe.matmul(at(j), ones[0:1, :], bias, start=False, stop=True)
                t = M(mm)
                if n_out == 1:
                    views = bank[0][:, 0:F * nb].rearrange("p (a f) -> p a f", a=nb)
                else:
                    views = [at(j) for j in range(nb)]
                done[c] = evac(c, b0, nb, views, t)

        def onehot_nodes(P, k, a, u):
            return V(dve.tensor_tensor(P[:, u, :, :], bc(iota[:, None, :], [128, 8, 128]),
                                       bc(loc[k][:, bass.ds(a, 8)][:, :, None], [128, 8, 128]), ALU.is_equal),
                     f"P{u}")

        def onehot_aside(P, k, a, u, seen):
            if seen is not None:
                last_use(g, pool, cp, f"mm{u}", seen)
            t = G(pool.tensor_tensor(P[:, u, :, :], bc(iota[:, None, :], [128, 8, 128]),
                                     bc(loc[k][:, bass.ds(a, 8)][:, :, None], [128, 8, 128]), ALU.subtract))
            g.wait(pool, t)
            g.wait(act, G(pool.tensor_tensor(P[:, u, :, :], P[:, u, :, :], P[:, u, :, :], ALU.mult)))
            pv = P[:, u, :, :].rearrange("p n e -> p (n e)")
            A(act.activation(pv, pv, ACT.Relu, bias=ones[:, 0:1], scale=-1.0))

        def blocks(eng, R, k, a):
            eng.load(R, bI[k][0:1, bass.ds(a, 8)])
            return [eng.snap(r, min_val=0, max_val=B - 1) for r in R]

        def gathers(table, X, RI, k, i, u, free):
            for c, label in free:
                g.before(pool, c, label)
            t = G(pool.tensor_copy(RI[:, u, :], idx[k][:, bass.ds(i * 16 + 8 * u, 8)]))
            g.wait(pool, t)
            hold(pool)
            return [cx[2 * u + n // 4].inc(pool.indirect_dma_start(
                X[:, u, n, :], None, table, bass.IndirectOffsetOnAxis(ap=RI[:, u, n:n + 1], axis=0)))
                for n in range(8)][3::4]

        def add_blocks(acc, bs, view, F, u, i):
            for n in range(8):
                t = V(dve.tensor_tensor(acc[:, bass.ds(bs[n], 1), :].rearrange("p a f -> p (a f)"),
                                        acc[:, bass.ds(bs[n], 1), :].rearrange("p a f -> p (a f)"),
                                        view(n), ALU.add), f"add{u}" if n == 7 else None)
                g.wait(dve, t)

        def transposed(P, PT, u, bank, last):
            g.wait(pe, last)
            hold(pe)
            for n in range(8):
                mm = pe.transpose(PS[bank + n // 4][:, 128 * (n % 4):128 * (n % 4) + 128], P[:, u, n, :], ident[:, :])
                if n % 4 == 3:
                    g.wait(act, M(mm))
                    t = A(act.copy(PT[:, u, n - 3:n + 1, :].rearrange("p a e -> p (a e)"), PS[bank + n // 4][:, :]), f"PT{u}")
            return t

        def ahead(i, u):
            return i * 16 + 8 * (u + 1), 1 - u

        V(dve.memset(x[:, :, :], 0.0))
        VV(dve.memset(padm[:, :], 0.0))
        pcol, _ = area(0, [128, 1])
        g.wait(dve, G(io(pcol, [[0, 1]], 1)))
        VV(dve.tensor_scalar(padm[:, B - 1:B], pcol, float(N - 128 * (B - 1)), None, ALU.is_ge))
        g.wait(sp, cv.now())
        load(x[:, 0:B - 1, :], None, d["x"][0:128 * (B - 1), :].rearrange("(b p) f -> p b f", p=128))
        load(x[0:N - 128 * (B - 1), B - 1, :], None, d["x"][128 * (B - 1):N, :])
        phase()

        def network0():
            o = 0
            CAT, o = area(o, [128, B, 128])
            X, o = area(o, [128, 2, 8, 64])
            P, o = area(o, [128, 2, 8, 128])
            RI, o = area(o, [128, 2, 8], I32)
            tmp, o = area(o, [128, B, 64])
            st, o = area(o, [128, 4, B])
            rdeg, o = area(o, [128, B])
            CT, o = area(o, [128, 2, 512])
            Wc, o = area(o, [128, 3, 64])
            prm, o = area(o, [128, 5, 64])
            sc, o = area(o, [128, 3, 64])
            bi, o = area(o, [128, 3, 64])
            ta, o = area(o, [128, 2, 4, 64])
            te, o = area(o, [128, 2, 4, 64])
            assert o <= WORDS
            table = dram("t0", [NP, 64])
            h = CAT[:, :, 64:128]
            norm(h, x[:, :, :], 64, st, True, sq=tmp)
            g.wait(dve, M(pe.transpose(PS[7][:, 0:B], cnt[:, :], ident[0:B, 0:B])))
            VV(dve.tensor_scalar(rdeg, PS[7][:, 0:B], 1.0, None, ALU.max))
            VV(dve.reciprocal(rdeg, rdeg))
            for l in range(3):
                load(Wc[0:64, l, :], None, d["L0_gnn_W_l"][l])
                load(Wc[64:128, l, :], None, d["L0_gnn_W_r"][l])
                for j, n in enumerate(["b", "gamma", "beta", "run_mean", "run_var"]):
                    t = loadb(prm[:, j, :], d["L0_gnn_" + n][l])
                g.wait(dve, t, cl.now())
                g.wait(act, VV(dve.tensor_scalar(prm[:, 4, :], prm[:, 4, :], 1e-5, None, ALU.add)))
                g.wait(dve, A(act.sqrt(sc[:, l, :], prm[:, 4, :])))
                VV(dve.reciprocal(sc[:, l, :], sc[:, l, :]))
                VV(dve.tensor_tensor(sc[:, l, :], sc[:, l, :], prm[:, 1, :], ALU.mult))
                VV(dve.tensor_tensor(bi[:, l, :], prm[:, 0, :], prm[:, 3, :], ALU.subtract))
                VV(dve.tensor_tensor(bi[:, l, :], bi[:, l, :], sc[:, l, :], ALU.mult))
                VV(dve.tensor_tensor(bi[:, l, :], bi[:, l, :], prm[:, 2, :], ALU.add))
                g.wait(sp, VV(dve.tensor_tensor(Wc[:, l, :], Wc[:, l, :], sc[:, l, :], ALU.mult)))
            for l in range(3):
                g.wait(sp, cv.now())
                cl.inc(sp.dma_start(table.rearrange("(b p) f -> p b f", p=128), h))
                V(dve.memset(CAT[:, :, 0:64], 0.0))
                phase()
                with g.loop(NG) as i:
                    for u in range(2):
                        gt = gathers(table, X, RI, 0, i, u, [(cp, f"mm{u}")])
                        g.before(dve, cp, f"mm{u}")
                        g.wait(pe, onehot_nodes(P, 0, i * 16 + 8 * u, u))
                        bs = blocks(dve, R_dve, 0, i * 16 + 8 * u)
                        for n in range(8):
                            if n % 4 == 0:
                                g.wait(pe, gt[n // 4])
                            mm = pe.matmul(PS[u][:, 64 * n:64 * n + 64], P[:, u, n, :], X[:, u, n, :], start=True, stop=True)
                        g.wait(dve, M(mm, f"mm{u}"))
                        add_blocks(CAT[:, :, 0:64], bs, lambda n: PS[u][:, 64 * n:64 * n + 64], 64, u, i)
                phase()
                VV(dve.tensor_tensor(CAT[:, :, 0:64], CAT[:, :, 0:64], bc(rdeg[:, :, None], [128, B, 64]), ALU.mult))
                g.wait(pe, cv.now())

                def evac(c, b0, nb, ps, t):
                    a, e = ta[:, c % 2, 0:nb, :], te[:, c % 2, 0:nb, :]
                    g.wait(dve, t)
                    r = VV(dve.tensor_tensor(a, ps, bc(bi[:, l, :][:, None, :], [128, nb, 64]), ALU.add))
                    VV(dve.tensor_scalar(e, a, 0.0, None, ALU.min))
                    g.wait(act, cv.now())
                    g.wait(dve, A(act.activation(e, e, ACT.Exp)))
                    VV(dve.tensor_scalar(a, a, 0.0, -1.0, ALU.max, ALU.add))
                    VV(dve.tensor_tensor(h[:, b0:b0 + nb, :], a, e, ALU.add))
                    return [r]

                dense(lambda b: CAT[:, b, :], 128, Wc[:, l, :], 64, None, CT, evac)
            VV(dve.tensor_tensor(x[:, :, :], x[:, :, :], h, ALU.add))
            phase()

        network0()

        def network1():
            o = 0
            TB, o = area(o, [128, B, 66])
            X, o = area(o, [128, 2, 8, 66])
            P, o = area(o, [128, 2, 8, 128])
            PT, o = area(o, [128, 2, 8, 128])
            RI, o = area(o, [128, 2, 8], I32)
            tmp, o = area(o, [128, B, 64])
            st, o = area(o, [128, 4, B])
            S1, o = area(o, [128, B, 2])
            acc, o = area(o, [128, B, 130])
            wa, o = area(o, [128, 2, 2, 64])
            wv, o = area(o, [128, 2, 64])
            eg, o = area(o, [128, 2, 8, 2])
            el, o = area(o, [128, 2, 8, 2])
            ms, o = area(o, [128, 2, 8, 130])
            assert o <= WORDS, o
            table = dram("t1", [NP, 66])
            h = TB[:, :, 0:64]
            norm(h, x[:, :, :], 64, st, True, sq=tmp)
            for q in range(2):
                loadb(wv[:, q, :], d["L1_gnn_W"][q])
                loadb(wa[:, q, :, :].rearrange("p a f -> p (a f)"), d["L1_gnn_a"][q])
            g.wait(dve, cl.now())
            for q in range(2):
                for s_ in range(2):
                    VV(dve.tensor_tensor(wa[:, q, s_, :], wa[:, q, s_, :], wv[:, q, :], ALU.mult))
                    VV(dve.tensor_tensor(tmp, h, bc(wa[:, q, s_, :][:, None, :], [128, B, 64]), ALU.mult))
                    VV(dve.tensor_reduce(S1[:, :, q] if s_ == 0 else TB[:, :, 64 + q], tmp, AX.X, ALU.add))
            g.wait(sp, cv.now())
            cl.inc(sp.dma_start(table.rearrange("(b p) f -> p b f", p=128), TB))
            V(dve.memset(acc, 0.0))
            phase()

            def prepare(a, u, inside, seen=None):
                if inside:
                    last_use(g, dve, cp, f"mm{u}", seen)
                g.wait(pe, onehot_nodes(P, 1, a, u))
                bp = blocks(pe, R_pe, 1, a)
                last = None if not inside else prepare.t if u else (cs, "PT1")
                if last == (cs, "PT1"):
                    g.before(pe, cs, "PT1")
                    last = None
                prepare.t = transposed(P, PT, u, 0, last)
                g.wait(pe, prepare.t)
                for n in range(8):
                    mm = pe.matmul(PS[2][:, 64 * u + 2 * n:64 * u + 2 * n + 2], PT[:, u, n, :],
                                   S1[:, bass.ds(bp[n], 1), :].rearrange("p a f -> p (a f)"), start=True, stop=True)
                return M(mm, f"s{u}")

            prepare(0, 0, False)
            phase()
            with g.loop(NG) as i:
                seen = {}
                for u in range(2):
                    gt = gathers(table, X, RI, 1, i, u, [(cv, f"msg{u}")])
                    if u:
                        g.wait(dve, nxt)
                    else:
                        g.before(dve, cp, "s0")
                    g.wait(dve, gt[1])
                    V(dve.tensor_tensor(eg[:, u], PS[2][:, 64 * u:64 * u + 16].rearrange("p (n f) -> p n f", f=2),
                                        X[:, u, :, 64:66], ALU.add))
                    g.wait(dve, cv.now())
                    t = V(dve.scalar_tensor_tensor(eg[:, u], eg[:, u], 0.2, eg[:, u], ALU.mult, ALU.max))
                    g.wait(act, t)
                    t = A(act.activation(el[:, u], eg[:, u], ACT.Exp))
                    g.wait(dve, t)
                    for q in range(2):
                        V(dve.tensor_tensor(ms[:, u, :, 64 * q:64 * q + 64], X[:, u, :, 0:64],
                                            bc(el[:, u, :, q:q + 1], [128, 8, 64]), ALU.mult))
                    t = V(dve.tensor_copy(ms[:, u, :, 128:130], el[:, u]), f"msg{u}")
                    g.wait(pe, t)
                    view = lambda n: PS[3 + n // 3][:, 130 * (n % 3):130 * (n % 3) + 130]
                    for n in range(8):
                        mm = pe.matmul(view(n), P[:, u, n, :], ms[:, u, n, :], start=True, stop=True)
                    seen[f"mm{u}"] = t = M(mm, f"mm{u}")
                    nxt = prepare(*ahead(i, u), True, seen)
                    bs = blocks(dve, R_dve, 1, i * 16 + 8 * u)
                    g.wait(dve, t)
                    add_blocks(acc, bs, view, 130, u, i)
            phase()
            r = st
            for q in range(2):
                VV(dve.tensor_tensor(r[:, q, :], acc[:, :, 128 + q], padm[:, :], ALU.add))
                VV(dve.reciprocal(r[:, q, :], r[:, q, :]))
                VV(dve.scalar_tensor_tensor(tmp, acc[:, :, 64 * q:64 * q + 64], 0.5,
                                            bc(r[:, q, :][:, :, None], [128, B, 64]), ALU.mult, ALU.mult))
                VV(dve.tensor_tensor(x[:, :, :], x[:, :, :], tmp, ALU.add))
            phase()

        network1()

        def id_flags(k, H, FL, IDT, stage, SF, CC, row):
            P_ = 16 * H
            nv = node[k][:, :].rearrange("p (c j) -> p c j", c=16)
            cop = {}
            sv = stage[:, 0:52 * P_].rearrange("p (j c h) -> p j c h", j=52, c=16)
            for j in range(52):
                V(dve.tensor_copy(sv[:, j], bc(nv[:, :, j:j + 1], [128, 16, H])))
            g.wait(pe, cv.now())
            for q in range(13):
                g.wait(pe, cop.get(q - 2))
                for j in range(4):
                    mm = pe.transpose(PS[q % 2][0:P_, 128 * j:128 * j + 128],
                                      stage[:, P_ * (4 * q + j):P_ * (4 * q + j) + P_], ident[:, :])
                g.wait(act, M(mm))
                cop[q] = A(act.copy(IDT[0:P_, 512 * q:512 * q + 512], PS[q % 2][0:P_, :]))
            g.wait(dve, cs.now())
            V(dve.memset(FL[:, :], 0.0))
            g.wait(dve, cv.now())
            VV(dve.tensor_tensor(FL[0:P_, 1:6656], IDT[0:P_, 1:6656], IDT[0:P_, 0:6655], ALU.is_equal))
            VV(dve.tensor_scalar(FL[0:P_, 1:6656], FL[0:P_, 1:6656], -1.0, BIG, ALU.add, ALU.mult))
            V(dve.tensor_copy(CC[0:P_, 0:1], IDT[0:P_, 0:1]))
            VV(dve.tensor_copy(CC[0:P_, 1:2], IDT[0:P_, 6655:6656]))
            to_row(CC, H, row)
            VV(dve.memset(SF[0:1, :], 0.0))
            n = H * 32
            VV(dve.tensor_tensor(SF[0:1, 1:n], row[0:1, 2:n + 1], row[0:1, 1:n], ALU.is_equal))
            for h_ in range(H):
                VV(dve.memset(SF[0:1, 32 * h_:32 * h_ + 1], 0.0))
            VV(dve.tensor_scalar(SF[0:1, 0:n + 1], SF[0:1, 0:n + 1], -1.0, BIG, ALU.add, ALU.mult))

        def to_row(CC, H, row):
            P_ = 16 * H
            g.wait(pe, cv.now(), cs.now())
            for w in range(2):
                mm = pe.transpose(PS[7][0:1, 128 * w:128 * w + P_], CC[0:P_, w:w + 1], ident[0:P_, 0:P_])
            g.wait(dve, M(mm))
            rv = row[0:1, 1:1 + 32 * H].rearrange("p (h c w) -> p h c w", h=H, c=16)
            for w in range(2):
                VV(dve.tensor_copy(rv[:, :, :, w], PS[7][0:1, 128 * w:128 * w + P_].rearrange("p (c h) -> p h c", h=H)))

        def softmax_weights(H, Ev, AT, Fm, FL, SF, CC, row, rowf, rowb, cr):
            P_, n = 16 * H, 32 * H
            ev = Ev[:, 0:T, :].rearrange("p (c j) h -> p c j h", c=16)
            cop = {}
            sv = Fm[:, 0:52 * P_].rearrange("p (j c h) -> p j c h", j=52, c=16)
            for q in range(13):
                t = V(dve.tensor_copy(sv[:, 4 * q:4 * q + 4], ev[:, :, 4 * q:4 * q + 4, :].rearrange("p c j h -> p j c h")))
                g.wait(pe, t, cop.get(q - 2))
                for j in range(4):
                    mm = pe.transpose(PS[q % 2][0:P_, 128 * j:128 * j + 128],
                                      Fm[:, P_ * (4 * q + j):P_ * (4 * q + j) + P_], ident[:, :])
                g.wait(act, M(mm))
                cop[q] = A(act.copy(AT[0:P_, 512 * q:512 * q + 512], PS[q % 2][0:P_, :]))
            g.wait(dve, cs.now())
            fwd = lambda ini: VV(dve.tensor_tensor_scan(Fm[0:P_, 0:6656], FL[0:P_, 0:6656], AT[0:P_, 0:6656], ini, ALU.add, ALU.max))
            back = lambda ini: VV(dve.tensor_tensor_scan(Fm[0:P_, 6655::-1] if False else Fm[0:P_, 0:6656][:, ::-1],
                                                         FL[0:P_, 1:6657][:, ::-1],
                                                         Fm[0:P_, 0:6656][:, ::-1], ini, ALU.add, ALU.max))
            fwd(-BIG)
            VV(dve.tensor_copy(CC[0:P_, 1:2], Fm[0:P_, 6655:6656]))
            back(-BIG)
            VV(dve.tensor_copy(CC[0:P_, 0:1], Fm[0:P_, 0:1]))
            for r in (row, rowf, rowb):
                VV(dve.memset(r[0:1, :], -BIG))
            to_row(CC, H, row)
            VV(dve.tensor_tensor_scan(rowf[0:1, 1:n + 1], SF[0:1, 0:n], row[0:1, 1:n + 1], -BIG, ALU.add, ALU.max))
            VV(dve.tensor_tensor_scan(rowb[0:1, 1:n + 1][:, ::-1], SF[0:1, 1:n + 1][:, ::-1],
                                      row[0:1, 1:n + 1][:, ::-1], -BIG, ALU.add, ALU.max))
            sf0 = SF[0:1, 0:n].rearrange("p (h c w) -> p h c w", h=H, c=16)[:, :, :, 0]
            sf2 = SF[0:1, 1:n + 1].rearrange("p (h c w) -> p h c w", h=H, c=16)[:, :, :, 1]
            lf = rowf[0:1, 0:n].rearrange("p (h c w) -> p h c w", h=H, c=16)[:, :, :, 0]
            rb = rowb[0:1, 2:n + 2].rearrange("p (h c w) -> p h c w", h=H, c=16)[:, :, :, 1]
            cv_ = lambda w: cr[0:1, w, 0:P_].rearrange("p (c h) -> p h c", h=H)
            VV(dve.tensor_tensor(cv_(0), lf, sf0, ALU.add))
            g.wait(pe, VV(dve.tensor_tensor(cv_(1), rb, sf2, ALU.add)))
            for w in range(2):
                mm = pe.matmul(PS[7][0:P_, 256 + w:257 + w], cr[0:1, w, 0:P_], ones[0:1, 0:1], start=True, stop=True)
            g.wait(dve, M(mm))
            VV(dve.tensor_copy(CC[0:P_, 0:2], PS[7][0:P_, 256:258]))
            fwd(CC[0:P_, 0:1])
            back(CC[0:P_, 1:2])
            for q in range(13):
                s = slice(512 * q, 512 * q + 512)
                g.wait(act, V(dve.tensor_tensor(AT[0:P_, s], AT[0:P_, s], Fm[0:P_, s], ALU.subtract)))
                g.wait(pe, A(act.activation(AT[0:P_, s], AT[0:P_, s], ACT.Exp)), cop.get(("b", q - 2)))
                w = 4 * P_
                for j in range(4):
                    mm = pe.transpose(PS[2 + q % 2][:, P_ * j:P_ * j + P_], AT[0:P_, 512 * q + 128 * j:512 * q + 128 * j + 128],
                                      ident[0:P_, 0:P_])
                g.wait(act, M(mm))
                for j in range(4):
                    cop["b", q] = A(act.copy(ev[:, :, 4 * q + j, :], PS[2 + q % 2][:, P_ * j:P_ * j + P_].rearrange("p (c h) -> p c h", h=H)))
            phase()

        def weigh(k, H, Ev, vsp, acc, Vr, P, ms):
            F = 16 * H
            W = F + H
            per = 512 // W
            VV(dve.memset(acc, 0.0))

            def weighed(a, m, u, seen):
                if seen is not None:
                    g.before(sp, cv, f"msg{u}")
                ld = ca[u].inc(sp.dma_start(Vr[:, u], vsp[:, bass.ds(m, 1), :]))
                ex = Ev[:, bass.ds(a, 8), :]
                if seen is not None:
                    last_use(g, dve, cp, f"mm{u}", seen)
                g.wait(dve, ld)
                V(dve.tensor_tensor(ms[:, u, :, 0:F].rearrange("p n (h e) -> p n h e", h=H),
                                    Vr[:, u].rearrange("p (n h e) -> p n h e", n=8, h=H),
                                    bc(ex[:, :, :, None], [128, 8, H, 16]), ALU.mult), f"msg{u}")
                if seen is not None:
                    last_use(g, act, cp, f"mm{u}", seen)
                A(act.copy(ms[:, u, :, F:W], ex))
                onehot_aside(P, k, a, u, seen)
                cs.now(f"ex{u}")

            weighed(0, 0, 0, None)
            phase()
            with g.loop(NG) as i:
                seen = {}
                for u in range(2):
                    if u:
                        g.wait(pe, cv_msg, cs.now())
                    else:
                        g.before(pe, cv, "msg0")
                        g.before(pe, cs, "ex0")
                    view = lambda n: PS[4 * u + n // per][:, W * (n % per):W * (n % per) + W]
                    if u:
                        g.before(pe, cv, "add1")
                    for n in range(8):
                        mm = pe.matmul(view(n), P[:, u, n, :], ms[:, u, n, :], start=True, stop=True)
                    seen[f"mm{u}"] = t = M(mm, f"mm{u}")
                    weighed(ahead(i, u)[0], i * 2 + u + 1, 1 - u, seen)
                    cv_msg = cv.now()
                    bs = blocks(dve, R_dve, k, i * 16 + 8 * u)
                    g.wait(dve, t)
                    add_blocks(acc, bs, view, W, u, i)
            phase()

        def unused_unit(vsp, zeros, Ev):
            V(dve.memset(Ev[:, T:T + 8, :], 0.0))
            g.wait(sp, V(dve.memset(zeros, 0.0)))
            cl.inc(sp.dma_start(vsp[:, 2 * NG, :], zeros))
            phase()

        def network2():
            h, o = area(0, [128, B, 128])
            Ev, o = area(o, [128, T + 8, 8])
            FL, o = area(o, [128, 6658], BF)
            SM, o = area(o, [128, 2048])
            Wp, o = area(o, [128, 3 * 512])
            vec, o = area(o, [128, 6, 128])
            brow, o = area(o, [1, 512 + 512 + 128])
            SF, o = area(o, [1, 258])
            CC, o = area(o, [128, 2])
            row, o = area(o, [1, 260])
            rowf, o = area(o, [1, 260])
            rowb, o = area(o, [1, 260])
            cr, o = area(o, [1, 2, 128])
            st, o = area(o, [128, 4, B])
            RI, o = area(o, [128, 2, 8], I32)
            U = o
            assert U + 13312 <= WORDS, U
            q_, o = area(U, [128, B, 128])
            X, o = area(o, [128, 2, 8, 256])
            P, o = area(o, [128, 2, 8, 128])
            PT = SM.rearrange("p (u n e) -> p u n e", u=2, n=8)
            AT, o = area(U, [128, 6656])
            Fm, o = area(o, [128, 6656])
            acc, o = area(U, [128, B, 136])
            Vr, o = area(o, [128, 2, 1024])
            P2, o = area(o, [128, 2, 8, 128])
            ms, o = area(o, [128, 2, 8, 136])
            assert o <= U + 13312
            xr = Ev.rearrange("p t h -> p (t h)")[:, 0:B * 128].rearrange("p (b f) -> p b f", b=B)
            tmp, _ = area(U + B * 136, [128, B, 128])
            CT, _ = area(U + B * 128, [128, 2, 512])
            KV, _ = area(U + B * 128 + 1024, [128, 2, 4, 256])
            table = dram("t2", [NP, 256])
            vsp = dram("v2", [128, 2 * NG + 1, 1024])
            unused_unit(vsp, tmp.rearrange("p b f -> p (b f)")[:, 0:1024], Ev)
            Wq = Wp[:, 0:512]
            W1 = Wp[:, 512:1024]
            W2 = Wp[:, 1024:1536].rearrange("p (a f) -> p a f", a=4)

            x0 = tmp[:, :, 0:64]
            norm(x0, x[:, :, :], 64, st, True, sq=tmp[:, :, 64:128])
            load(Wp[0:64, 0:128], "WiT")
            t = load(brow[:, 0:128], None, d["L2_gnn_bi"][None, :])
            g.wait(pe, cv.now(), t, cl.now())
            CT0 = SM[:, 0:1024].rearrange("p (a f) -> p a f", a=2)

            def ev0(c, b0, nb, ps, t):
                g.wait(act, t)
                return [A(act.activation(h[:, b0:b0 + nb, :], ps, ACT.Gelu))]

            dense(lambda b: x0[:, b, :], 64, Wp[0:64, 0:128], 128, brow[:, 0:128], CT0, ev0)
            phase()
            id_flags(0, 8, FL, AT, Fm, SF, CC, row)
            phase()
            for l in range(4):
                load(Wp, None, d["W2all"][l])
                load(brow, None, d["b2all"][l][None, :])
                for j, n in enumerate(["ln_g", "ln_b", "b2"]):
                    loadb(vec[:, j, :], d["L2_gnn_" + n][l])
                t = cl.inc(sp.dma_start(vec[:, 3:6, :].rearrange("p a f -> p (a f)"),
                                        d["L2_gnn_Wbeta"][l].to_broadcast([128, 384])))
                phase()
                prev = {}

                def ev1(c, b0, nb, ps, t):
                    g.wait(act, t, prev.get(c - 2))
                    for j in range(nb):
                        A(act.activation(q_[:, b0 + j, :], ps[j][:, 0:128], ACT.Copy, scale=0.25))
                        a_ = A(act.copy(KV[:, c % 2, j, :], ps[j][:, 128:384]))
                    g.wait(sp, a_)
                    prev[c] = cb[c % 2].inc(sp.dma_start(
                        table[128 * b0:128 * (b0 + nb), :].rearrange("(b p) f -> p b f", p=128), KV[:, c % 2, 0:nb, :]))
                    return [a_]

                dense(lambda b: h[:, b, :], 128, Wq[:, 0:384], 384, brow[:, 0:384], CT, ev1)
                phase()

                def prepare(a, u, inside):
                    if inside:
                        g.before(dve, cp, f"tr{u}")
                    t = onehot_nodes(P, 0, a, u)
                    g.wait(pe, t)
                    bp = blocks(pe, R_pe, 0, a)
                    last = None
                    if inside and u:
                        last = prepare.t
                    elif inside:
                        g.before(pe, cs, "PT1")
                    prepare.t = transposed(P, PT, u, 0, last)
                    g.wait(pe, prepare.t)
                    for n in range(8):
                        mm = pe.matmul(PS[2 + 2 * u + n // 4][:, 128 * (n % 4):128 * (n % 4) + 128], PT[:, u, n, :],
                                       q_[:, bass.ds(bp[n], 1), :].rearrange("p a f -> p (a f)"), start=True, stop=True)
                    return M(mm, f"tr{u}")

                prepare(0, 0, False)
                phase()
                with g.loop(NG) as i:
                    for u in range(2):
                        gt = gathers(table, X, RI, 0, i, u, [(cv, f"prod{u}"), (cb[u], f"sp{u}")])
                        me = nxt if u else None
                        nxt = prepare(*ahead(i, u), True)
                        g.wait(sp, *gt)
                        cb[u].inc(sp.dma_start(vsp[:, bass.ds(i * 2 + u, 1), :].rearrange("p a (n f) -> p (a n) f", n=8),
                                               X[:, u, :, 128:256]), f"sp{u}")
                        if u:
                            g.wait(dve, me)
                        else:
                            g.before(dve, cp, "tr0")
                        for z in range(2):
                            kx = X[:, u, 4 * z:4 * z + 4, 0:128]
                            g.wait(dve, gt[z])
                            VV(dve.tensor_tensor(kx, kx, PS[2 + 2 * u + z][:, :].rearrange("p (n f) -> p n f", n=4), ALU.mult))
                            t = V(dve.tensor_reduce(Ev[:, bass.ds(i * 16 + 8 * u + 4 * z, 4), :],
                                                    kx.rearrange("p n (h e) -> p n h e", h=8), AX.X, ALU.add), f"prod{u}")
                phase()
                softmax_weights(8, Ev, AT, Fm, FL, SF, CC, row, rowf, rowb, cr)
                weigh(0, 8, Ev, vsp, acc, Vr, P2, ms)

                rd = SM[:, 0:B * 8].rearrange("p (b h) -> p b h", b=B)
                VV(dve.tensor_scalar(rd, acc[:, :, 128:136], 1e-16, None, ALU.add))
                VV(dve.reciprocal(rd, rd))
                out = acc[:, :, 0:128]
                for h_ in range(8):
                    oh = acc[:, :, 16 * h_:16 * h_ + 16]
                    V(dve.tensor_tensor(oh, oh, bc(rd[:, :, h_:h_ + 1], [128, B, 16]), ALU.mult))
                g.wait(dve, cv.now())
                g.wait(pe, cv.now())

                def ev2(c, b0, nb, ps, t):
                    g.wait(act, t)
                    return [A(act.copy(xr[:, b0:b0 + nb, :], ps))]

                CT2 = SM[:, 512:1536].rearrange("p (a f) -> p a f", a=2)
                dense(lambda b: h[:, b, :], 128, Wq[:, 384:512], 128, brow[:, 384:512], CT2, ev2)
                g.wait(dve, cs.now())
                VV(dve.tensor_tensor(vec[:, 3, :], vec[:, 3, :], vec[:, 5, :], ALU.add))
                VV(dve.tensor_tensor(vec[:, 4, :], vec[:, 4, :], vec[:, 5, :], ALU.subtract))
                S = [128, B, 128]
                z0, z1 = st[:, 0, :], st[:, 1, :]
                VV(dve.tensor_tensor(tmp, out, bc(vec[:, 3, :][:, None, :], S), ALU.mult))
                VV(dve.tensor_reduce(z0, tmp, AX.X, ALU.add))
                VV(dve.tensor_tensor(tmp, xr, bc(vec[:, 4, :][:, None, :], S), ALU.mult))
                VV(dve.tensor_reduce(z1, tmp, AX.X, ALU.add))
                g.wait(act, VV(dve.tensor_tensor(z0, z0, z1, ALU.add)))
                g.wait(dve, A(act.activation(z0, z0, ACT.Exp, scale=-1.0)))
                VV(dve.tensor_scalar(z0, z0, 1.0, None, ALU.add))
                VV(dve.reciprocal(z0, z0))
                VV(dve.tensor_tensor(xr, xr, out, ALU.subtract))
                VV(dve.tensor_tensor(xr, xr, bc(z0[:, :, None], S), ALU.mult))
                VV(dve.tensor_tensor(xr, xr, out, ALU.add))
                VV(dve.tensor_tensor(xr, xr, h, ALU.add))
                norm(h, xr, 128, st, False, vec[:, 0, :], vec[:, 1, :], sq=tmp)
                hT = SM[:, 0:256].rearrange("p (a f) -> p a f", a=2)
                ge = SM[:, 512:1536].rearrange("p (a q f) -> p a q f", a=2, q=4)
                V(dve.tensor_tensor(xr, h, bc(vec[:, 2, :][:, None, :], S), ALU.add))
                g.wait(pe, cv.now())
                tA, tB, tC, tD = {}, {}, {}, {}

                def first_half(b):
                    g.wait(pe, tA.get(b - 2))
                    t = M(pe.transpose(PS[b % 2][:, 0:128], h[:, b, :], ident[:, :]))
                    g.wait(act, t)
                    tA[b] = A(act.copy(hT[:, b % 2, :], PS[b % 2][:, 0:128]))
                    g.wait(pe, tA[b], tB.get(b - 2))
                    for q in range(4):
                        v = PS[2 + b % 2][:, 128 * q:128 * q + 128]
                        pe.matmul(v, W1[:, 128 * q:128 * q + 128], hT[:, b % 2, :], start=True, stop=False)
                        mm = pe.matmul(v, brow[:, 512 + 128 * q:640 + 128 * q], ones[0:1, :], start=False, stop=True)
                    g.wait(act, M(mm), tC.get(b - 2))
                    tB[b] = A(act.activation(ge[:, b % 2].rearrange("p q f -> p (q f)"), PS[2 + b % 2][:, :], ACT.Gelu))

                def second_half(b):
                    g.wait(pe, tB[b], tD.get(b - 2))
                    for q in range(4):
                        mm = pe.matmul(PS[4 + b % 2][:, 0:128], ge[:, b % 2, q, :], W2[:, q, :], start=q == 0, stop=q == 3)
                    tC[b] = M(mm)
                    g.wait(dve, tC[b])
                    tD[b] = V(dve.tensor_tensor(h[:, b, :], xr[:, b, :], PS[4 + b % 2][:, 0:128], ALU.add))

                for b in range(B + 1):
                    if b < B:
                        first_half(b)
                    if b:
                        second_half(b - 1)
                phase()
            load(Wp[:, 0:64], "WoT")
            t = load(brow[:, 0:64], None, d["L2_gnn_bo"][None, :])
            g.wait(pe, t, cl.now())

            def ev3(c, b0, nb, ps, t):
                g.wait(dve, t)
                return [V(dve.tensor_tensor(x[:, b0:b0 + nb, :], x[:, b0:b0 + nb, :], ps, ALU.add))]

            dense(lambda b: h[:, b, :], 128, Wp[:, 0:64], 64, brow[:, 0:64], CT0, ev3)
            phase()

        network2()

        def network3():
            Ev, o = area(0, [128, T + 8, 4])
            FL, o = area(o, [128, 6658], BF)
            PT, o = area(o, [128, 2, 8, 128])
            Wk, o = area(o, [64, 128])
            Wr, o = area(o, [19, 128])
            bq, o = area(o, [1, 128])
            SF, o = area(o, [1, 258])
            CC, o = area(o, [128, 2])
            row, o = area(o, [1, 260])
            rowf, o = area(o, [1, 260])
            rowb, o = area(o, [1, 260])
            cr, o = area(o, [1, 2, 128])
            st, o = area(o, [128, 4, B])
            RI, o = area(o, [128, 2, 8], I32)
            U = o
            q_, o = area(U, [128, B, 32])
            X, o = area(o, [128, 2, 8, 96])
            P, o = area(o, [128, 2, 8, 128])
            AB, o = area(o, [128, 2, 8, 20], I32)
            AtT, o = area(o, [19, 2, 8, 128])
            ve, o = area(o, [128, 2, 8, 64])
            kx, o = area(o, [128, 2, 8, 32])
            CT, o = area(o, [128, 2, 512])
            KV, o = area(o, [128, 2, 4, 96])
            h, o = area(o, [128, B, 64])
            tmp, o = area(o, [128, B, 64])
            assert o <= WORDS
            AT, o = area(U, [128, 6656])
            Fm, o = area(o, [128, 6656])
            assert o <= WORDS
            acc, o = area(U, [128, B, 68])
            Vr, o = area(o, [128, 2, 512])
            P2, o = area(o, [128, 2, 8, 128])
            ms, o = area(o, [128, 2, 8, 68])
            assert o <= WORDS
            table = dram("t3", [NP, 96])
            vsp = dram("v3", [128, 2 * NG + 1, 512])
            unused_unit(vsp, tmp.rearrange("p b f -> p (b f)")[:, 0:512], Ev)
            norm(h, x[:, :, :], 64, st, True, sq=tmp)
            load(Wk, "L3_gnn_qkv_w")
            load(bq, None, d["L3_gnn_qkv_b"][None, :])
            load(Wr, "rpe_wb")
            phase()
            prev = {}

            def ev1(c, b0, nb, ps, t):
                g.wait(act, t, prev.get(c - 2))
                A(act.activation(q_[:, b0:b0 + nb, :], ps[:, :, 0:32], ACT.Copy, scale=float(np.float32(8.0) ** np.float32(-0.5))))
                a_ = A(act.copy(KV[:, c % 2, 0:nb, :], ps[:, :, 32:128]))
                g.wait(sp, a_)
                prev[c] = cb[c % 2].inc(sp.dma_start(
                    table[128 * b0:128 * (b0 + nb), :].rearrange("(b p) f -> p b f", p=128), KV[:, c % 2, 0:nb, :]))
                return [a_]

            dense(lambda b: h[:, b, :], 64, Wk, 128, bq, CT, ev1)
            phase()
            tb = tab[1].rearrange("(p t) w -> p t w", p=128)
            V(dve.memset(AtT[:, :, :, :], 1.0))

            def prepare(a, u, inside):
                if inside:
                    g.before(sp, cp, f"at{u}")
                ld = ca[u].inc(sp.dma_start(AB[:, u], tb[:, bass.ds(a, 8), :]))
                if inside:
                    g.before(dve, cp, f"tr{u}")
                g.wait(pe, onehot_nodes(P, 1, a, u))
                bp = blocks(pe, R_pe, 1, a)
                if inside and not u:
                    g.before(pe, cs, "at1")
                pt = transposed(P, PT, u, 0, prepare.t if inside and u else None)
                g.wait(pe, ld)
                hold(pe)
                for n in range(8):
                    mm = pe.transpose(PS[2 + n // 4][0:18, 128 * (n % 4):128 * (n % 4) + 128],
                                      AB[:, u, n, 2:20].bitcast(F32), ident[:, :])
                g.wait(act, M(mm, f"at{u}"))
                for z in range(2):
                    prepare.t = A(act.copy(AtT[0:18, u, 4 * z:4 * z + 4, :].rearrange("p a e -> p (a e)"), PS[2 + z][0:18, :]), f"at{u}")
                g.wait(pe, prepare.t)
                for n in range(8):
                    v = PS[4 + 2 * u + n // 4][:, 128 * (n % 4):128 * (n % 4) + 128]
                    pe.matmul(v, AtT[:, u, n, :], Wr, start=True, stop=False)
                    mm = pe.matmul(v[:, 0:32], PT[:, u, n, :],
                                   q_[:, bass.ds(bp[n], 1), :].rearrange("p a f -> p (a f)"), start=False, stop=True)
                return M(mm, f"tr{u}")

            g.wait(act, cv.now())
            prepare(0, 0, False)
            phase()
            with g.loop(NG) as i:
                for u in range(2):
                    a = i * 16 + 8 * u
                    gt = gathers(table, X, RI, 1, i, u, [(cv, f"ve{u}")])
                    me = nxt if u else None
                    nxt = prepare(*ahead(i, u), True)
                    if u:
                        g.wait(dve, me)
                    else:
                        g.before(dve, cp, "tr0")
                    g.before(dve, cb[u], f"sp{u}")
                    for z in range(2):
                        ps = PS[4 + 2 * u + z][:, :].rearrange("p (n f) -> p n f", n=4)
                        r = slice(4 * z, 4 * z + 4)
                        g.wait(dve, gt[z])
                        V(dve.tensor_tensor(kx[:, u, r, :], X[:, u, r, 0:32], ps[:, :, 32:64], ALU.add))
                        V(dve.tensor_tensor(ve[:, u, r, :], X[:, u, r, 32:96], ps[:, :, 64:128], ALU.add), f"ve{u}")
                        g.wait(dve, cv.now())
                        VV(dve.tensor_tensor(kx[:, u, r, :], kx[:, u, r, :], ps[:, :, 0:32], ALU.mult))
                        t = VV(dve.tensor_reduce(Ev[:, bass.ds(a + 4 * z, 4), :],
                                                 kx[:, u, r, :].rearrange("p n (h e) -> p n h e", h=4), AX.X, ALU.add))
                    g.wait(sp, t)
                    cb[u].inc(sp.dma_start(vsp[:, bass.ds(i * 2 + u, 1), :],
                                           ve[:, u].rearrange("p n f -> p (n f)")), f"sp{u}")
            phase()
            id_flags(1, 4, FL, AT, Fm, SF, CC, row)
            phase()
            softmax_weights(4, Ev, AT, Fm, FL, SF, CC, row, rowf, rowb, cr)
            weigh(1, 4, Ev, vsp, acc, Vr, P2, ms)
            rd = PT[:, 0, 0:2, :].rearrange("p a b -> p (a b)")[:, 0:B * 4].rearrange("p (b h) -> p b h", b=B)
            VV(dve.tensor_scalar(rd, acc[:, :, 64:68], 1e-16, None, ALU.add))
            VV(dve.reciprocal(rd, rd))
            for h_ in range(4):
                s = slice(16 * h_, 16 * h_ + 16)
                VV(dve.tensor_tensor(acc[:, :, s], acc[:, :, s], bc(rd[:, :, h_:h_ + 1], [128, B, 16]), ALU.mult))
                VV(dve.tensor_tensor(x[:, :, s], x[:, :, s], acc[:, :, s], ALU.add))

        network3()
        g.wait(sp, cv.now())
        cl.inc(sp.dma_start(d["out"][0:128 * (B - 1), :].rearrange("(b p) f -> p b f", p=128), x[:, 0:B - 1, :]))
        cl.inc(sp.dma_start(d["out"][128 * (B - 1):N, :], x[0:N - 128 * (B - 1), B - 1, :]))
        phase()



def prepare(inputs):
    f = lambda name: np.ascontiguousarray(inputs[name])
    a = {}
    src, dst = f("src"), f("dst")
    a["src"], a["dst"] = src.reshape(EP, ET), dst.reshape(EP, ET)
    a["srcT"] = np.ascontiguousarray(a["src"].T)
    a["dstT"] = np.ascontiguousarray(a["dst"].T)
    a["pair"] = np.stack([a["src"], a["dst"]], axis=-1)
    a["attr"] = f("edge_attr_18").reshape(EP, ET, 18)
    a["x"] = f("x")
    for n_ in ("W_l", "W_r", "b", "gamma", "beta", "run_mean", "run_var"):
        a["L0_gnn_" + n_] = f("L0_gnn_" + n_)
    a["L1_gnn_W"], a["L1_gnn_a"] = f("L1_gnn_W"), f("L1_gnn_a")
    T_ = lambda n_: f("L2_gnn_" + n_).transpose(0, 2, 1)
    W2T = T_("W2").reshape(4, 4, 128, 128).transpose(0, 2, 1, 3).reshape(4, 128, 512)
    a["W2all"] = np.concatenate([T_("Wq"), T_("Wk"), T_("Wv"), T_("Ws"), T_("W1"), W2T], axis=2)
    a["b2all"] = np.concatenate([f("L2_gnn_" + n_) for n_ in ("bq", "bk", "bv", "bs", "b1", "b2")], axis=1)[:, 0:1152]
    a["WiT"], a["WoT"] = f("L2_gnn_Wi").T, f("L2_gnn_Wo").T
    for n_ in ("bi", "ln_g", "ln_b", "b2", "Wbeta", "bo"):
        a["L2_gnn_" + n_] = f("L2_gnn_" + n_)
    a["L3_gnn_qkv_w"], a["L3_gnn_qkv_b"] = f("L3_gnn_qkv_w"), f("L3_gnn_qkv_b")
    a["rpe_wb"] = np.concatenate([np.concatenate([f(f"L3_gnn_{n_}_rpe_w"), f(f"L3_gnn_{n_}_rpe_b")[None]], axis=0)
                                  for n_ in "qkv"], axis=1)
    return {k: np.ascontiguousarray(v) for k, v in a.items()}


def program(new, arrays, outputs):
    plan = {}
    for dry in (True, False):
        nc = new()
        d = {k: nc.dram_tensor(f"in_{k}", list(v.shape), mybir.dt.from_np(v.dtype), kind="ExternalInput").ap()
             for k, v in arrays.items()}
        for k, shape in outputs.items():
            d[k] = nc.dram_tensor(k, shape, F32, kind="ExternalOutput").ap()
        build(nc, d, plan, dry)
    return nc


def kernel(**inputs):
    import concourse.bacc as bacc
    from concourse.bass_utils import run_bass_kernel_spmd

    arrays = prepare(inputs)
    nc = program(lambda: bacc.Bacc("TRN2", target_bir_lowering=False, num_devices=1), arrays, {"out": [N, 64]})
    r = run_bass_kernel_spmd(nc, [{f"in_{k}": v for k, v in arrays.items()}], core_ids=[0])
    return r.results[0]["out"]
```

```python
from contextlib import ExitStack

import numpy as np
import concourse.bass as bass
from concourse import mybir

F32 = mybir.dt.float32
I32 = mybir.dt.int32
BF = mybir.dt.bfloat16
ALU = mybir.AluOpType
ACT = mybir.ActivationFunctionType
AX = mybir.AxisListType

N, E, B = 6250, 100000, 49
NP = B * 128
EP, ET = 125, 800
T = 832
NG = T // 16
TR = T + 8
BIG = 1.0e30
LEAD = 512


class Count:

    def __init__(self, g, sem, step=1, eng=None):
        self.g, self.sem, self.step, self.at = g, sem, step, 0
        self.enter, self.eng = 0, eng
        g.counts.append(self)

    def inc(self, ins, label=None):
        ins.then_inc(self.sem, self.step)
        if self.eng is not None:
            self.g.waited = {w for w in self.g.waited if w[0] != self.eng.engine}
        self.at += self.step
        return self.now(label)

    def now(self, label=None):
        t = (self, self.at)
        if label is not None:
            self.g.plan[(self.g.loop_no, label)] = self.at - self.enter
        return t


class Gen:

    def __init__(self, nc, plan, dry):
        self.nc, self.plan, self.dry = nc, plan, dry
        self.counts, self.i, self.loop_no, self.n_loops = [], None, None, 0
        self.waited = set()

    def loop(self, n):
        return Loop(self, n)

    def wait(self, eng, *toks):
        for tok in toks:
            if tok is None:
                continue
            c, v = tok
            if self.i is not None and v > c.enter:
                per = self.plan.get((self.loop_no, id_of(self, c)), 1)
                self.wait_reg(eng, c, self.i * per + v)
            elif v > 0:
                eng.wait_ge(c.sem, v)

    def wait_reg(self, eng, c, v):
        if (eng.engine, c.sem) in self.waited:
            eng.sem_inc(self.misc, 1)
            self.waited = {w for w in self.waited if w[0] != eng.engine}
        eng.wait_ge(c.sem, v)
        if eng is self.nc.sync:
            eng.sem_inc(self.misc, 1)
        else:
            self.waited.add((eng.engine, c.sem))

    def before(self, eng, c, label):
        per = self.plan.get((self.loop_no, id_of(self, c)), 1)
        at = self.plan.get((self.loop_no, label), 1)
        v = c.enter + at - per
        assert self.dry or v > 0
        self.wait_reg(eng, c, self.i * per + max(v, 1))


def last_use(g, eng, c, label, seen):
    if label in seen:
        g.wait(eng, seen[label])
    else:
        g.before(eng, c, label)


def id_of(g, c):
    return ("per", g.counts.index(c))


class Loop:
    def __init__(self, g, n):
        self.g, self.n = g, n

    def __enter__(self):
        g = self.g
        g.loop_no = g.n_loops
        g.n_loops += 1
        for c in g.counts:
            c.enter = c.at
        self.f = g.nc.Fori(0, self.n)
        g.i = self.f.__enter__()
        return g.i

    def __exit__(self, *a):
        g = self.g
        for c in g.counts:
            per = c.at - c.enter
            key = (g.loop_no, id_of(g, c))
            assert g.dry or g.plan.get(key) == per
            g.plan[key] = per
            c.at = c.enter + per * self.n
            c.enter = 0
        g.i = g.loop_no = None
        self.f.__exit__(*a)


def build(nc, d, plan, dry):
    with ExitStack() as ctx:
        g = Gen(nc, plan, dry)
        sp, act, dve, pe, pool = nc.sync, nc.scalar, nc.vector, nc.tensor, nc.gpsimd

        def sb(name, shape, dt=F32):
            return ctx.enter_context(nc.sbuf_tensor(name, shape, dt))

        def dram(name, shape, dt=F32):
            return nc.dram_tensor(name, shape, dt, kind="Internal").ap()

        def count(name, step=1, eng=None):
            return Count(g, ctx.enter_context(nc.semaphore(name)), step, eng)

        PS = [ctx.enter_context(nc.psum_tensor(f"ps{i}", [128, 512], F32)) for i in range(8)]

        cv, cs = count("c_dve", 1, dve), count("c_act", 1, act)
        cp, cg = count("c_pe", 1, pe), count("c_pool", 1, pool)
        misc = count("c_misc")
        g.misc = misc.sem
        cx = [count(f"c_x{k}", 16) for k in range(8)]
        ca = [count(f"c_in{k}", 16) for k in range(2)]
        cb = [count(f"c_out{k}", 16) for k in range(2)]
        cl, ck, cm = count("c_load", 16), count("c_skip0", 16), count("c_skip1", 16)
        for c in [c for c in g.counts if c not in cx]:
            sp.sem_inc(c.sem, LEAD)
            c.at = LEAD
        nc.all_engine_barrier()

        def V(ins, label=None):
            return cv.inc(ins, label)

        def A(ins, label=None):
            return cs.inc(ins, label)

        def M(ins, label=None):
            return cp.inc(ins, label)

        def G(ins, label=None):
            return cg.inc(ins, label)

        def VV(ins):
            t = cv.inc(ins)
            g.wait(dve, t)
            return t

        def AA(ins):
            t = cs.inc(ins)
            g.wait(act, t)
            return t

        def phase():
            for c in [*cx, *ca, *cb, cl, ck, cm]:
                g.wait(sp, c.now())
            nc.all_engine_barrier()

        def regs(eng, n, name):
            return [eng.alloc_register(f"{name}{k}") for k in range(n)]

        R_dve, R_pe = regs(dve, 32, "bd"), regs(pe, 8, "bp")

        iota = sb("iota", [128, 128])
        iotab = sb("iotab", [128, 128], BF)
        ident = sb("ident", [128, 128])
        identb = sb("identb", [128, 128], BF)
        tri = sb("tri", [128, 128])
        ones = sb("ones", [128, 128])
        zer = sb("zer", [128, 128], BF)
        io = lambda out, pat, cm: pool.iota(out, pat, base=0, channel_multiplier=cm,
                                            allow_small_or_imprecise_dtypes=True)
        G(io(iota[:, :], [[1, 128]], 0))
        G(io(iotab[:, :], [[1, 128]], 0))
        G(io(tri[:, :], [[1, 128]], -1))
        V(dve.memset(ones[:, :], 1.0))
        V(dve.memset(zer[:, :], 0.0))
        g.wait(dve, cg.now())
        V(dve.tensor_scalar(ident[:, :], tri[:, :], 0.0, None, ALU.is_equal))
        VV(dve.tensor_scalar(identb[:, :], tri[:, :], 0.0, None, ALU.is_equal))
        VV(dve.tensor_scalar(tri[:, :], tri[:, :], 0.0, None, ALU.is_lt))

        phase()

        def hold(eng):
            eng.sem_inc(misc.sem, 1)

        idx = [sb(f"idx{k}", [128, T + 8], I32) for k in range(2)]
        node = [sb(f"node{k}", [128, T]) for k in range(2)]
        loc = [sb(f"loc{k}", [128, T + 16]) for k in range(2)]
        bI = [sb(f"bI{k}", [1, T + 8], I32) for k in range(2)]
        cnt = sb("cnt", [B, 128])

        WORDS = 38400
        WORK = sb("work", [128, WORDS])

        def area(off, shape, dt=F32):
            n = int(np.prod(shape[1:]))
            w = n if dt != BF else n // 2
            v = WORK[0:shape[0], off:off + w]
            if dt != F32:
                v = v.bitcast(dt)
            if len(shape) == 3:
                v = v.rearrange("p (a b) -> p a b", a=shape[1])
            elif len(shape) == 4:
                v = v.rearrange("p (a b c) -> p a b c", a=shape[1], b=shape[2])
            return v, off + w

        first, _ = area(0, [128, 8, 2], I32)
        zi, _ = area(16, [128, 1], I32)
        g.wait(pool, V(dve.memset(zi, 0)))
        for k in range(8):
            cx[k].inc(pool.indirect_dma_start(first[:, k, :], None, d["pair"].rearrange("p t w -> (p t) w"),
                                              bass.IndirectOffsetOnAxis(ap=zi, axis=0)))
        phase()

        WT = [2, 20]
        tab = [dram("tab0", [128 * TR, 2], I32), dram("tab1", [128 * TR, 20], I32)]

        def group_edges():
            keys = [(d["dst"], d["dstT"]), (d["src"], d["srcT"])]
            o = 0
            ki, o = area(o, [EP, 2, ET], I32)
            kf, o = area(o, [EP, 2, ET])
            hi, o = area(o, [EP, 2, ET])
            lo, o = area(o, [EP, 2, ET])
            fill, o = area(o, [128, 56, 20], I32)
            OHh, o = area(o, [EP, 4, 8, 64], BF)
            OHl, o = area(o, [EP, 4, 8, 128], BF)
            OHhT, o = area(o, [50, 4, 8, 128])
            KT, o = area(o, [EP, 4, 8, EP], I32)
            JO = o
            junk, o = area(o, [EP, 16, 128])
            junk2, o = area(o, [EP, 16, 128])
            Rs, o = area(o, [B, 4, 128])
            PAY0, o = area(o, [EP, 2, 8, 2], I32)
            PAY1, o = area(o, [EP, 2, 8, 20], I32)
            POS, o = area(o, [EP, 2, 16])
            RNK, o = area(o, [EP, 2, 16])
            kg, o = area(o, [EP, 2, 16])
            ti, o = area(o, [EP, 2, 16], I32)
            tf, o = area(o, [EP, 2, 16])
            rowI, o = area(o, [EP, 2, 16], I32)
            s1, o = area(o, [B, 2, 128])
            s2, o = area(o, [B, 128])
            c1, o = area(o, [B, 8])
            c1i, o = area(o, [B, 8], I32)
            cmp, o = area(o, [B, T])
            tio, o = area(o, [B, T])
            assert o <= WORDS, o
            PAY = [PAY0, PAY1]
            for k in range(2):
                cl.inc(sp.dma_start(ki[:, k, :], keys[k][0]))
            V(dve.memset(fill, 0))
            g.wait(dve, cv.now())
            g.wait(act, V(dve.memset(fill[:, :, 0], -1)))
            for q in range(15):
                ck.inc(act.dma_start(tab[1].rearrange("(p q a) w -> p q (a w)", p=128, q=15)[:, q, :],
                                     fill.rearrange("p a w -> p (a w)")))
            fill0, _ = area(JO, [128, TR, 2], I32)
            V(dve.memset(fill0, 0))
            g.wait(dve, cv.now())
            g.wait(act, V(dve.memset(fill0[:, :, 1], -1)))
            ck.inc(act.dma_start(tab[0].rearrange("(p a) w -> p a w", p=128), fill0))
            G(io(tio, [[1, T]], 0))
            g.wait(dve, cl.now(), cg.now())
            t1 = lo.bitcast(I32)
            V(dve.tensor_scalar(t1, ki, 7, None, ALU.arith_shift_right))
            V(dve.tensor_copy(kf, ki))
            g.wait(dve, cv.now())
            VV(dve.tensor_copy(hi, t1))
            VV(dve.tensor_scalar(ki, ki, 127, None, ALU.bitwise_and))
            VV(dve.tensor_copy(lo, ki))
            R = [PS[0][0:B, 0:128], PS[1][0:B, 0:128]]
            for k in range(2):
                M(pe.matmul(R[k], zer[:, 0:B], zer[:, :], start=True, stop=False, skip_group_check=True))
            phase()

            def onehots_hi(i, k, u):
                a = i * 16 + 8 * u
                return V(dve.tensor_tensor(OHh[:, 2 * k + u, :, 0:50],
                                           iota[0:EP, None, 0:50].to_broadcast([EP, 8, 50]),
                                           hi[:, k, bass.ds(a, 8)][:, :, None].to_broadcast([EP, 8, 50]),
                                           ALU.is_equal))

            def onehots(i, k, u):
                a = i * 16 + 8 * u
                onehots_hi(i, k, u)
                return V(dve.tensor_tensor(OHl[:, 2 * k + u, :, :],
                                           iota[0:EP, None, :].to_broadcast([EP, 8, 128]),
                                           lo[:, k, bass.ds(a, 8)][:, :, None].to_broadcast([EP, 8, 128]),
                                           ALU.is_equal))

            with g.loop(ET // 16) as i:
                for u in range(2):
                    for k in range(2):
                        g.before(dve, cp, f"h{k}{u}")
                        if k == 0:
                            g.wait(pe, onehots(i, k, u))
                        else:
                            g.wait(pe, onehots_hi(i, k, u))
                            g.before(pool, cp, f"h{k}{u}")
                            g.wait(act, G(pool.tensor_tensor(
                                OHl[:, 2 * k + u, :, :], iota[0:EP, None, :].to_broadcast([EP, 8, 128]),
                                lo[:, k, bass.ds(i * 16 + 8 * u, 8)][:, :, None].to_broadcast([EP, 8, 128]),
                                ALU.subtract)))
                            ov = OHl[:, 2 * k + u, :, :].rearrange("p n e -> p (n e)")
                            AA(act.activation(ov, ov, ACT.Square))
                            g.wait(pe, A(act.activation(ov, ov, ACT.Relu, bias=ones[0:EP, 0:1], scale=-1.0)))
                        for n in range(8):
                            mm = pe.matmul(R[k], OHh[:, 2 * k + u, n, 0:B], OHl[:, 2 * k + u, n, :], start=False,
                                           stop=False, skip_group_check=True)
                        M(mm, f"h{k}{u}")
            phase()
            g.wait(dve, M(pe.transpose(PS[2][0:B, 0:B], tri[0:B, 0:B], ident[0:B, 0:B])))
            triT = junk[0:B, 0, 0:B]
            VV(dve.tensor_copy(triT, PS[2][0:B, 0:B]))
            for k in range(2):
                s = s1[:, k, :]
                VV(dve.tensor_copy(s, R[k]))
                if k == 0:
                    V(dve.tensor_copy(cnt[:, :], s))
                VV(dve.tensor_tensor_scan(s2, ones[0:B, :], s, 0.0, ALU.mult, ALU.add))
                VV(dve.tensor_scalar(c1[:, 0:1], s2[:, 127:128], 127.0, None, ALU.add))
                VV(dve.tensor_copy(c1i[:, 0:1], c1[:, 0:1]))
                VV(dve.tensor_scalar(c1i[:, 1:2], c1i[:, 0:1], 7, None, ALU.arith_shift_right))
                VV(dve.tensor_copy(c1[:, 1:2], c1i[:, 1:2]))
                VV(dve.tensor_tensor(s, s2, s, ALU.subtract))
                g.wait(pe, cv.now())
                g.wait(dve, M(pe.matmul(PS[3][0:B, 0:1], triT, c1[:, 1:2], start=True, stop=True)))
                VV(dve.tensor_copy(c1[:, 2:3], PS[3][0:B, 0:1]))
                VV(dve.tensor_scalar(c1[:, 3:4], c1[:, 2:3], 128.0, None, ALU.mult))
                VV(dve.tensor_scalar(s, s, c1[:, 3:4], None, ALU.add))
                VV(dve.tensor_scalar(cmp, tio, c1[:, 2:3], None, ALU.is_ge))
                g.wait(pe, cv.now())
                pe.matmul(PS[4][:, 0:416], ones[0:B, :], cmp[:, 0:416], start=True, stop=True)
                pe.matmul(PS[5][:, 0:416], ones[0:B, :], cmp[:, 416:832], start=True, stop=True)
                t = M(pe.matmul(R[k], ident[0:B, 0:B], s, start=True, stop=False, skip_group_check=True))
                g.wait(dve, t)
                V(dve.memset(bI[k][0:1, T:T + 8], 0))
                for q in range(2):
                    V(dve.tensor_scalar(loc[k][:, 416 * q:416 * q + 416], PS[4 + q][:, 0:416], -1.0, None, ALU.add))
                    V(dve.tensor_scalar(bI[k][0:1, 416 * q:416 * q + 416], PS[4 + q][0:1, 0:416], -1.0, None, ALU.add))
                g.wait(dve, cv.now())
                g.wait(pe, cv.now())
                g.wait(act, t)
                A(act.copy(Rs[:, 2 * k, :], R[k]))
            phase()

            BT = [PS[2][0:50, :].bitcast(BF), PS[3][0:50, :].bitcast(BF)]
            with g.loop(ET // 16) as i:
                snap = {}
                for u in range(2):
                    a = i * 16 + 8 * u
                    kt, pt, oh, oht = {}, {}, {}, {}
                    g.before(sp, cv, f"rank{u}")
                    for k in range(2):
                        kt[k] = ca[u].inc(sp.dma_start(
                            KT[:, 2 * k + u, :, :], keys[k][1][bass.ds(a, 8), :][None, :, :].to_broadcast([EP, 8, EP])))
                    for k in range(2):
                        g.before(sp, cx[2 * k + u], f"sc{k}.{u}")
                    for k in range(2):
                        pt = cb[u].inc(sp.dma_start(PAY[k][:, u, :, 0:2], d["pair"][:, bass.ds(a, 8), :]))
                    pt = cb[u].inc(sp.dma_start(PAY1[:, u, :, 2:20], d["attr"][:, bass.ds(a, 8), :].bitcast(I32)))
                    g.before(dve, cp, f"m7{u}")
                    for k in range(2):
                        oh[k] = onehots(i, k, u)
                    V(dve.tensor_copy(kg[:, u, :].rearrange("p (k n) -> p k n", k=2), kf[:, :, bass.ds(a, 8)]))
                    for k in range(2):
                        g.wait(pe, oh[k])
                        if u == 0:
                            g.before(pe, cs, f"ohT{k}1")
                        else:
                            g.wait(pe, snap[0])
                        hold(pe)
                        for n in range(8):
                            mm = pe.transpose(BT[k][:, 128 * n:128 * n + EP], OHh[:, 2 * k + u, n, 0:50],
                                              identb[0:EP, 0:EP])
                        g.wait(act, M(mm))
                        oht[k] = A(act.copy(OHhT[:, 2 * k + u, :, 0:EP],
                                            BT[k].rearrange("p (n e) -> p n e", n=8)[:, :, 0:EP]), f"ohT{k}{u}")
                    g.wait(dve, kt[1])
                    g.wait(dve, cv.now())
                    for k in range(2):
                        for n in range(8):
                            jw = V(dve.scalar_tensor_tensor(
                                junk[:, 8 * k + n, 0:EP], KT[:, 2 * k + u, n, :], kg[:, u, 8 * k + n:8 * k + n + 1],
                                tri[0:EP, 0:EP], ALU.is_equal, ALU.mult,
                                accum_out=RNK[:, u, 8 * k + n:8 * k + n + 1]), f"rank{u}")
                    pos = {}
                    for n in range(8):
                        m1, m2 = {}, {}
                        for k in range(2):
                            if n == 0:
                                g.wait(pe, oht[k])
                            elif (k, n) in snap:
                                g.wait(pe, snap[k, n])
                            m2[k] = M(pe.matmul(R[k], OHh[:, 2 * k + u, n, 0:B], OHl[:, 2 * k + u, n, :], start=False,
                                                stop=False, skip_group_check=True))
                        for k in range(2):
                            g.wait(pe, pos.get((k, n - 2)))
                            m1[k] = M(pe.matmul(PS[4 + 2 * k + n % 2][0:EP, 0:128], OHhT[:, 2 * k + u, n, 0:EP][0:B, :],
                                                Rs[:, 2 * k + n % 2, :], start=True, stop=True), f"m{n}{u}")
                        for k in range(2):
                            g.wait(act, m2[k])
                            snap[k, n + 1] = snap[0] = A(act.copy(Rs[:, 2 * k + (n + 1) % 2, :], R[k]))
                        for k in range(2):
                            g.wait(dve, m1[k])
                            pos[k, n] = V(dve.scalar_tensor_tensor(
                                junk2[:, 8 * k + n, :], PS[4 + 2 * k + n % 2][0:EP, 0:128], 1.0, OHl[:, 2 * k + u, n, :],
                                ALU.mult, ALU.mult, accum_out=POS[:, u, 8 * k + n:8 * k + n + 1]))
                    g.wait(dve, cv.now())
                    VV(dve.tensor_tensor(POS[:, u, :], POS[:, u, :], RNK[:, u, :], ALU.add))
                    VV(dve.tensor_copy(ti[:, u, :], POS[:, u, :]))
                    for k in range(2):
                        g.before(dve, cx[2 * k + u], f"sc{k}.{u}")
                    VV(dve.tensor_scalar(rowI[:, u, :], ti[:, u, :], 7, None, ALU.arith_shift_right))
                    VV(dve.tensor_copy(tf[:, u, :], rowI[:, u, :]))
                    VV(dve.scalar_tensor_tensor(POS[:, u, :], tf[:, u, :], -128.0, POS[:, u, :], ALU.mult, ALU.add))
                    VV(dve.scalar_tensor_tensor(tf[:, u, :], POS[:, u, :], float(TR), tf[:, u, :], ALU.mult, ALU.add))
                    ro = V(dve.tensor_copy(rowI[:, u, :], tf[:, u, :]))
                    g.wait(pool, ro, pt)
                    hold(pool)
                    for k in range(2):
                        for n in range(8):
                            cx[2 * k + u].inc(pool.indirect_dma_start(
                                tab[k], bass.IndirectOffsetOnAxis(ap=rowI[:, u, 8 * k + n:8 * k + n + 1], axis=0),
                                PAY[k][:, u, n, :], None), f"sc{k}.{u}")
            phase()
            S4 = T // 4
            for k in range(2):
                W = WT[k]
                bF, o = area(0, [128, T])
                g.wait(dve, cv.now())
                V(dve.tensor_copy(bF, loc[k][:, 0:T]))
                for q in range(4):
                    stage, _ = area(T + 20 * S4 * (q % 2), [128, S4, W], I32)
                    g.wait(sp, rd[q - 2] if q >= 2 else cv.now())
                    ld = ca[q % 2].inc(sp.dma_start(stage, tab[k].rearrange("(p t) w -> p t w", p=128)[:, S4 * q:S4 * q + S4, :]))
                    g.wait(dve, ld)
                    V(dve.tensor_copy(idx[k][:, S4 * q:S4 * q + S4], stage[:, :, 1 if k else 0]))
                    t = V(dve.tensor_copy(node[k][:, S4 * q:S4 * q + S4], stage[:, :, 0 if k else 1]))
                    rd = {q: t} if q == 0 else {**rd, q: t}
                V(dve.memset(idx[k][:, T:T + 8], 0))
                g.wait(dve, cv.now())
                VV(dve.scalar_tensor_tensor(loc[k][:, 0:T], bF, -128.0, node[k][:, :], ALU.mult, ALU.add))
                VV(dve.memset(loc[k][:, T:T + 16], -1.0))
            phase()


        group_edges()
        x = sb("x", [128, B, 64])
        padm = sb("padm", [128, B])

        def bc(v, shape):
            return v.to_broadcast(shape)

        def load(dst, name, src=None):
            return cl.inc(sp.dma_start(dst, d[name] if src is None else src))

        def loadb(dst, ap1):
            return cl.inc(sp.dma_start(dst, ap1[None, :].to_broadcast([128, ap1.shape[0]])))

        def norm(out, src, F, st, relu, gam=None, bet=None, sq=None):
            m, v = st[:, 0, :], st[:, 1, :]
            VV(dve.tensor_reduce(m, src, AX.X, ALU.add))
            VV(dve.tensor_scalar(m, m, 1.0 / F, None, ALU.mult))
            VV(dve.tensor_tensor(out, src, bc(m[:, :, None], [128, B, F]), ALU.subtract))
            VV(dve.tensor_tensor(sq, out, out, ALU.mult))
            VV(dve.tensor_reduce(v, sq, AX.X, ALU.add))
            g.wait(act, VV(dve.tensor_scalar(v, v, 1.0 / F, 1e-5, ALU.mult, ALU.add)))
            g.wait(dve, A(act.sqrt(m, v)))
            VV(dve.reciprocal(v, m))
            VV(dve.tensor_tensor(out, out, bc(v[:, :, None], [128, B, F]), ALU.mult))
            if relu:
                VV(dve.tensor_scalar(out, out, 0.0, None, ALU.max))
            if gam is not None:
                VV(dve.tensor_tensor(out, out, bc(gam[:, None, :], [128, B, F]), ALU.mult))
                VV(dve.tensor_tensor(out, out, bc(bet[:, None, :], [128, B, F]), ALU.add))

        def dense(src, K, rhs, F, bias, CT, evac):
            done, copied = {}, {}
            n_out = 1 if F <= 128 else 4
            for c in range((B + 3) // 4):
                b0, nb = 4 * c, min(4, B - 4 * c)
                g.wait(pe, copied.get(c - 2))
                for j in range(nb):
                    mm = pe.transpose(PS[c % 2][0:K, 128 * j:128 * j + 128], src(b0 + j), ident[:, :])
                g.wait(act, M(mm))
                t = A(act.copy(CT[0:K, c % 2, 0:128 * nb], PS[c % 2][0:K, 0:128 * nb]))
                copied[c] = t
                g.wait(pe, t)
                if n_out == 1:
                    bank = [PS[2 + c % 2]]
                    g.wait(pe, *done.get(c - 2, []))
                    at = lambda j: bank[0][:, F * j:F * j + F]
                else:
                    bank = PS[2:2 + n_out]
                    g.wait(pe, *done.get(c - 1, []))
                    at = lambda j: bank[j][:, 0:F]
                for j in range(nb):
                    mm = pe.matmul(at(j), CT[0:K, c % 2, 128 * j:128 * j + 128], rhs, start=True, stop=bias is None)
                    if bias is not None:
                        mm = pe.matmul(at(j), ones[0:1, :], bias, start=False, stop=True)
                t = M(mm)
                if n_out == 1:
                    views = bank[0][:, 0:F * nb].rearrange("p (a f) -> p a f", a=nb)
                else:
                    views = [at(j) for j in range(nb)]
                done[c] = evac(c, b0, nb, views, t)

        def onehot_nodes(P, k, a, u):
            return V(dve.tensor_tensor(P[:, u, :, :], bc(iota[:, None, :], [128, 8, 128]),
                                       bc(loc[k][:, bass.ds(a, 8)][:, :, None], [128, 8, 128]), ALU.is_equal),
                     f"P{u}")

        def onehot_aside(P, k, a, u, seen):
            if seen is not None:
                last_use(g, pool, cp, f"mm{u}", seen)
            g.wait(act, G(pool.tensor_tensor(P[:, u, :, :], bc(iota[:, None, :], [128, 8, 128]),
                                             bc(loc[k][:, bass.ds(a, 8)][:, :, None], [128, 8, 128]), ALU.subtract)))
            pv = P[:, u, :, :].rearrange("p n e -> p (n e)")
            AA(act.activation(pv, pv, ACT.Square))
            A(act.activation(pv, pv, ACT.Relu, bias=ones[:, 0:1], scale=-1.0))

        def blocks(eng, R, k, a, n=8):
            eng.load(R[0:n], bI[k][0:1, bass.ds(a, n)])
            return [eng.snap(r, min_val=0, max_val=B - 1) for r in R[0:n]]

        def gathers(table, X, RI, k, i, u, free, by_dve):
            for c, label in free:
                g.before(pool, c, label)
            if not by_dve:
                g.wait(pool, G(pool.tensor_copy(RI[:, u, :], idx[k][:, bass.ds(i * 16 + 8 * u, 8)])))
            elif u:
                g.wait(pool, rows[1])
            else:
                g.before(pool, cv, "rows0")
            hold(pool)
            if by_dve:
                a, v = ahead(i, u)
                rows[v] = V(dve.tensor_copy(RI[:, v, :], idx[k][:, bass.ds(a, 8)]), f"rows{v}")
            return [cx[2 * u + n // 4].inc(pool.indirect_dma_start(
                X[:, u, n, :], None, table, bass.IndirectOffsetOnAxis(ap=RI[:, u, n:n + 1], axis=0)))
                for n in range(8)][3::4]

        rows = {}

        def first_rows(RI, k):
            V(dve.tensor_copy(RI[:, 0, :], idx[k][:, 0:8]))

        def add_blocks(accs, bs, view, u, parts):
            for n in range(8):
                g.wait(dve, parts.get(n))
                av = accs[n % len(accs)][:, bass.ds(bs[n], 1), :].rearrange("p a f -> p (a f)")
                added[n % len(accs)] = t = V(dve.tensor_tensor(av, av, view(n), ALU.add), f"add{u}" if n == 7 else None)
                g.wait(dve, added.get((n + 1) % len(accs)))
            added.clear()

        added = {}

        def transposed(P, PT, u, bank):
            hold(pe)
            for n in range(8):
                mm = pe.transpose(PS[bank + n // 4][:, 128 * (n % 4):128 * (n % 4) + 128], P[:, u, n, :], ident[:, :])
                if n % 4 == 3:
                    g.wait(act, M(mm))
                    t = A(act.copy(PT[:, u, n - 3:n + 1, :].rearrange("p a e -> p (a e)"), PS[bank + n // 4][:, :]), f"PT{u}")
            return t

        def ahead(i, u):
            return i * 16 + 8 * (u + 1), 1 - u

        V(dve.memset(x[:, :, :], 0.0))
        VV(dve.memset(padm[:, :], 0.0))
        pcol, _ = area(0, [128, 1])
        g.wait(dve, G(io(pcol, [[0, 1]], 1)))
        VV(dve.tensor_scalar(padm[:, B - 1:B], pcol, float(N - 128 * (B - 1)), None, ALU.is_ge))
        g.wait(sp, cv.now())
        load(x[:, 0:B - 1, :], None, d["x"][0:128 * (B - 1), :].rearrange("(b p) f -> p b f", p=128))
        load(x[0:N - 128 * (B - 1), B - 1, :], None, d["x"][128 * (B - 1):N, :])
        phase()

        def network0():
            o = 0
            CAT, o = area(o, [128, B, 128])
            X, o = area(o, [128, 2, 8, 64])
            P, o = area(o, [128, 2, 8, 128])
            RI, o = area(o, [128, 2, 8], I32)
            tmp, o = area(o, [128, B, 64])
            st, o = area(o, [128, 4, B])
            rdeg, o = area(o, [128, B])
            CT, o = area(o, [128, 2, 512])
            Wc, o = area(o, [128, 3, 64])
            prm, o = area(o, [128, 5, 64])
            sc, o = area(o, [128, 3, 64])
            bi, o = area(o, [128, 3, 64])
            ta, o = area(o, [128, 2, 4, 64])
            te, o = area(o, [128, 2, 4, 64])
            assert o <= WORDS
            table = dram("t0", [NP, 64])
            h = CAT[:, :, 64:128]
            norm(h, x[:, :, :], 64, st, True, sq=tmp)
            g.wait(dve, M(pe.transpose(PS[7][:, 0:B], cnt[:, :], ident[0:B, 0:B])))
            VV(dve.tensor_scalar(rdeg, PS[7][:, 0:B], 1.0, None, ALU.max))
            VV(dve.reciprocal(rdeg, rdeg))
            for l in range(3):
                load(Wc[0:64, l, :], None, d["L0_gnn_W_l"][l])
                load(Wc[64:128, l, :], None, d["L0_gnn_W_r"][l])
                for j, n in enumerate(["b", "gamma", "beta", "run_mean", "run_var"]):
                    t = loadb(prm[:, j, :], d["L0_gnn_" + n][l])
                g.wait(dve, t, cl.now())
                g.wait(act, VV(dve.tensor_scalar(prm[:, 4, :], prm[:, 4, :], 1e-5, None, ALU.add)))
                g.wait(dve, A(act.sqrt(sc[:, l, :], prm[:, 4, :])))
                VV(dve.reciprocal(sc[:, l, :], sc[:, l, :]))
                VV(dve.tensor_tensor(sc[:, l, :], sc[:, l, :], prm[:, 1, :], ALU.mult))
                VV(dve.tensor_tensor(bi[:, l, :], prm[:, 0, :], prm[:, 3, :], ALU.subtract))
                VV(dve.tensor_tensor(bi[:, l, :], bi[:, l, :], sc[:, l, :], ALU.mult))
                VV(dve.tensor_tensor(bi[:, l, :], bi[:, l, :], prm[:, 2, :], ALU.add))
                g.wait(sp, VV(dve.tensor_tensor(Wc[:, l, :], Wc[:, l, :], sc[:, l, :], ALU.mult)))
            for l in range(3):
                g.wait(sp, cv.now())
                cl.inc(sp.dma_start(table.rearrange("(b p) f -> p b f", p=128), h))
                V(dve.memset(CAT[:, :, 0:64], 0.0))
                phase()
                with g.loop(NG) as i:
                    for u in range(2):
                        gt = gathers(table, X, RI, 0, i, u, [(cp, f"mm{u}")], False)
                        g.before(dve, cp, f"mm{u}")
                        g.wait(pe, onehot_nodes(P, 0, i * 16 + 8 * u, u))
                        bs = blocks(dve, R_dve, 0, i * 16 + 8 * u)
                        for n in range(8):
                            if n % 4 == 0:
                                g.wait(pe, gt[n // 4])
                            mm = pe.matmul(PS[u][:, 64 * n:64 * n + 64], P[:, u, n, :], X[:, u, n, :], start=True, stop=True)
                        add_blocks([CAT[:, :, 0:64]], bs, lambda n: PS[u][:, 64 * n:64 * n + 64], u,
                                   {0: M(mm, f"mm{u}")})
                phase()
                VV(dve.tensor_tensor(CAT[:, :, 0:64], CAT[:, :, 0:64], bc(rdeg[:, :, None], [128, B, 64]), ALU.mult))
                g.wait(pe, cv.now())

                def evac(c, b0, nb, ps, t):
                    a, e = ta[:, c % 2, 0:nb, :], te[:, c % 2, 0:nb, :]
                    g.wait(dve, t)
                    r = VV(dve.tensor_tensor(a, ps, bc(bi[:, l, :][:, None, :], [128, nb, 64]), ALU.add))
                    VV(dve.tensor_scalar(e, a, 0.0, None, ALU.min))
                    g.wait(act, cv.now())
                    g.wait(dve, A(act.activation(e, e, ACT.Exp)))
                    VV(dve.tensor_scalar(a, a, 0.0, -1.0, ALU.max, ALU.add))
                    VV(dve.tensor_tensor(h[:, b0:b0 + nb, :], a, e, ALU.add))
                    return [r]

                dense(lambda b: CAT[:, b, :], 128, Wc[:, l, :], 64, None, CT, evac)
            VV(dve.tensor_tensor(x[:, :, :], x[:, :, :], h, ALU.add))
            phase()

        network0()

        def network1():
            o = 0
            TB, o = area(o, [128, B, 66])
            X, o = area(o, [128, 2, 8, 66])
            P, o = area(o, [128, 2, 8, 128])
            PT, o = area(o, [128, 2, 8, 128])
            RI, o = area(o, [128, 2, 8], I32)
            tmp, o = area(o, [128, B, 64])
            st, o = area(o, [128, 4, B])
            S1, o = area(o, [128, B, 2])
            acc, o = area(o, [128, B, 130])
            wa, o = area(o, [128, 2, 2, 64])
            wv, o = area(o, [128, 2, 64])
            eg, o = area(o, [128, 2, 8, 2])
            el, o = area(o, [128, 2, 8, 2])
            ms, o = area(o, [128, 2, 8, 130])
            acc1, o = area(o, [128, B, 130])
            assert o <= WORDS, o
            table = dram("t1", [NP, 66])
            h = TB[:, :, 0:64]
            norm(h, x[:, :, :], 64, st, True, sq=tmp)
            for q in range(2):
                loadb(wv[:, q, :], d["L1_gnn_W"][q])
                loadb(wa[:, q, :, :].rearrange("p a f -> p (a f)"), d["L1_gnn_a"][q])
            g.wait(dve, cl.now())
            for q in range(2):
                for s_ in range(2):
                    VV(dve.tensor_tensor(wa[:, q, s_, :], wa[:, q, s_, :], wv[:, q, :], ALU.mult))
                    VV(dve.tensor_tensor(tmp, h, bc(wa[:, q, s_, :][:, None, :], [128, B, 64]), ALU.mult))
                    VV(dve.tensor_reduce(S1[:, :, q] if s_ == 0 else TB[:, :, 64 + q], tmp, AX.X, ALU.add))
            g.wait(sp, cv.now())
            cl.inc(sp.dma_start(table.rearrange("(b p) f -> p b f", p=128), TB))
            V(dve.memset(acc, 0.0))
            V(dve.memset(acc1, 0.0))
            phase()

            def prepare(a, u, seen):
                if seen is not None:
                    last_use(g, dve, cp, f"mm{u}", seen)
                g.wait(pe, onehot_nodes(P, 1, a, u))
                return transposed(P, PT, u, 0)

            def scores(a, u, t):
                bp = blocks(pe, R_pe, 1, a)
                g.wait(pe, t)
                for n in range(8):
                    mm = pe.matmul(PS[2 + 4 * u][:, 2 * n:2 * n + 2], PT[:, u, n, :],
                                   S1[:, bass.ds(bp[n], 1), :].rearrange("p a f -> p (a f)"), start=True, stop=True)
                return M(mm, f"s{u}")

            scores(0, 0, prepare(0, 0, None))
            phase()
            with g.loop(NG) as i:
                seen = {}
                for u in range(2):
                    gt = gathers(table, X, RI, 1, i, u, [(cv, f"msg{u}")], False)
                    if u:
                        g.wait(dve, scored)
                    else:
                        g.before(dve, cp, "s0")
                    g.wait(dve, gt[1])
                    V(dve.tensor_tensor(eg[:, u], PS[2 + 4 * u][:, 0:16].rearrange("p (n f) -> p n f", f=2),
                                        X[:, u, :, 64:66], ALU.add))
                    g.wait(dve, cv.now())
                    t = V(dve.scalar_tensor_tensor(eg[:, u], eg[:, u], 0.2, eg[:, u], ALU.mult, ALU.max))
                    g.wait(act, t)
                    t_e = A(act.activation(el[:, u], eg[:, u], ACT.Exp))
                    a, v = ahead(i, u)
                    t_pt = prepare(a, v, seen)
                    g.wait(dve, t_e)
                    for q in range(2):
                        V(dve.tensor_tensor(ms[:, u, :, 64 * q:64 * q + 64], X[:, u, :, 0:64],
                                            bc(el[:, u, :, q:q + 1], [128, 8, 64]), ALU.mult))
                    g.wait(pe, V(dve.tensor_copy(ms[:, u, :, 128:130], el[:, u]), f"msg{u}"))
                    view = lambda n: PS[3 + n // 3][:, 130 * (n % 3):130 * (n % 3) + 130]
                    parts = {}
                    for n in range(8):
                        mm = pe.matmul(view(n), P[:, u, n, :], ms[:, u, n, :], start=True, stop=True)
                        if n in (2, 5, 7):
                            parts[n - n % 3] = M(mm, f"mm{u}" if n == 7 else None)
                    seen[f"mm{u}"] = parts[6]
                    scored = scores(a, v, t_pt)
                    add_blocks([acc, acc1], blocks(dve, R_dve, 1, i * 16 + 8 * u), view, u, parts)
            phase()
            VV(dve.tensor_tensor(acc, acc, acc1, ALU.add))
            r = st
            for q in range(2):
                VV(dve.tensor_tensor(r[:, q, :], acc[:, :, 128 + q], padm[:, :], ALU.add))
                VV(dve.reciprocal(r[:, q, :], r[:, q, :]))
                VV(dve.scalar_tensor_tensor(tmp, acc[:, :, 64 * q:64 * q + 64], 0.5,
                                            bc(r[:, q, :][:, :, None], [128, B, 64]), ALU.mult, ALU.mult))
                VV(dve.tensor_tensor(x[:, :, :], x[:, :, :], tmp, ALU.add))
            phase()

        network1()

        def id_flags(k, H, FL, IDT, stage, SF, CC, row):
            P_ = 16 * H
            nv = node[k][:, :].rearrange("p (c j) -> p c j", c=16)
            cop = {}
            sv = stage[:, 0:52 * P_].rearrange("p (j c h) -> p j c h", j=52, c=16)
            for j in range(52):
                V(dve.tensor_copy(sv[:, j], bc(nv[:, :, j:j + 1], [128, 16, H])))
            g.wait(pe, cv.now())
            for q in range(13):
                g.wait(pe, cop.get(q - 2))
                for j in range(4):
                    mm = pe.transpose(PS[q % 2][0:P_, 128 * j:128 * j + 128],
                                      stage[:, P_ * (4 * q + j):P_ * (4 * q + j) + P_], ident[:, :])
                g.wait(act, M(mm))
                cop[q] = A(act.copy(IDT[0:P_, 512 * q:512 * q + 512], PS[q % 2][0:P_, :]))
            g.wait(dve, cs.now())
            V(dve.memset(FL[:, :], 0.0))
            g.wait(dve, cv.now())
            VV(dve.tensor_tensor(FL[0:P_, 1:6656], IDT[0:P_, 1:6656], IDT[0:P_, 0:6655], ALU.is_equal))
            VV(dve.tensor_scalar(FL[0:P_, 1:6656], FL[0:P_, 1:6656], -1.0, BIG, ALU.add, ALU.mult))
            V(dve.tensor_copy(CC[0:P_, 0:1], IDT[0:P_, 0:1]))
            VV(dve.tensor_copy(CC[0:P_, 1:2], IDT[0:P_, 6655:6656]))
            to_row(CC, H, row)
            VV(dve.memset(SF[0:1, :], 0.0))
            n = H * 32
            VV(dve.tensor_tensor(SF[0:1, 1:n], row[0:1, 2:n + 1], row[0:1, 1:n], ALU.is_equal))
            for h_ in range(H):
                VV(dve.memset(SF[0:1, 32 * h_:32 * h_ + 1], 0.0))
            VV(dve.tensor_scalar(SF[0:1, 0:n + 1], SF[0:1, 0:n + 1], -1.0, BIG, ALU.add, ALU.mult))

        def to_row(CC, H, row):
            P_ = 16 * H
            g.wait(pe, cv.now(), cs.now())
            for w in range(2):
                mm = pe.transpose(PS[7][0:1, 128 * w:128 * w + P_], CC[0:P_, w:w + 1], ident[0:P_, 0:P_])
            g.wait(dve, M(mm))
            rv = row[0:1, 1:1 + 32 * H].rearrange("p (h c w) -> p h c w", h=H, c=16)
            for w in range(2):
                VV(dve.tensor_copy(rv[:, :, :, w], PS[7][0:1, 128 * w:128 * w + P_].rearrange("p (c h) -> p h c", h=H)))

        def softmax_weights(H, Ev, AT, Fm, FL, SF, CC, row, rowf, rowb, cr):
            P_, n = 16 * H, 32 * H
            ev = Ev[:, 0:T, :].rearrange("p (c j) h -> p c j h", c=16)
            cop = {}
            sv = Fm[:, 0:52 * P_].rearrange("p (j c h) -> p j c h", j=52, c=16)
            for q in range(13):
                t = V(dve.tensor_copy(sv[:, 4 * q:4 * q + 4], ev[:, :, 4 * q:4 * q + 4, :].rearrange("p c j h -> p j c h")))
                g.wait(pe, t, cop.get(q - 2))
                for j in range(4):
                    mm = pe.transpose(PS[q % 2][0:P_, 128 * j:128 * j + 128],
                                      Fm[:, P_ * (4 * q + j):P_ * (4 * q + j) + P_], ident[:, :])
                g.wait(act, M(mm))
                cop[q] = A(act.copy(AT[0:P_, 512 * q:512 * q + 512], PS[q % 2][0:P_, :]))
            g.wait(dve, cs.now())
            fwd = lambda ini: VV(dve.tensor_tensor_scan(Fm[0:P_, 0:6656], FL[0:P_, 0:6656], AT[0:P_, 0:6656], ini, ALU.add, ALU.max))
            back = lambda ini: VV(dve.tensor_tensor_scan(Fm[0:P_, 0:6656][:, ::-1],
                                                         FL[0:P_, 1:6657][:, ::-1],
                                                         Fm[0:P_, 0:6656][:, ::-1], ini, ALU.add, ALU.max))
            fwd(-BIG)
            VV(dve.tensor_copy(CC[0:P_, 1:2], Fm[0:P_, 6655:6656]))
            back(-BIG)
            VV(dve.tensor_copy(CC[0:P_, 0:1], Fm[0:P_, 0:1]))
            for r in (row, rowf, rowb):
                VV(dve.memset(r[0:1, :], -BIG))
            to_row(CC, H, row)
            VV(dve.tensor_tensor_scan(rowf[0:1, 1:n + 1], SF[0:1, 0:n], row[0:1, 1:n + 1], -BIG, ALU.add, ALU.max))
            VV(dve.tensor_tensor_scan(rowb[0:1, 1:n + 1][:, ::-1], SF[0:1, 1:n + 1][:, ::-1],
                                      row[0:1, 1:n + 1][:, ::-1], -BIG, ALU.add, ALU.max))
            sf0 = SF[0:1, 0:n].rearrange("p (h c w) -> p h c w", h=H, c=16)[:, :, :, 0]
            sf2 = SF[0:1, 1:n + 1].rearrange("p (h c w) -> p h c w", h=H, c=16)[:, :, :, 1]
            lf = rowf[0:1, 0:n].rearrange("p (h c w) -> p h c w", h=H, c=16)[:, :, :, 0]
            rb = rowb[0:1, 2:n + 2].rearrange("p (h c w) -> p h c w", h=H, c=16)[:, :, :, 1]
            cv_ = lambda w: cr[0:1, w, 0:P_].rearrange("p (c h) -> p h c", h=H)
            VV(dve.tensor_tensor(cv_(0), lf, sf0, ALU.add))
            g.wait(pe, VV(dve.tensor_tensor(cv_(1), rb, sf2, ALU.add)))
            for w in range(2):
                mm = pe.matmul(PS[7][0:P_, 256 + w:257 + w], cr[0:1, w, 0:P_], ones[0:1, 0:1], start=True, stop=True)
            g.wait(dve, M(mm))
            VV(dve.tensor_copy(CC[0:P_, 0:2], PS[7][0:P_, 256:258]))
            fwd(CC[0:P_, 0:1])
            back(CC[0:P_, 1:2])
            done = {}

            def put_back(q):
                g.wait(dve if q % 2 else act, done[q])
                cop["b", q] = []
                for j in range(4):
                    out, src = ev[:, :, 4 * q + j, :], PS[2 + q % 2][:, P_ * j:P_ * j + P_].rearrange("p (c h) -> p c h", h=H)
                    cop["b", q].append(V(dve.tensor_copy(out, src)) if q % 2 else A(act.copy(out, src)))

            for q in range(13):
                s = slice(512 * q, 512 * q + 512)
                g.wait(act, V(dve.tensor_tensor(AT[0:P_, s], AT[0:P_, s], Fm[0:P_, s], ALU.subtract)))
                g.wait(pe, A(act.activation(AT[0:P_, s], AT[0:P_, s], ACT.Exp)), *cop.get(("b", q - 2), []))
                for j in range(4):
                    mm = pe.transpose(PS[2 + q % 2][:, P_ * j:P_ * j + P_], AT[0:P_, 512 * q + 128 * j:512 * q + 128 * j + 128],
                                      ident[0:P_, 0:P_])
                done[q] = M(mm)
                if q:
                    put_back(q - 1)
            put_back(12)
            phase()

        def weigh(k, H, Ev, vsp, acc, Vr, P, ms):
            F = 16 * H
            W = F + H
            per = 512 // W
            VV(dve.memset(acc, 0.0))

            def loaded(m, u, z):
                s = slice(4 * F * z, 4 * F * z + 4 * F)
                return [ca[u], cb[u]][z].inc(sp.dma_start(Vr[:, u, s], vsp[:, bass.ds(m, 1), s]))

            def sides(a, u, seen):
                if seen is not None:
                    g.wait(act, seen[f"mm{u}"])
                A(act.copy(ms[:, u, :, F:W], Ev[:, bass.ds(a, 8), :]))
                onehot_aside(P, k, a, u, seen)

            def weighed(a, u, n):
                ex = Ev[:, bass.ds(a, 8), :]
                V(dve.tensor_tensor(ms[:, u, n, 0:F].rearrange("p (h e) -> p h e", h=H),
                                    Vr[:, u].rearrange("p (n h e) -> p n h e", n=8, h=H)[:, n],
                                    bc(ex[:, n, :, None], [128, H, 16]), ALU.mult))

            for u in range(2):
                g.wait(dve, loaded(u, u, 0), loaded(u, u, 1))
                sides(8 * u, u, None)
                for n in range(8):
                    weighed(8 * u, u, n)
            phase()
            last_of = {}

            def free(eng, c, label, w):
                if w < 2:
                    g.before(eng, c, f"{label}{w + 2}")
                else:
                    g.wait(eng, last_of[label, w - 2])

            with g.loop(NG // 2) as i:
                bs = blocks(dve, R_dve, k, i * 32, 32)
                for w in range(4):
                    u = w % 2
                    ld = []
                    for z in range(2):
                        free(sp, cv, "msg" if z else "half", w)
                        ld.append(loaded(i * 4 + (w + 2), u, z))
                    free(pe, cv, "msg", w)
                    free(pe, cs, "ex", w)
                    view = lambda n: PS[4 * u + n // per][:, W * (n % per):W * (n % per) + W]
                    for n in range(8):
                        mm = pe.matmul(view(n), P[:, u, n, :], ms[:, u, n, :], start=True, stop=True)
                        if n == per - 1:
                            first = M(mm)
                    rest = M(mm)
                    a = i * 32 + (16 + 8 * w)
                    sides(a, u, {f"mm{u}": rest})
                    last_of["ex", w] = cs.now(f"ex{w}")
                    for n in range(8):
                        if n or w:
                            g.wait(dve, added)
                        else:
                            g.before(dve, cv, "add")
                        if n == 0:
                            g.wait(dve, first)
                        if n % 4 == 0:
                            g.wait(dve, ld[n // 4])
                        if n == per:
                            g.wait(dve, rest)
                        av = acc[:, bass.ds(bs[8 * w + n], 1), :].rearrange("p a f -> p (a f)")
                        added = V(dve.tensor_tensor(av, av, view(n), ALU.add), "add" if (n, w) == (7, 3) else None)
                        weighed(a, u, n)
                        if n == 3:
                            last_of["half", w] = cv.now(f"half{w}")
                    last_of["msg", w] = cv.now(f"msg{w}")
            phase()

        def unused_units(vsp, zeros, Ev):
            V(dve.memset(Ev[:, T:T + 16, :], 0.0))
            g.wait(sp, V(dve.memset(zeros, 0.0)))
            for u in range(2):
                cl.inc(sp.dma_start(vsp[:, 2 * NG + u, :], zeros))
            phase()

        def prepare_and_score(l, q_, X, P, PT, RI, Ev, table, vsp):
            phase()
            def prepare(a, u, inside):
                if inside:
                    g.before(dve, cp, f"tr{u}")
                t = onehot_nodes(P, 0, a, u)
                g.wait(pe, t)
                bp = blocks(pe, R_pe, 0, a)
                g.wait(pe, transposed(P, PT, u, 0))
                for n in range(8):
                    mm = pe.matmul(PS[2 + 2 * u + n // 4][:, 128 * (n % 4):128 * (n % 4) + 128], PT[:, u, n, :],
                                   q_[:, bass.ds(bp[n], 1), :].rearrange("p a f -> p (a f)"), start=True, stop=True)
                return M(mm, f"tr{u}")

            first_rows(RI, 0)
            prepare(0, 0, False)
            phase()
            with g.loop(NG) as i:
                for u in range(2):
                    gt = gathers(table, X, RI, 0, i, u, [(cv, f"prod{u}"), (cb[u], f"sp{u}")], True)
                    me = nxt if u else None
                    nxt = prepare(*ahead(i, u), True)
                    g.wait(sp, *gt)
                    cb[u].inc(sp.dma_start(vsp[:, bass.ds(i * 2 + u, 1), :].rearrange("p a (n f) -> p (a n) f", n=8),
                                           X[:, u, :, 128:256]), f"sp{u}")
                    if u:
                        g.wait(dve, me)
                    else:
                        g.before(dve, cp, "tr0")
                    for z in range(2):
                        kx = X[:, u, 4 * z:4 * z + 4, 0:128]
                        g.wait(dve, gt[z])
                        VV(dve.tensor_tensor(kx, kx, PS[2 + 2 * u + z][:, :].rearrange("p (n f) -> p n f", n=4), ALU.mult))
                        t = V(dve.tensor_reduce(Ev[:, bass.ds(i * 16 + 8 * u + 4 * z, 4), :],
                                                kx.rearrange("p n (h e) -> p n h e", h=8), AX.X, ALU.add), f"prod{u}")
            phase()

        def network2():
            C = 7
            h, o = area(0, [128, B, 128])
            EO = o
            Ev, o = area(o, [128, T + 16, 8])
            FL, o = area(o, [128, 6658], BF)
            SO = o
            SM, o = area(o, [128, 2048])
            Wq, o = area(o, [128, 2, 512])
            Wp, o = area(o, [128, 1024])
            vec, o = area(o, [128, 6, 128])
            bq, o = area(o, [128, 2, 512])
            b1, o = area(o, [128, 4])
            SF, o = area(o, [1, 258])
            CC, o = area(o, [128, 2])
            row, o = area(o, [1, 260])
            rowf, o = area(o, [1, 260])
            rowb, o = area(o, [1, 260])
            cr, o = area(o, [1, 2, 128])
            st, o = area(o, [128, 4, B])
            RI, o = area(o, [128, 2, 8], I32)
            U = o
            assert U + 13312 <= WORDS, U
            q_, o = area(U, [128, B, 128])
            X, o = area(o, [128, 2, 8, 256])
            P, o = area(o, [128, 2, 8, 128])
            PT = SM.rearrange("p (u n e) -> p u n e", u=2, n=8)
            AT, o = area(U, [128, 6656])
            Fm, o = area(o, [128, 6656])
            acc, o = area(U, [128, B, 136])
            Vr, o = area(o, [128, 2, 1024])
            P2, o = area(o, [128, 2, 8, 128])
            ms, o = area(o, [128, 2, 8, 136])
            assert o <= U + 13312
            oc, o = area(U + B * 136, [128, 2, C, 128])
            x2, o = area(o, [128, 2, C, 128])
            hT, o = area(o, [128, 2, 512])
            hT2, o = area(o, [128, 2, 512])
            assert o <= U + 13312
            xc, o = area(EO, [128, 2, C, 128])
            zz, o = area(o, [128, 2, C, 128])
            ge, o = area(o, [128, 4, 512])
            sq, o = area(o, [128, C, 128])
            assert o <= EO + (T + 16) * 8
            ST, o = area(SO, [128, 4, 384])
            rd, o = area(o, [128, B, 8])
            assert o <= SO + 2048
            tmp, _ = area(U + B * 136, [128, B, 128])
            table = dram("t2", [NP, 256])
            xsp = dram("x2", [128, B, 128])
            vsp = dram("v2", [128, 2 * NG + 2, 1024])
            unused_units(vsp, tmp.rearrange("p b f -> p (b f)")[:, 0:1024], Ev)
            W1 = Wp[:, 0:512]
            W2 = Wp[:, 512:1024].rearrange("p (a f) -> p a f", a=4)

            def load_q(l):
                load(Wq[:, l % 2, :], None, d["W2all"][l][:, 0:512])
                t = loadb(bq[:, l % 2, :], d["b2all"][l][0:512])
                g.wait(dve, t)
                V(dve.tensor_scalar(Wq[:, l % 2, 0:128], Wq[:, l % 2, 0:128], 0.25, None, ALU.mult))
                t = V(dve.tensor_scalar(bq[:, l % 2, 0:128], bq[:, l % 2, 0:128], 0.25, None, ALU.mult))
                g.wait(pe, t)
                g.wait(dve, t)

            def load_rest(l):
                load(Wp, None, d["W2all"][l][:, 512:1536])
                load(b1, None, d["b1T"][l])
                for j, n in enumerate(["ln_g", "ln_b", "b2"]):
                    loadb(vec[:, j, :], d["L2_gnn_" + n][l])
                t = cl.inc(sp.dma_start(vec[:, 3:6, :].rearrange("p a f -> p (a f)"),
                                        d["L2_gnn_Wbeta"][l].to_broadcast([128, 384])))
                g.wait(dve, t)
                VV(dve.tensor_tensor(vec[:, 3, :], vec[:, 3, :], vec[:, 5, :], ALU.add))
                VV(dve.tensor_tensor(vec[:, 4, :], vec[:, 4, :], vec[:, 5, :], ALU.subtract))

            Q = {}

            def subs(c):
                b0 = C * c
                return [(b0, 4), (b0 + 4, C - 4)]

            def stage_q(c, l):
                for s_, (b0, nb) in enumerate(subs(c)):
                    g.wait(pe, ready[c, s_], Q.get("T"))
                    for j in range(nb):
                        mm = pe.transpose(PS[1][:, 128 * j:128 * j + 128], h[:, b0 + j, :], ident[:, :])
                    g.wait(act, M(mm), Q.get(("mm", s_)))
                    Q["T"] = t = A(act.copy(hT2[:, s_, 0:128 * nb], PS[1][:, 0:128 * nb]))
                    g.wait(pe, t)
                    for j in range(nb):
                        b = b0 + j
                        bank, sb_ = b % 2, b % 4
                        g.wait(pe, Q.get(("ev", bank)))
                        mm = M(pe.matmul(PS[6 + bank][:, :], hT2[:, s_, 128 * j:128 * j + 128], Wq[:, l % 2, :],
                                         start=True, stop=True))
                        Q["mm", s_] = mm
                        g.wait(dve, mm, Q.get(("st", sb_)))
                        V(dve.tensor_tensor(q_[:, b, :], PS[6 + bank][:, 0:128], bq[:, l % 2, 0:128], ALU.add))
                        Q["ev", bank] = t = V(dve.tensor_tensor(ST[:, sb_, :], PS[6 + bank][:, 128:512], bq[:, l % 2, 128:512], ALU.add))
                        g.wait(sp, t)
                        on = [ca[0], ca[1], cb[0], cb[1]][sb_]
                        on.inc(sp.dma_start(table[128 * b:128 * b + 128, :], ST[:, sb_, 0:256]))
                        Q["st", sb_] = on.inc(sp.dma_start(xsp[:, b, :], ST[:, sb_, 256:384]))

            x0 = tmp[:, :, 0:64]
            norm(x0, x[:, :, :], 64, st, True, sq=tmp[:, :, 64:128])
            load(Wp[0:64, 0:128], "WiT")
            t = loadb(vec[:, 0, :], d["L2_gnn_bi"])
            g.wait(pe, cv.now(), t)
            CT0 = SM[:, 0:1024].rearrange("p (a f) -> p a f", a=2)
            ready = {}

            def ev0(c, b0, nb, ps, t):
                g.wait(dve, t)
                t = V(dve.tensor_tensor(h[:, b0:b0 + nb, :], ps, bc(vec[:, 0, :][:, None, :], [128, nb, 128]), ALU.add))
                g.wait(act, t)
                A(act.activation(h[:, b0:b0 + nb, :], h[:, b0:b0 + nb, :], ACT.Gelu))
                return [t]

            g.wait(dve, cl.now())
            dense(lambda b: x0[:, b, :], 64, Wp[0:64, 0:128], 128, None, CT0, ev0)
            phase()
            id_flags(0, 8, FL, AT, Fm, SF, CC, row)
            phase()
            load_q(0)
            NC = B // C
            for c in range(NC):
                ready[c, 0] = ready[c, 1] = None
                stage_q(c, 0)

            for l in range(4):
                phase()
                load_rest(l)
                prepare_and_score(l, q_, X, P, PT, RI, Ev, table, vsp)
                softmax_weights(8, Ev, AT, Fm, FL, SF, CC, row, rowf, rowb, cr)
                weigh(0, 8, Ev, vsp, acc, Vr, P2, ms)
                if l < 3:
                    load_q(l + 1)
                VV(dve.tensor_scalar(rd, acc[:, :, 128:136], 1e-16, None, ALU.add))
                VV(dve.reciprocal(rd, rd))
                S = [128, C, 128]
                D, Mt = {}, {}

                def stage_d(c):
                    b, e = C * c, C * c + C
                    w = c % 2
                    out, sk, hc = oc[:, w], xc[:, w], h[:, b:e, :]
                    g.wait(dve, D.get(("pool", c - 2)), D.get(("x2", c - 2)))
                    VV(dve.tensor_tensor(out.rearrange("p b (h e) -> p b h e", h=8),
                                         acc[:, b:e, 0:128].rearrange("p b (h e) -> p b h e", h=8),
                                         bc(rd[:, b:e, :, None], [128, C, 8, 16]), ALU.mult))
                    g.wait(pool, D["ld", c], cv.now())
                    tz = G(pool.tensor_tensor(zz[:, 1], sk, bc(vec[:, 4, :][:, None, :], S), ALU.mult))
                    g.wait(pool, D.get(("x2", c - 2)), Mt.get(("add", c - 2)))
                    to = G(pool.tensor_tensor(x2[:, w], hc, out, ALU.add))
                    VV(dve.tensor_tensor(zz[:, 0], out, bc(vec[:, 3, :][:, None, :], S), ALU.mult))
                    z, z0, z1 = st[:, 0, 0:2 * C], st[:, 0, 0:C], st[:, 0, C:2 * C]
                    g.wait(dve, tz)
                    VV(dve.tensor_reduce(z, zz.rearrange("p a b f -> p (a b) f"), AX.X, ALU.add))
                    t = V(dve.tensor_tensor(z0, z0, z1, ALU.add))
                    g.wait(dve, t)
                    VV(dve.tensor_tensor(sk, sk, out, ALU.subtract))
                    yield
                    g.wait(act, t)
                    g.wait(dve, A(act.activation(z0, z0, ACT.Exp, scale=-1.0)))
                    VV(dve.tensor_scalar(z0, z0, 1.0, None, ALU.add))
                    VV(dve.reciprocal(z0, z0))
                    VV(dve.tensor_tensor(sk, sk, bc(z0[:, :, None], S), ALU.mult))
                    g.wait(dve, to)
                    y = x2[:, w]
                    VV(dve.tensor_tensor(sk, sk, y, ALU.add))
                    m, v = st[:, 1, 0:C], st[:, 2, 0:C]
                    VV(dve.tensor_reduce(m, sk, AX.X, ALU.add))
                    VV(dve.tensor_scalar(m, m, 1.0 / 128, None, ALU.mult))
                    VV(dve.tensor_tensor(sk, sk, bc(m[:, :, None], S), ALU.subtract))
                    VV(dve.tensor_tensor(sq, sk, sk, ALU.mult))
                    VV(dve.tensor_reduce(v, sq, AX.X, ALU.add))
                    yield
                    g.wait(act, VV(dve.tensor_scalar(v, v, 1.0 / 128, 1e-5, ALU.mult, ALU.add)))
                    g.wait(dve, A(act.sqrt(m, v)))
                    VV(dve.reciprocal(v, m))
                    VV(dve.tensor_tensor(sk, sk, bc(v[:, :, None], S), ALU.mult))
                    VV(dve.tensor_tensor(sk, sk, bc(vec[:, 0, :][:, None, :], S), ALU.mult))
                    D["h", c] = t = VV(dve.tensor_tensor(hc, sk, bc(vec[:, 1, :][:, None, :], S), ALU.add))
                    g.wait(pool, t)
                    D["x2", c] = D["pool", c] = G(pool.tensor_tensor(x2[:, w], hc, bc(vec[:, 2, :][:, None, :], S), ALU.add))
                    if c + 2 < NC:
                        g.wait(sp, t)
                        load_skip(c + 2)

                def load_skip(c):
                    D["ld", c] = [ck, cm][c % 2].inc(sp.dma_start(xc[:, c % 2], xsp[:, C * c:C * c + C, :]))

                def stage_m(c, s_):
                    b0, nb = subs(c)[s_]
                    F_ = 128 * nb
                    g.wait(pe, D["h", c], Mt.get("T"))
                    for j in range(nb):
                        mm = pe.transpose(PS[0][:, 128 * j:128 * j + 128], h[:, b0 + j, :], ident[:, :])
                    g.wait(act, M(mm))
                    Mt["T"] = A(act.copy(hT[:, s_, 0:F_], PS[0][:, 0:F_]))
                    g.wait(pe, Mt["T"])
                    for q in range(4):
                        g.wait(pe, Mt.get(("ge", q % 2)))
                        t = M(pe.matmul(PS[2 + q % 2][:, 0:F_], W1[:, 128 * q:128 * q + 128], hT[:, s_, 0:F_],
                                        start=True, stop=True))
                        g.wait(act, t, Mt.get("w2"))
                        Mt["ge", q % 2] = A(act.activation(ge[:, q, 0:F_], PS[2 + q % 2][:, 0:F_], ACT.Gelu,
                                                           bias=b1[:, q:q + 1]))
                    g.wait(pe, Mt["ge", 1], Mt.get(("s", s_)))
                    for j in range(nb):
                        for q in range(4):
                            mm = pe.matmul(PS[4 + s_][:, 128 * j:128 * j + 128], ge[:, q, 128 * j:128 * j + 128], W2[:, q, :],
                                           start=q == 0, stop=q == 3)
                    Mt["w2"] = Mt["done", s_] = M(mm)

                def stage_a(c):
                    for s_, (b0, nb) in enumerate(subs(c)):
                        F_ = 128 * nb
                        g.wait(dve, Mt["done", s_], D["x2", c])
                        ready[c, s_] = Mt["s", s_] = Mt["add", c] = V(dve.tensor_tensor(
                            h[:, b0:b0 + nb, :], x2[:, c % 2, b0 - C * c:b0 - C * c + nb, :],
                            PS[4 + s_][:, 0:F_].rearrange("p (a f) -> p a f", a=nb), ALU.add))

                load_skip(0)
                load_skip(1)
                for c in range(NC + 2):
                    d_ = stage_d(c) if c < NC else iter(())
                    for s_ in range(2):
                        next(d_, None)
                        if 1 <= c <= NC:
                            stage_m(c - 1, s_)
                    next(d_, None)
                    if 1 <= c <= NC:
                        stage_a(c - 1)
                    if c >= 2 and l < 3:
                        stage_q(c - 2, l + 1)
                phase()
            load(Wp[:, 0:64], "WoT")
            t = loadb(vec[:, 0, 0:64], d["L2_gnn_bo"])
            g.wait(pe, t)
            g.wait(dve, t)

            def ev3(c, b0, nb, ps, t):
                g.wait(dve, t)
                t = V(dve.tensor_tensor(x[:, b0:b0 + nb, :], x[:, b0:b0 + nb, :], ps, ALU.add))
                g.wait(dve, t)
                V(dve.tensor_tensor(x[:, b0:b0 + nb, :], x[:, b0:b0 + nb, :], bc(vec[:, 0, 0:64][:, None, :], [128, nb, 64]), ALU.add))
                return [t]

            CT = hT
            dense(lambda b: h[:, b, :], 128, Wp[:, 0:64], 64, None, CT, ev3)
            phase()

        network2()

        def network3():
            Ev, o = area(0, [128, T + 16, 4])
            FL, o = area(o, [128, 6658], BF)
            PT, o = area(o, [128, 2, 8, 128])
            Wk, o = area(o, [64, 128])
            Wr, o = area(o, [19, 128])
            bq, o = area(o, [1, 128])
            SF, o = area(o, [1, 258])
            CC, o = area(o, [128, 2])
            row, o = area(o, [1, 260])
            rowf, o = area(o, [1, 260])
            rowb, o = area(o, [1, 260])
            cr, o = area(o, [1, 2, 128])
            st, o = area(o, [128, 4, B])
            RI, o = area(o, [128, 2, 8], I32)
            U = o
            q_, o = area(U, [128, B, 32])
            X, o = area(o, [128, 2, 8, 96])
            P, o = area(o, [128, 2, 8, 128])
            AB, o = area(o, [128, 2, 8, 20], I32)
            AtT, o = area(o, [19, 2, 8, 128])
            ve, o = area(o, [128, 2, 8, 64])
            kx, o = area(o, [128, 2, 8, 32])
            CT, o = area(o, [128, 2, 512])
            KV, o = area(o, [128, 2, 4, 96])
            h, o = area(o, [128, B, 64])
            tmp, o = area(o, [128, B, 64])
            assert o <= WORDS
            AT, o = area(U, [128, 6656])
            Fm, o = area(o, [128, 6656])
            assert o <= WORDS
            acc, o = area(U, [128, B, 68])
            Vr, o = area(o, [128, 2, 512])
            P2, o = area(o, [128, 2, 8, 128])
            ms, o = area(o, [128, 2, 8, 68])
            assert o <= WORDS
            table = dram("t3", [NP, 96])
            vsp = dram("v3", [128, 2 * NG + 2, 512])
            unused_units(vsp, tmp.rearrange("p b f -> p (b f)")[:, 0:512], Ev)
            norm(h, x[:, :, :], 64, st, True, sq=tmp)
            load(Wk, "L3_gnn_qkv_w")
            load(bq, None, d["L3_gnn_qkv_b"][None, :])
            load(Wr, "rpe_wb")
            phase()
            prev = {}

            def ev1(c, b0, nb, ps, t):
                g.wait(act, t, prev.get(c - 2))
                A(act.activation(q_[:, b0:b0 + nb, :], ps[:, :, 0:32], ACT.Copy, scale=float(np.float32(8.0) ** np.float32(-0.5))))
                a_ = A(act.copy(KV[:, c % 2, 0:nb, :], ps[:, :, 32:128]))
                g.wait(sp, a_)
                prev[c] = cb[c % 2].inc(sp.dma_start(
                    table[128 * b0:128 * (b0 + nb), :].rearrange("(b p) f -> p b f", p=128), KV[:, c % 2, 0:nb, :]))
                return [a_]

            dense(lambda b: h[:, b, :], 64, Wk, 128, bq, CT, ev1)
            phase()
            tb = tab[1].rearrange("(p t) w -> p t w", p=128)
            V(dve.memset(AtT[:, :, :, :], 1.0))

            def prepare(a, u, inside):
                if inside:
                    g.before(sp, cp, f"at{u}")
                ld = ca[u].inc(sp.dma_start(AB[:, u], tb[:, bass.ds(a, 8), :]))
                if inside:
                    g.before(dve, cp, f"tr{u}")
                t_p = onehot_nodes(P, 1, a, u)
                bp = blocks(pe, R_pe, 1, a)
                g.wait(pe, ld)
                hold(pe)
                for n in range(8):
                    mm = pe.transpose(PS[2 + n // 4][0:18, 128 * (n % 4):128 * (n % 4) + 128],
                                      AB[:, u, n, 2:20].bitcast(F32), ident[:, :])
                g.wait(act, M(mm, f"at{u}"))
                for z in range(2):
                    A(act.copy(AtT[0:18, u, 4 * z:4 * z + 4, :].rearrange("p a e -> p (a e)"), PS[2 + z][0:18, :]))
                g.wait(pe, t_p)
                t_pt = transposed(P, PT, u, 0)
                view = lambda n: PS[4 + 2 * u + n // 4][:, 128 * (n % 4):128 * (n % 4) + 128]
                g.wait(pe, t_pt)
                for n in range(8):
                    pe.matmul(view(n), AtT[:, u, n, :], Wr, start=True, stop=False)
                    mm = pe.matmul(view(n)[:, 0:32], PT[:, u, n, :],
                                   q_[:, bass.ds(bp[n], 1), :].rearrange("p a f -> p (a f)"), start=False, stop=True)
                return M(mm, f"tr{u}")

            g.wait(act, cv.now())
            first_rows(RI, 1)
            prepare(0, 0, False)
            phase()
            with g.loop(NG) as i:
                for u in range(2):
                    a = i * 16 + 8 * u
                    gt = gathers(table, X, RI, 1, i, u, [(cv, f"ve{u}")], True)
                    me = nxt if u else None
                    nxt = prepare(*ahead(i, u), True)
                    if u:
                        g.wait(dve, me)
                    else:
                        g.before(dve, cp, "tr0")
                    g.before(dve, cb[u], f"sp{u}")
                    for z in range(2):
                        ps = PS[4 + 2 * u + z][:, :].rearrange("p (n f) -> p n f", n=4)
                        r = slice(4 * z, 4 * z + 4)
                        g.wait(dve, gt[z])
                        V(dve.tensor_tensor(kx[:, u, r, :], X[:, u, r, 0:32], ps[:, :, 32:64], ALU.add))
                        V(dve.tensor_tensor(ve[:, u, r, :], X[:, u, r, 32:96], ps[:, :, 64:128], ALU.add), f"ve{u}")
                        g.wait(dve, cv.now())
                        VV(dve.tensor_tensor(kx[:, u, r, :], kx[:, u, r, :], ps[:, :, 0:32], ALU.mult))
                        t = VV(dve.tensor_reduce(Ev[:, bass.ds(a + 4 * z, 4), :],
                                                 kx[:, u, r, :].rearrange("p n (h e) -> p n h e", h=4), AX.X, ALU.add))
                    g.wait(sp, t)
                    cb[u].inc(sp.dma_start(vsp[:, bass.ds(i * 2 + u, 1), :],
                                           ve[:, u].rearrange("p n f -> p (n f)")), f"sp{u}")
            phase()
            id_flags(1, 4, FL, AT, Fm, SF, CC, row)
            phase()
            softmax_weights(4, Ev, AT, Fm, FL, SF, CC, row, rowf, rowb, cr)
            weigh(1, 4, Ev, vsp, acc, Vr, P2, ms)
            rd = PT[:, 0, 0:2, :].rearrange("p a b -> p (a b)")[:, 0:B * 4].rearrange("p (b h) -> p b h", b=B)
            VV(dve.tensor_scalar(rd, acc[:, :, 64:68], 1e-16, None, ALU.add))
            VV(dve.reciprocal(rd, rd))
            for h_ in range(4):
                s = slice(16 * h_, 16 * h_ + 16)
                VV(dve.tensor_tensor(acc[:, :, s], acc[:, :, s], bc(rd[:, :, h_:h_ + 1], [128, B, 16]), ALU.mult))
                VV(dve.tensor_tensor(x[:, :, s], x[:, :, s], acc[:, :, s], ALU.add))

        network3()
        g.wait(sp, cv.now())
        cl.inc(sp.dma_start(d["out"][0:128 * (B - 1), :].rearrange("(b p) f -> p b f", p=128), x[:, 0:B - 1, :]))
        cl.inc(sp.dma_start(d["out"][128 * (B - 1):N, :], x[0:N - 128 * (B - 1), B - 1, :]))
        phase()



def prepare(inputs):
    f = lambda name: np.ascontiguousarray(inputs[name])
    a = {}
    src, dst = f("src"), f("dst")
    a["src"], a["dst"] = src.reshape(EP, ET), dst.reshape(EP, ET)
    a["srcT"] = np.ascontiguousarray(a["src"].T)
    a["dstT"] = np.ascontiguousarray(a["dst"].T)
    a["pair"] = np.stack([a["src"], a["dst"]], axis=-1)
    a["attr"] = f("edge_attr_18").reshape(EP, ET, 18)
    a["x"] = f("x")
    for n_ in ("W_l", "W_r", "b", "gamma", "beta", "run_mean", "run_var"):
        a["L0_gnn_" + n_] = f("L0_gnn_" + n_)
    a["L1_gnn_W"], a["L1_gnn_a"] = f("L1_gnn_W"), f("L1_gnn_a")
    T_ = lambda n_: f("L2_gnn_" + n_).transpose(0, 2, 1)
    W2T = T_("W2").reshape(4, 4, 128, 128).transpose(0, 2, 1, 3).reshape(4, 128, 512)
    a["W2all"] = np.concatenate([T_("Wq"), T_("Wk"), T_("Wv"), T_("Ws"), T_("W1"), W2T], axis=2)
    a["b2all"] = np.concatenate([f("L2_gnn_" + n_) for n_ in ("bq", "bk", "bv", "bs")], axis=1)
    a["b1T"] = f("L2_gnn_b1").reshape(4, 4, 128).transpose(0, 2, 1)
    a["WiT"], a["WoT"] = f("L2_gnn_Wi").T, f("L2_gnn_Wo").T
    for n_ in ("bi", "ln_g", "ln_b", "b2", "Wbeta", "bo"):
        a["L2_gnn_" + n_] = f("L2_gnn_" + n_)
    a["L3_gnn_qkv_w"], a["L3_gnn_qkv_b"] = f("L3_gnn_qkv_w"), f("L3_gnn_qkv_b")
    a["rpe_wb"] = np.concatenate([np.concatenate([f(f"L3_gnn_{n_}_rpe_w"), f(f"L3_gnn_{n_}_rpe_b")[None]], axis=0)
                                  for n_ in "qkv"], axis=1)
    return {k: np.ascontiguousarray(v) for k, v in a.items()}


def program(new, arrays, outputs):
    plan = {}
    for dry in (True, False):
        nc = new()
        d = {k: nc.dram_tensor(f"in_{k}", list(v.shape), mybir.dt.from_np(v.dtype), kind="ExternalInput").ap()
             for k, v in arrays.items()}
        for k, shape in outputs.items():
            d[k] = nc.dram_tensor(k, shape, F32, kind="ExternalOutput").ap()
        build(nc, d, plan, dry)
    return nc


def kernel(**inputs):
    import concourse.bacc as bacc
    from concourse.bass_utils import run_bass_kernel_spmd

    arrays = prepare(inputs)
    nc = program(lambda: bacc.Bacc("TRN2", target_bir_lowering=False, num_devices=1), arrays, {"out": [N, 64]})
    r = run_bass_kernel_spmd(nc, [{f"in_{k}": v for k, v in arrays.items()}], core_ids=[0])
    return r.results[0]["out"]
```
